# Optimizing a Trainium2 kernel written in Bass

```python
import numpy as np
import jax
import jax.numpy as jnp

def _softmax(x, axis=-1):
    return jax.nn.softmax(x, axis=axis)

def _gelu(x):
    return jax.nn.gelu(x, approximate=True)

def _silu(x):
    return jax.nn.silu(x)

def _sigmoid(x):
    return jax.nn.sigmoid(x)

def _layernorm(x, axis=-1, eps=1e-05):
    m = jnp.mean(x, axis=axis, keepdims=True)
    v = jnp.var(x, axis=axis, keepdims=True)
    return (x - m) / jnp.sqrt(v + eps)

def _scatter_add(tgt, idx, src, axis=0):
    return tgt.at[idx].add(src)

def _segment_sum(src, seg, n):
    return jax.ops.segment_sum(src, seg, n)
kernel_name = 'mk_xattn_ffn_d1_seqx_r4_d55149'

def setup_inputs(seed: int=0):
    np.random.seed(seed)
    _w = jnp.asarray

    def _rec_inputs():
        import jax
        import jax.numpy as jnp
        _rk = jax.random.key(seed)
        x = 7.22e-05 + 1 * jax.random.normal(jax.random.fold_in(_rk, 1), (16, 128, 512), jnp.float32)
        _lenS = 128 - jax.random.randint(jax.random.fold_in(_rk, 7), (16,), 0, max(1, 128 // 4) + 1, jnp.int32)
        _lenS2 = 128 - jax.random.randint(jax.random.fold_in(_rk, 8), (16,), 0, max(1, 128 // 4) + 1, jnp.int32)
        _ctx_1024P = jax.random.normal(jax.random.fold_in(_rk, 11), (16, 16, 256), jnp.float32)
        _ctx_1024c = jax.random.dirichlet(jax.random.fold_in(_rk, 511), 0.3 * jnp.ones((16,), jnp.float32), (16, 128))
        _ctx_1024t = jnp.einsum('bsk,bkd->bsd', _ctx_1024c, _ctx_1024P)
        _ctx_1024t = _ctx_1024t * jax.lax.rsqrt(jnp.mean(jnp.square(_ctx_1024t)) + 1e-12) * 0.953939
        ctx_1024 = -1.39393e-06 + 0.999914 * (_ctx_1024t + 0.3 * jax.random.normal(jax.random.fold_in(_rk, 611), (16, 128, 256), jnp.float32))
        fside_BxSx2_0 = jax.random.uniform(jax.random.fold_in(_rk, 12), (16, 128, 2), jnp.float32, 0.0, 0.999707)
        return (x, ctx_1024, fside_BxSx2_0)
    x, ctx_1024, fside_BxSx2_0 = _rec_inputs()

    def _L0_xattn_setup():
        import jax, jax.numpy as jnp
        import numpy as np
        DIM = 512
        CTX_DIM = 256
        N_HEADS = 32
        HEAD_DIM = DIM // N_HEADS
        POS_DIM = 2
        B, N, CTXN = (2, 512, 512)
        ROPE_BASE = 10000.0

        def apply_axial_rope(x, pos):
            b, n, h, d = x.shape
            p = pos.shape[-1]
            dpa = d // p
            half = dpa // 2
            freqs = ROPE_BASE ** (-jnp.arange(half, dtype=x.dtype) / half)
            ang = pos[..., :, None] * freqs
            cos = jnp.cos(ang)[:, :, None, :, :]
            sin = jnp.sin(ang)[:, :, None, :, :]
            xr = x.reshape(b, n, h, p, half, 2)
            x1, x2 = (xr[..., 0], xr[..., 1])
            out = jnp.stack([x1 * cos - x2 * sin, x1 * sin + x2 * cos], axis=-1)
            return out.reshape(b, n, h, d)
        key = jax.random.key(seed)
        ks = jax.random.split(key, 8)
        x = jax.random.normal(ks[0], (B, N, DIM), jnp.float32)
        ctx = jax.random.normal(ks[1], (B, CTXN, CTX_DIM), jnp.float32)
        pos_map = jax.random.uniform(ks[2], (B, N, POS_DIM), jnp.float32)
        ctx_pos_map = jax.random.uniform(ks[3], (B, CTXN, POS_DIM), jnp.float32)
        Wq = jax.random.normal(ks[4], (DIM, DIM), jnp.float32) / np.sqrt(DIM)
        Wkv = jax.random.normal(ks[5], (CTX_DIM, 2 * DIM), jnp.float32) / np.sqrt(CTX_DIM)
        Wout = jax.random.normal(ks[6], (DIM, DIM), jnp.float32) / np.sqrt(DIM)
        bout = jnp.zeros((DIM,), jnp.float32)
        return {'x': x, 'ctx': ctx, 'pos_map': pos_map, 'ctx_pos_map': ctx_pos_map, 'Wq': Wq, 'Wkv': Wkv, 'Wout': Wout, 'bout': bout}
    _L0_xattn_all = _L0_xattn_setup()
    _L0_xattn_in = {k: v for k, v in _L0_xattn_all.items() if k in ('Wq', 'Wkv', 'Wout', 'bout')}
    del _L0_xattn_all

    def _L0_ffn_setup():
        import jax, jax.numpy as jnp
        import numpy as np
        B, S, H = (4, 512, 512)
        I, E, K = (352, 16, 2)

        def _swiglu(x, a, b, c):
            return jax.nn.silu(x @ a.T) * (x @ b.T) @ c.T
        key = jax.random.key(seed)
        ks = jax.random.split(key, 8)
        sc = 0.02
        return {'hidden_states': jax.random.normal(ks[0], (B, S, H), jnp.float32), 'gate_w': jax.random.normal(ks[1], (E, H), jnp.float32) * sc, 'bias': jnp.zeros((E,), jnp.float32), 'shared_w1': jax.random.normal(ks[2], (I, H), jnp.float32) * sc, 'shared_w3': jax.random.normal(ks[3], (I, H), jnp.float32) * sc, 'shared_w2': jax.random.normal(ks[4], (H, I), jnp.float32) * sc, 'w1': jax.random.normal(ks[5], (E, I, H), jnp.float32) * sc, 'w3': jax.random.normal(ks[6], (E, I, H), jnp.float32) * sc, 'w2': jax.random.normal(ks[7], (E, H, I), jnp.float32) * sc}
    _L0_ffn_all = _L0_ffn_setup()
    _L0_ffn_in = {k: v for k, v in _L0_ffn_all.items() if k in ('gate_w', 'bias', 'shared_w1', 'shared_w3', 'shared_w2', 'w1', 'w3', 'w2')}
    del _L0_ffn_all
    return {'x': x, 'ctx_1024': ctx_1024, 'fside_BxSx2_0': fside_BxSx2_0, 'L0_xattn_Wq': _L0_xattn_in['Wq'], 'L0_xattn_Wkv': _L0_xattn_in['Wkv'], 'L0_xattn_Wout': _L0_xattn_in['Wout'], 'L0_xattn_bout': _L0_xattn_in['bout'], 'L0_ffn_gate_w': _L0_ffn_in['gate_w'], 'L0_ffn_bias': _L0_ffn_in['bias'], 'L0_ffn_shared_w1': _L0_ffn_in['shared_w1'], 'L0_ffn_shared_w3': _L0_ffn_in['shared_w3'], 'L0_ffn_shared_w2': _L0_ffn_in['shared_w2'], 'L0_ffn_w1': _L0_ffn_in['w1'], 'L0_ffn_w3': _L0_ffn_in['w3'], 'L0_ffn_w2': _L0_ffn_in['w2']}

def reference(x, ctx_1024, fside_BxSx2_0, L0_xattn_Wq, L0_xattn_Wkv, L0_xattn_Wout, L0_xattn_bout, L0_ffn_gate_w, L0_ffn_bias, L0_ffn_shared_w1, L0_ffn_shared_w3, L0_ffn_shared_w2, L0_ffn_w1, L0_ffn_w3, L0_ffn_w2):
    import jax
    import jax.numpy as jnp

    def _L0_xattn_ref(x, ctx, pos_map, ctx_pos_map, Wq, Wkv, Wout, bout):
        import jax, jax.numpy as jnp
        import numpy as np
        DIM = 512
        CTX_DIM = 256
        N_HEADS = 32
        HEAD_DIM = DIM // N_HEADS
        POS_DIM = 2
        B, N, CTXN = (2, 512, 512)
        ROPE_BASE = 10000.0

        def apply_axial_rope(x, pos):
            b, n, h, d = x.shape
            p = pos.shape[-1]
            dpa = d // p
            half = dpa // 2
            freqs = ROPE_BASE ** (-jnp.arange(half, dtype=x.dtype) / half)
            ang = pos[..., :, None] * freqs
            cos = jnp.cos(ang)[:, :, None, :, :]
            sin = jnp.sin(ang)[:, :, None, :, :]
            xr = x.reshape(b, n, h, p, half, 2)
            x1, x2 = (xr[..., 0], xr[..., 1])
            out = jnp.stack([x1 * cos - x2 * sin, x1 * sin + x2 * cos], axis=-1)
            return out.reshape(b, n, h, d)
        b, n, _ = x.shape
        ctx_n = ctx.shape[1]
        q = (x @ Wq).reshape(b, n, N_HEADS, HEAD_DIM)
        k, v = jnp.split(ctx @ Wkv, 2, axis=-1)
        k = k.reshape(b, ctx_n, N_HEADS, HEAD_DIM)
        v = v.reshape(b, ctx_n, N_HEADS, HEAD_DIM)
        q = apply_axial_rope(q, pos_map)
        k = apply_axial_rope(k, ctx_pos_map)
        scale = 1.0 / np.sqrt(HEAD_DIM).astype(np.float32)
        logits = jnp.einsum('bqhd,bkhd->bhqk', q, k) * scale
        w = jax.nn.softmax(logits, axis=-1)
        attn = jnp.einsum('bhqk,bkhd->bqhd', w, v)
        attn = attn.reshape(b, n, N_HEADS * HEAD_DIM)
        return attn @ Wout + bout

    def _L0_ffn_ref(hidden_states, gate_w, bias, shared_w1, shared_w3, shared_w2, w1, w3, w2):
        import jax, jax.numpy as jnp
        import numpy as np
        B, S, H = (4, 512, 512)
        I, E, K = (352, 16, 2)

        def _swiglu(x, a, b, c):
            return jax.nn.silu(x @ a.T) * (x @ b.T) @ c.T
        orig_shape = hidden_states.shape
        x = hidden_states.reshape(-1, orig_shape[-1])
        T = x.shape[0]
        shared_output = _swiglu(x, shared_w1, shared_w3, shared_w2)
        logits = x @ gate_w.T
        scores = jax.nn.sigmoid(logits)
        routing_scores = scores + bias
        _, topk_idx = jax.lax.top_k(routing_scores, K)
        sel = jnp.take_along_axis(scores, topk_idx, axis=1)
        gating = sel / sel.sum(axis=-1, keepdims=True)
        combine = jnp.zeros((T, E), x.dtype).at[jnp.arange(T)[:, None], topk_idx].add(gating)
        routed_output = jnp.zeros_like(x)
        for e in range(E):
            y = _swiglu(x, w1[e], w3[e], w2[e])
            routed_output = routed_output + combine[:, e:e + 1] * y
        return (shared_output + routed_output).reshape(orig_shape)
    x = x + _L0_xattn_ref(_layernorm(x, axis=-1), ctx_1024, fside_BxSx2_0, fside_BxSx2_0, L0_xattn_Wq, L0_xattn_Wkv, L0_xattn_Wout, L0_xattn_bout)
    x = x + _L0_ffn_ref(_layernorm(x, axis=-1), L0_ffn_gate_w, L0_ffn_bias, L0_ffn_shared_w1, L0_ffn_shared_w3, L0_ffn_shared_w2, L0_ffn_w1, L0_ffn_w3, L0_ffn_w2)
    return x

_drawn_inputs = setup_inputs


def setup_inputs(seed=0):
    import zlib

    import numpy as np

    out = dict(_drawn_inputs(seed))
    spreads = {'L0_xattn_bout': (0.0, 0.1), 'L0_ffn_bias': (0.0, 2.0)}
    factors = {'L0_ffn_gate_w': 8.365}
    for name, (base, spread) in spreads.items():
        noise = np.random.default_rng([zlib.crc32(name.encode()), seed]).standard_normal(out[name].shape)
        drawn = base * np.exp(spread * noise) if base else spread * noise
        out[name] = jnp.asarray(drawn.astype(out[name].dtype))
    for name, factor in factors.items():
        out[name] = (out[name] * factor).astype(out[name].dtype)
    return out
```

```python
from contextlib import ExitStack
from math import pi

import concourse.bass as bass
from concourse import mybir

F32 = mybir.dt.float32
F16 = mybir.dt.float16
U32 = mybir.dt.uint32
I32 = mybir.dt.int32
ACT = mybir.ActivationFunctionType
ALU = mybir.AluOpType
AX_X = mybir.AxisListType.X

P = 128
B = 16
DIM, CTX_DIM = 512, 256
KC, KCC = DIM // P, CTX_DIM // P
HEADS, HD = 32, 16
PAIRS = HEADS // 2
STACK = 4 * HD
VW = HD + 1
CH = 4
NCH = HEADS // CH
HALF = HEADS // 2
RING = 4
SCATTERS = 8
PEELED = 8
ROT = HD // 2
E, TOPK = 16, 2
INNER = 352
W13 = 2 * INNER
ICH = [(0, P), (P, P), (2 * P, INNER - 2 * P)]
T = B * P
GROUPS = B * TOPK
TILES = (T * TOPK) // P + E - 1
EPS = 1e-5
SCALE = HD ** -0.5
ROUND = float(3 << 22)


def build(nc, x, ctxT, pos, wq, wkv, wo, bout, gateT, gbias, s13, s2, e13, e2, out):
    with ExitStack() as stack:
        def sb(name, shape, dt=F32):
            return stack.enter_context(nc.sbuf_tensor(name, shape, dt))

        def ps(name, shape, dt=F32):
            return stack.enter_context(nc.psum_tensor(name, shape, dt))

        def sem(name):
            return stack.enter_context(nc.semaphore(name))

        xn2_dram = nc.dram_tensor("xn2_dram", [T, DIM], F32, kind="Internal").ap()
        table_dram = nc.dram_tensor("table_dram", [P * TILES, 1], U32, kind="Internal").ap()
        y_dram = nc.dram_tensor("y_dram", [TILES * P, DIM], F32, kind="Internal").ap()

        stream = sb("stream", [P, B, DIM])
        wq_sb = sb("wq_sb", [P, KC, DIM])
        wkv_sb = sb("wkv_sb", [P, KCC, 2 * DIM])
        wo_sb = sb("wo_sb", [P, KC, DIM])
        bout_sb = sb("bout_sb", [P, DIM])
        gate_sb = sb("gate_sb", [P, KC, E])
        gbias_sb = sb("gbias_sb", [P, E])
        pos_sb = sb("pos_sb", [P, B, 2])
        ident = sb("ident", [P, P])
        ident16 = sb("ident16", [P, P], F16)
        select = sb("select", [P, HEADS, P], F16)
        before = sb("before", [P, P], F16)
        ones16 = sb("ones16", [P, P], F16)
        carrier_dve, carrier_pool = sb("carrier_dve", [P, 1]), sb("carrier_pool", [P, 1])
        minus_half = sb("minus_half", [P, 1])
        angle = sb("angle", [P, B, ROT])
        turns = sb("turns", [P, B, ROT])
        cos_t = sb("cos_t", [P, B, HD])
        sin_t = sb("sin_t", [P, B, HD])
        ctx_sb = sb("ctx_sb", [P, 2, KCC, P])
        stats1, mv1, rstd1 = sb("stats1", [P, 6]), sb("mv1", [P, 2]), sb("rstd1", [P, 1])
        stats2, mv2, rstd2 = sb("stats2", [P, 6]), sb("mv2", [P, 2]), sb("rstd2", [P, 1])
        xn = sb("xn", [P, DIM])
        xnT = sb("xnT", [P, KC, P])
        qk = sb("qk", [P, 2 * DIM])
        rot = sb("rot", [P, 2 * DIM])
        swp = sb("swp", [P, 2 * DIM])
        parts = sb("parts", [P, 2 * HEADS, STACK], F16)
        qT = sb("qT", [P, PAIRS, P], F16)
        kT = sb("kT", [P, PAIRS, 2, P], F16)
        vhi = sb("vhi", [P, 2, HEADS, VW], F16)
        vlo = sb("vlo", [P, 2, HEADS, VW], F16)
        rowmax = sb("rowmax", [P, HEADS])
        negmax = sb("negmax", [P, P], F16)
        negmaxT = sb("negmaxT", [P, P], F16)
        prob = sb("prob", [P, RING, CH * P])
        phi = sb("phi", [P, RING, CH * P], F16)
        plo = sb("plo", [P, RING, CH * P], F16)
        recip = sb("recip", [P, HALF])
        attn = sb("attn", [P, DIM])
        attnT = sb("attnT", [P, KC, P])
        xn2 = sb("xn2", [P, 2, DIM])
        xn2T = sb("xn2T", [P, KC, P])
        logits = sb("logits", [P, B, E])
        score = sb("score", [P, B, E])
        routing = sb("routing", [P, B, E])
        best = sb("best", [P, B, 8])
        best_at = sb("best_at", [P, B, 8], U32)
        chosen = sb("chosen", [P, B, TOPK])
        expert_no = sb("expert_no", [P, E])
        mask = sb("mask", [P, GROUPS, E])
        mask16 = sb("mask16", [P, GROUPS, E], F16)
        work = sb("work", [P, GROUPS, E])
        picked = sb("picked", [P, B, TOPK])
        pick_sum = sb("pick_sum", [P, B])
        gates = sb("gates", [P, B, TOPK])
        tiles_of = sb("tiles_of", [P, E])
        one_e = sb("one_e", [P, E])
        tiles_end = sb("tiles_end", [P, E])
        first_slot = sb("first_slot", [P, E])
        slot = sb("slot", [P, GROUPS])
        slot_tile = sb("slot_tile", [P, GROUPS])
        slot_at = sb("slot_at", [P, GROUPS])
        slot_u = sb("slot_u", [P, GROUPS], U32)
        slot_at_u = sb("slot_at_u", [P, GROUPS], U32)
        token_no = sb("token_no", [P, GROUPS], U32)
        zero_table = sb("zero_table", [P, TILES], U32)
        tile_no = sb("tile_no", [P, TILES])
        tile_cmp = sb("tile_cmp", [P, TILES, E])
        tile_expert = sb("tile_expert", [P, TILES])
        tile_expert_i = sb("tile_expert_i", [P, TILES], I32)
        tile_new = sb("tile_new", [P, TILES], I32)
        table = sb("table", [P, TILES], U32)
        scat_at = sb("scat_at", [P, SCATTERS, 1], U32)
        scat_id = sb("scat_id", [P, SCATTERS, 1], U32)
        w13 = sb("w13", [P, 2, KC, W13])
        w2 = sb("w2", [P, 2, len(ICH), DIM])
        row_at = sb("row_at", [P, 2, 1], U32)
        xe = sb("xe", [P, 2, DIM])
        xeT = sb("xeT", [P, 2, KC, P])
        act_g = sb("act_g", [P, INNER])
        hidden = sb("hidden", [P, INNER])
        hiddenT = sb("hiddenT", [P, len(ICH), P])
        ye = sb("ye", [P, 2, DIM])
        y_at = sb("y_at", [P, 2, TOPK], U32)
        y_got = [[prob[:, 2 * p + k, :] for k in range(TOPK)] for p in range(2)]

        p_tr = ps("p_tr", [P, KC, P])
        p_qk = ps("p_qk", [P, 2 * DIM])
        p_v = ps("p_v", [P, DIM])
        p_st32 = ps("p_st", [P, 512])
        p_st = p_st32[:].bitcast(F16).rearrange("p (n t) -> p n t", t=P)
        p_sc = [ps(f"p_sc{n}", [P, CH * P]) for n in range(2)]
        p_pv = ps("p_pv", [P, 512])
        pv = p_pv[:, 0:HALF * VW].rearrange("p (h d) -> p h d", d=VW)
        p_xT, p_g, p_u, p_hT = p_tr, p_qk[:, 0:INNER], p_qk[:, DIM:DIM + INNER], p_v
        p_y = p_sc
        p_rank = p_st32[:].rearrange("p (g e) -> p g e", e=E)
        p_total = p_pv[:, 0:E]

        w_early = sem("w_early"); w_late = sem("w_late"); w_shared = sem("w_shared")
        x_early = sem("x_early"); x_late = sem("x_late"); pos_loaded = sem("pos_loaded")
        ctx_loaded = sem("ctx_loaded")
        cleared = sem("cleared"); consts = sem("consts"); zeroed = sem("zeroed")
        trig = sem("trig"); sines = sem("sines"); rot_setup = sem("rot_setup"); tables_ready = sem("tables_ready"); w_bout = sem("w_bout"); table_cleared = sem("table_cleared")
        ln1_step = sem("ln1_step"); rstd1_ready = sem("rstd1_ready")
        xnT_done = sem("xnT_done"); xnT_ready = sem("xnT_ready")
        qk_done = sem("qk_done"); v_done = sem("v_done")
        qk_ready = sem("qk_ready"); vhi_ready = sem("vhi_ready"); vlo_ready = sem("vlo_ready")
        swapped = sem("swapped"); rot_step = sem("rot_step")
        hi_ready = sem("hi_ready"); lo_ready = sem("lo_ready"); parts_ready = sem("parts_ready")
        bias_added = sem("bias_added")
        st_done = sem("st_done"); qT_ready = sem("qT_ready"); kT_ready = sem("kT_ready")
        scored = sem("scored"); max_ready = sem("max_ready"); neg_step = sem("neg_step")
        negT_done = sem("negT_done"); negT_ready = sem("negT_ready")
        shifted = sem("shifted"); exp_ready = sem("exp_ready")
        phi_ready = sem("phi_ready"); plo_ready = sem("plo_ready")
        pv_done = sem("pv_done"); recip_ready = sem("recip_ready"); attn_ready = sem("attn_ready")
        attnT_done = sem("attnT_done"); attnT_ready = sem("attnT_ready")
        wo_done = sem("wo_done"); ln2_step = sem("ln2_step"); rstd2_ready = sem("rstd2_ready")
        xn2T_done = sem("xn2T_done"); xn2T_ready = sem("xn2T_ready")
        xn2_stored = sem("xn2_stored"); gate_done = sem("gate_done"); logits_kept = sem("logits_kept")
        gate_exp = sem("gate_exp"); route = sem("route"); masks_ready = sem("masks_ready")
        counted = sem("counted"); experts_known = sem("experts_known"); slots_known = sem("slots_known")
        gates_known = sem("gates_known")
        ids = sem("ids"); scat_copied = sem("scat_copied")
        scattered = sem("scattered")
        table_loaded = sem("table_loaded")
        xe_loaded = [sem(f"xe_loaded{n}") for n in range(2)]
        xe_gathered = [sem(f"xe_gathered{n}") for n in range(2)]
        w13_loaded = [sem(f"w13_loaded{n}") for n in range(2)]
        w2_loaded = [sem(f"w2_loaded{n}") for n in range(2)]
        row_copied = sem("row_copied")
        xeT_done = sem("xeT_done"); xeT_ready = sem("xeT_ready")
        g_done = sem("g_done"); u_done = sem("u_done"); act_ready = sem("act_ready")
        hidden_ready = sem("hidden_ready"); hT_done = sem("hT_done"); hT_ready = sem("hT_ready")
        y_done = sem("y_done"); y_ready = sem("y_ready")
        y_stored = [sem(f"y_stored{n}") for n in range(2)]
        y_at_copied = sem("y_at_copied")
        y_gathered = [sem(f"y_gathered{n}") for n in range(2)]
        summed = sem("summed")
        out_stored = sem("out_stored")

        x_t = x.rearrange("b p d -> p b d")
        out_t = out.rearrange("b p d -> p b d")

        block = stack.enter_context(nc.Block())

        def batches(body, eng):
            body(0, 0, False, True, True)
            with eng.Fori(0, (B - 4) // 2) as r:
                for u in (1, 2):
                    body(r * 2 + u, u % 2, True, True, True)
            for b in (B - 3, B - 2, B - 1):
                body(b, b % 2, True, b + 1 < B, b + 2 < B)

        def expert_tiles(body, eng, beside=lambda n: None):
            kinds = ["shared"] * B + ["routed"] * TILES + [None, None]

            def one(n):
                body(n, n // 2, n % 2, *kinds[n:n + 3])

            for n in range(PEELED):
                one(n)
                beside(n)
            with eng.Fori(0, (B - 2 - PEELED) // 2) as r:
                for u in range(2):
                    body(r * 2 + (PEELED + u), r + PEELED // 2, u, *["shared"] * 3)
            one(B - 2)
            one(B - 1)
            with eng.Fori(0, (TILES - 3) // 2) as r:
                for u in range(2):
                    body(r * 2 + (B + u), r + B // 2, u, *["routed"] * 3)
            for n in range(B + TILES - 3, B + TILES):
                one(n)

        assert B % 2 == 0 and TILES % 2 == 1

        @block.sync
        def _(sp):
            sp.nop().then_inc(xn2_stored, 16)
            sp.nop().then_inc(y_stored[0], 16)
            sp.nop().then_inc(y_stored[1], 16)
            sp.dma_start(stream[:, 0:2, :], x_t[:, 0:2, :]).then_inc(x_early, 16)
            sp.dma_start(ctx_sb[:, 0], ctxT[0].rearrange("(c p) t -> p c t", p=P)).then_inc(ctx_loaded, 16)
            sp.wait_ge(ctx_loaded, 16)
            sp.dma_start(ctx_sb[:, 1], ctxT[1].rearrange("(c p) t -> p c t", p=P)).then_inc(ctx_loaded, 16)
            sp.dma_start(wq_sb[:], wq.rearrange("(c p) n -> p c n", p=P)).then_inc(w_early, 16)
            sp.dma_start(wkv_sb[:], wkv.rearrange("(c p) n -> p c n", p=P)).then_inc(w_early, 16)
            sp.dma_start(stream[:, 2:B, :], x_t[:, 2:B, :]).then_inc(x_late, 16)
            sp.dma_start(wo_sb[:], wo.rearrange("(c p) n -> p c n", p=P)).then_inc(w_late, 16)
            sp.dma_start(gate_sb[:], gateT.rearrange("(c p) n -> p c n", p=P)).then_inc(w_late, 16)
            sp.dma_start(gbias_sb[:], gbias.partition_broadcast(P)).then_inc(w_late, 16)
            sp.dma_start(w13[:, 0], s13.rearrange("(c p) n -> p c n", p=P)).then_inc(w_shared, 16)
            sp.dma_start(w2[:, 0, 0:2, :], s2[0:2 * P].rearrange("(c p) n -> p c n", p=P)).then_inc(w_shared, 16)
            sp.dma_start(w2[0:ICH[2][1], 0, 2, :], s2[2 * P:INNER]).then_inc(w_shared, 16)
            sp.wait_ge(consts, 1)
            sp.dma_start(table_dram.rearrange("(p t) o -> p (t o)", p=P), zero_table[:]).then_inc(table_cleared, 16)

            def store_xn2(b, par):
                sp.wait_ge(xn2_stored, b * 16 + 16)
                sp.wait_ge(ln2_step, b * 5 + 5)
                sp.dma_start(xn2_dram[bass.ds(b * P, P)], xn2[:, par, :]).then_inc(xn2_stored, 16)

            def load_ctx(b, half):
                sp.wait_ge(v_done, b - 1)
                sp.wait_ge(ctx_loaded, b * 16)
                sp.dma_start(ctx_sb[:, half], ctxT[bass.ds(b, 1)].rearrange("o (c p) t -> p (o c) t", p=P)).then_inc(ctx_loaded, 16)

            def batch(b, par, prev, nxt, nxt2):
                if prev:
                    store_xn2(b - 1, 1 - par)
                if nxt2:
                    load_ctx(b + 2, par)
                if not nxt:
                    store_xn2(b, par)

            batches(batch, sp)

            def load_weights(n, j, buf, kept):
                e = sp.value_load(tile_expert_i[0:1, bass.ds(j, 1)], min_val=0, max_val=E - 1)
                new = {"cond": sp.value_load(tile_new[0:1, bass.ds(j, 1)], min_val=0, max_val=1)} if kept else {}
                if not (isinstance(n, int) and n == B - 2):
                    sp.wait_ge(u_done, n + 1)
                sp.dma_start(w13[:, buf], e13[bass.ds(e, 1)].rearrange("o (c p) n -> p (o c) n", p=P), **new).then_inc(w13_loaded[buf], 16)
                if not (isinstance(n, int) and n == B - 2):
                    sp.wait_ge(y_done, n + 1)
                sp.dma_start(w2[:, buf, 0:2, :], e2[bass.ds(e, 1), 0:2 * P].rearrange("o (c p) n -> p (o c) n", p=P), **new).then_inc(w2_loaded[buf], 16)
                sp.dma_start(w2[0:ICH[2][1], buf, 2, :], e2[bass.ds(e, 1), 2 * P:INNER].rearrange("o p n -> (o p) n"), **new).then_inc(w2_loaded[buf], 16)

            def load_rows(n, par):
                sp.dma_start(xe[:, par], xn2_dram[bass.ds(n * P, P)]).then_inc(xe_loaded[par], 16)

            sp.wait_ge(xn2_stored, B * 16 + 16)
            load_rows(0, 0)
            load_rows(1, 1)

            def tile(n, m, par, kind, following, beyond):
                if beyond == "shared":
                    sp.wait_ge(xeT_done, n + 1)
                    load_rows(n + 2, par)
                if beyond == "routed":
                    if kind == "shared":
                        sp.wait_ge(experts_known, 2)
                    load_weights(n, n - (B - 2), 1 - par, kept=kind == "routed")
                if kind == "routed":
                    sp.wait_ge(y_ready, n + 1)
                    sp.dma_start(y_dram[bass.ds((n - B) * P, P)], ye[:, par]).then_inc(y_stored[par], 16)

            expert_tiles(tile, sp)

            with sp.Fori(0, B) as b:
                sp.wait_ge(summed, b * 2 + 6)
                sp.dma_start(out_t[:, bass.ds(b, 1), :], stream[:, bass.ds(b, 1), :]).then_inc(out_stored, 16)
            sp.wait_ge(out_stored, B * 16)

        @block.tensor
        def _(pe):
            def transpose_rows(rows, done):
                for c in range(KC):
                    mm = pe.transpose(p_tr[:, c, :], rows[:, c * P:(c + 1) * P], ident[:])
                mm.then_inc(done, 1)

            def xn_transpose(b):
                pe.wait_ge(ln1_step, b * 4 + 4)
                transpose_rows(xn, xnT_done)

            def project_q(b, part):
                if part == 0:
                    pe.wait_ge(xnT_ready, b + 1)
                for c in (2 * part, 2 * part + 1):
                    mm = pe.matmul(p_qk[:, 0:DIM], xnT[:, c, :], wq_sb[:, c, :], start=(c == 0), stop=(c == KC - 1))

            def project_k(b, par):
                pe.wait_ge(ctx_loaded, b * 16 + 16)
                for c in range(KCC):
                    mm = pe.matmul(p_qk[:, DIM:2 * DIM], ctx_sb[:, par, c, :], wkv_sb[:, c, 0:DIM], start=(c == 0), stop=(c == KCC - 1))
                mm.then_inc(qk_done, 1)

            def project_v(b, par):
                for c in range(KCC):
                    mm = pe.matmul(p_v[:], ctx_sb[:, par, c, :], wkv_sb[:, c, DIM:2 * DIM], start=(c == 0), stop=(c == KCC - 1))
                mm.then_inc(v_done, 1)

            def stack_transpose(b, g):
                if g == 0:
                    pe.wait_ge(parts_ready, b * 3 + 3)
                elif g <= 2:
                    pe.wait_ge(qT_ready, b * 2 + g)
                else:
                    pe.wait_ge(kT_ready, b * 4 + 2)
                for n in range(8):
                    h = 2 * (8 * g + n)
                    mm = pe.transpose(p_st[:, n, :], parts[:, h:h + 2, :].rearrange("p h k -> p (h k)"), ident16[:])
                mm.then_inc(st_done, 1)

            def scores(b, c, prev):
                if c == 0:
                    pe.wait_ge(kT_ready, b * 4 + 4)
                if c >= 2:
                    pe.wait_ge(max_ready, b * NCH + c - 1)
                elif prev:
                    pe.wait_ge(exp_ready, b * NCH - 1 + c)
                for n in range(2):
                    pair = 2 * c + n
                    mm = pe.matmul(p_sc[c % 2][:, 2 * n * P:(2 * n + 2) * P], qT[:, pair, :],
                                   kT[:, pair].rearrange("p a t -> p (a t)"), start=True, stop=True)
                mm.then_inc(scored, 1)

            def negmax_transpose(b):
                pe.wait_ge(neg_step, b * 2 + 2)
                pe.transpose(p_st[:, 0, :], negmax[:], ident16[:]).then_inc(negT_done, 1)

            def shifted_scores(b, c):
                if c == 0:
                    pe.wait_ge(negT_ready, b + 1)
                if c >= 2:
                    pe.wait_ge(exp_ready, b * NCH + c - 1)
                for n in range(CH):
                    h = CH * c + n
                    to = p_sc[c % 2][:, n * P:(n + 1) * P]
                    pe.matmul(to, kT[:, h // 2, h % 2, :], qT[:, h // 2, :], start=True, stop=False)
                    mm = pe.matmul(to, select[:, h, :], negmaxT[:], start=False, stop=True)
                mm.then_inc(shifted, 1)

            def weigh_values(b, c, par, prev):
                if c == 0:
                    pe.wait_ge(vlo_ready, b + 1)
                if c == 0 and prev:
                    pe.wait_ge(attn_ready, b * 2)
                if c == NCH // 2:
                    pe.wait_ge(attn_ready, b * 2 + 1)
                pe.wait_ge(plo_ready, b * NCH + c + 1)
                for n in range(CH):
                    h = CH * c + n
                    to = pv[:, h % HALF, :]
                    w_hi, w_lo = (t[:, c % RING, n * P:(n + 1) * P] for t in (phi, plo))
                    pe.matmul(to, w_hi, vhi[:, par, h, :], start=True, stop=False)
                    pe.matmul(to, w_hi, vlo[:, par, h, :], start=False, stop=False)
                    mm = pe.matmul(to, w_lo, vhi[:, par, h, :], start=False, stop=True)
                mm.then_inc(pv_done, 1)

            def attn_transpose(b):
                pe.wait_ge(attn_ready, b * 2 + 2)
                transpose_rows(attn, attnT_done)

            def project_out(b):
                pe.wait_ge(attnT_ready, b + 1)
                for c in range(KC):
                    mm = pe.matmul(p_v[:], attnT[:, c, :], wo_sb[:, c, :], start=(c == 0), stop=(c == KC - 1))
                mm.then_inc(wo_done, 1)

            def xn2_transpose(b, par):
                pe.wait_ge(ln2_step, b * 5 + 5)
                transpose_rows(xn2[:, par], xn2T_done)

            def gate_logits(b):
                pe.wait_ge(xn2T_ready, b + 1)
                for c in range(KC):
                    mm = pe.matmul(p_tr[:, 0, 0:E], xn2T[:, c, :], gate_sb[:, c, :], start=(c == 0), stop=(c == KC - 1))
                mm.then_inc(gate_done, 1)

            pe.wait_ge(consts, 1)
            pe.wait_ge(w_early, 2 * 16)
            xn_transpose(0)
            project_q(0, 0)
            project_q(0, 1)
            project_k(0, 0)
            project_v(0, 0)
            pe.wait_ge(w_late, 3 * 16)
            pe.wait_ge(zeroed, 1)

            def batch(b, par, prev, nxt, nxt2):
                stack_transpose(b, 0)
                if prev:
                    attn_transpose(b - 1)
                stack_transpose(b, 1)
                if nxt:
                    if prev:
                        pe.wait_ge(attnT_ready, b)
                    xn_transpose(b + 1)
                stack_transpose(b, 2)
                if nxt:
                    pe.wait_ge(qk_ready, b + 1)
                    project_q(b + 1, 0)
                stack_transpose(b, 3)
                if nxt:
                    project_q(b + 1, 1)
                scores(b, 0, prev)
                scores(b, 1, prev)
                if nxt:
                    project_k(b + 1, 1 - par)
                scores(b, 2, prev)
                scores(b, 3, prev)
                pe.wait_ge(vlo_ready, b + 1)
                if prev:
                    project_out(b - 1)
                for c in range(4, NCH):
                    scores(b, c, prev)
                if nxt:
                    if prev:
                        pe.wait_ge(ln2_step, b * 5 - 4)
                    project_v(b + 1, 1 - par)
                negmax_transpose(b)
                for c in range(NCH):
                    shifted_scores(b, c)
                    if c == 3 and prev:
                        if nxt:
                            pe.wait_ge(xnT_ready, b + 2)
                        xn2_transpose(b - 1, 1 - par)
                    if c == 6 and prev:
                        gate_logits(b - 1)
                    if c >= 2:
                        weigh_values(b, c - 2, par, prev)
                weigh_values(b, NCH - 2, par, prev)
                weigh_values(b, NCH - 1, par, prev)
                if prev:
                    pe.wait_ge(logits_kept, b)
                else:
                    pe.wait_ge(xnT_ready, b + 2)
                if not nxt:
                    attn_transpose(b)
                    project_out(b)
                    xn2_transpose(b, par)
                    gate_logits(b)

            batches(batch, pe)

            def rows_transpose(n, m, par, kind):
                if kind == "shared":
                    pe.wait_ge(xe_loaded[par], m * 16 + 16)
                else:
                    pe.wait_ge(xe_gathered[par], (m - (B // 2 - 1)) * 16)
                for c in range(KC):
                    mm = pe.transpose(p_xT[:, c, :], xe[:, par, c * P:(c + 1) * P], ident[:])
                mm.then_inc(xeT_done, 1)

            def gate_up(n, m, par, kind):
                buf = 0
                pe.wait_ge(xeT_ready, n + 1)
                if kind == "routed":
                    buf = 1 - par
                    pe.wait_ge(w13_loaded[buf], (m - (B // 2 - 1)) * 16)
                for p_out, at, done in ((p_g, 0, g_done), (p_u, INNER, u_done)):
                    for c in range(KC):
                        mm = pe.matmul(p_out, xeT[:, par, c, :], w13[:, buf, c, at:at + INNER], start=(c == 0), stop=(c == KC - 1))
                    mm.then_inc(done, 1)

            def hidden_transpose(n):
                pe.wait_ge(hidden_ready, n + 1)
                for c, (i, k) in enumerate(ICH):
                    mm = pe.transpose(p_hT[0:k, c * P:(c + 1) * P], hidden[:, i:i + k], ident[:])
                mm.then_inc(hT_done, 1)

            def down(n, m, par, kind):
                pe.wait_ge(hT_ready, n * 2 + 2)
                if not (isinstance(n, int) and n < 2):
                    pe.wait_ge(y_ready, n - 1)
                buf = 0 if kind == "shared" else 1 - par
                if kind == "routed":
                    pe.wait_ge(w2_loaded[buf], (m - (B // 2 - 1)) * 32)
                for c, (i, k) in enumerate(ICH):
                    mm = pe.matmul(p_y[par][:], hiddenT[0:k, c, :], w2[0:k, buf, c, :], start=(c == 0), stop=(c == len(ICH) - 1))
                mm.then_inc(y_done, 1)

            def tile(n, m, par, kind, following, beyond):
                if following:
                    rows_transpose(n + 1, m + par, 1 - par, following)
                hidden_transpose(n)
                if following:
                    gate_up(n + 1, m + par, 1 - par, following)
                down(n, m, par, kind)

            def count(n):
                if n != 3:
                    return
                pe.wait_ge(masks_ready, 1)
                pe.matmul(p_st32[:], before[:], mask16[:].rearrange("p g e -> p (g e)"), start=True, stop=False)
                for g in range(GROUPS - 1):
                    rest = GROUPS - 1 - g
                    pe.matmul(p_rank[:, g + 1:GROUPS, :], ones16[:],
                              mask16[:, g:g + 1, :].broadcast_to([P, rest, E]),
                              start=False, stop=(g == GROUPS - 2))
                for g in range(GROUPS):
                    mm = pe.matmul(p_total, ones16[:], mask16[:, g, :], start=(g == 0), stop=(g == GROUPS - 1))
                mm.then_inc(counted, 1)

            pe.wait_ge(w_shared, 3 * 16)
            pe.wait_ge(logits_kept, B)
            pe.wait_ge(qk_ready, B)
            rows_transpose(0, 0, 0, "shared")
            gate_up(0, 0, 0, "shared")
            expert_tiles(tile, pe, count)

        @block.scalar
        def _(act):
            act.wait_ge(trig, 4)
            act.activation(sin_t[:].rearrange("p b (r two) -> p b r two", two=2)[:, :, :, 1], angle[:], ACT.Sin).then_inc(sines, 1)
            act.activation(cos_t[:].rearrange("p b (r two) -> p b r two", two=2)[:, :, :, 0], turns[:], ACT.Sin).then_inc(sines, 1)

            def read_tr(to, done, ready, n):
                act.wait_ge(done, n)
                act.copy(to, p_tr[:]).then_inc(ready, 1)

            def qT_copy(b, g):
                act.wait_ge(st_done, b * 4 + (g + 1))
                act.copy(qT[:, 8 * g:8 * g + 8, :], p_st[:]).then_inc(qT_ready, 1)

            def xnT_copy(b):
                if not (isinstance(b, int) and b == 0):
                    act.wait_ge(qk_done, b)
                read_tr(xnT[:], xnT_done, xnT_ready, b + 1)

            def qk_copy(b):
                act.wait_ge(qk_done, b + 1)
                if not (isinstance(b, int) and b == 0):
                    act.wait_ge(rot_step, b * 2)
                act.copy(qk[:], p_qk[:]).then_inc(qk_ready, 1)

            def vhi_copy(b, par):
                act.wait_ge(v_done, b + 1)
                if not (isinstance(b, int) and b < 2):
                    act.wait_ge(pv_done, b * NCH - NCH)
                act.copy(vhi[:, par, :, 0:HD], p_v[:].rearrange("p (h d) -> p h d", d=HD)).then_inc(vhi_ready, 1)

            def hi_copy(b):
                act.wait_ge(rot_step, b * 2 + 2)
                if not (isinstance(b, int) and b == 0):
                    act.wait_ge(st_done, b * 4)
                act.copy(parts[:, :, 0:HD], rot[:].rearrange("p (h d) -> p h d", d=HD)).then_inc(hi_ready, 1)

            def exp(b, c, prev):
                act.wait_ge(shifted, b * NCH + c + 1)
                if prev or c >= RING:
                    act.wait_ge(plo_ready, b * NCH + c + 1 - RING)
                act.activation(prob[:, c % RING, :], p_sc[c % 2][:], ACT.Exp, scale=SCALE).then_inc(exp_ready, 1)

            def keep_logits(b):
                act.wait_ge(gate_done, b + 1)
                act.copy(logits[:, bass.ds(b, 1), :], p_tr[:, 0:1, 0:E]).then_inc(logits_kept, 1)

            xnT_copy(0)
            qk_copy(0)
            act.wait_ge(zeroed, 1)
            vhi_copy(0, 0)
            hi_copy(0)

            def batch(b, par, prev, nxt, nxt2):
                qT_copy(b, 0)
                if prev:
                    read_tr(attnT[:], attnT_done, attnT_ready, b)
                qT_copy(b, 1)
                if nxt:
                    xnT_copy(b + 1)
                    qk_copy(b + 1)
                    vhi_copy(b + 1, 1 - par)
                exp(b, 0, prev)
                exp(b, 1, prev)
                if nxt:
                    hi_copy(b + 1)
                exp(b, 2, prev)
                exp(b, 3, prev)
                exp(b, 4, prev)
                if prev:
                    read_tr(xn2T[:], xn2T_done, xn2T_ready, b)
                for c in (5, 6, 7):
                    exp(b, c, prev)
                if prev:
                    keep_logits(b - 1)
                if not nxt:
                    read_tr(attnT[:], attnT_done, attnT_ready, b + 1)
                    read_tr(xn2T[:], xn2T_done, xn2T_ready, b + 1)
                    keep_logits(b)

            batches(batch, act)

            act.wait_ge(logits_kept, B)
            act.activation(score[:], logits[:], ACT.Exp, scale=-1.0).then_inc(gate_exp, 1)

            def xeT_copy(n, par):
                act.wait_ge(xeT_done, n + 1)
                if not (isinstance(n, int) and n < 2):
                    act.wait_ge(u_done, n - 1)
                act.copy(xeT[:, par], p_xT[:]).then_inc(xeT_ready, 1)

            def gate_act(n):
                act.wait_ge(g_done, n + 1)
                if not (isinstance(n, int) and n == 0):
                    act.wait_ge(hidden_ready, n)
                act.activation(act_g[:], p_g, ACT.Silu).then_inc(act_ready, 1)

            xeT_copy(0, 0)
            gate_act(0)

            def tile(n, m, par, kind, following, beyond):
                if following:
                    xeT_copy(n + 1, 1 - par)
                    gate_act(n + 1)

            expert_tiles(tile, act)

        @block.vector
        def _(dve):
            dve.memset(negmax[:].bitcast(F32), 0.0)
            dve.memset(kT[:].bitcast(F32).rearrange("p a b t -> p (a b t)"), 0.0)
            dve.memset(vhi[:], 1.0)
            dve.memset(vlo[:], 0.0).then_inc(zeroed, 1)
            dve.wait_ge(pos_loaded, 16)
            half = ROT // 2
            for p in range(2):
                for i in range(half):
                    last = dve.tensor_scalar(angle[:, :, p * half + i], pos_sb[:, :, p], 10000.0 ** (-i / half), None, ALU.mult)
            last.then_inc(trig, 1)
            dve.wait_ge(trig, 1)
            dve.tensor_scalar(turns[:], angle[:], 1 / (2 * pi), ROUND, ALU.mult, ALU.add).then_inc(trig, 1)
            dve.wait_ge(trig, 2)
            dve.tensor_scalar(turns[:], turns[:], -ROUND, -2 * pi, ALU.add, ALU.mult).then_inc(trig, 1)
            dve.wait_ge(trig, 3)
            dve.tensor_tensor(turns[:], turns[:], angle[:], ALU.add).then_inc(rot_setup, 1)
            dve.wait_ge(rot_setup, 1)
            dve.tensor_scalar(angle[:], turns[:], 3.1415925, -3.1415925, ALU.min, ALU.max).then_inc(rot_setup, 1)
            dve.wait_ge(rot_setup, 2)
            dve.scalar_tensor_tensor(turns[:], angle[:], -1.0, angle[:], ALU.mult, ALU.min).then_inc(rot_setup, 1)
            dve.wait_ge(rot_setup, 3)
            dve.tensor_scalar(turns[:], turns[:], pi / 2, None, ALU.add).then_inc(trig, 1)
            dve.wait_ge(sines, 2)
            cos_p = cos_t[:].rearrange("p b (r two) -> p b r two", two=2)
            sin_p = sin_t[:].rearrange("p b (r two) -> p b r two", two=2)
            dve.tensor_copy(cos_p[:, :, :, 1], cos_p[:, :, :, 0])
            dve.tensor_scalar(sin_p[:, :, :, 0], sin_p[:, :, :, 1], -1.0, None, ALU.mult).then_inc(tables_ready, 1)

            def ln(step, per, at, b, rows, stats, mv, rstd_ready, rstd, to, part):
                base = b * per + at
                if part == "stats":
                    dve.bn_stats(stats[:], rows).then_inc(step, 1)
                    dve.wait_ge(step, base + 1)
                    dve.memset(carrier_dve[:], 0.0)
                    dve.bn_aggr(mv[:], stats[:]).then_inc(step, 1)
                    dve.wait_ge(step, base + 2)
                    dve.tensor_scalar(mv[:, 1:2], mv[:, 1:2], EPS, None, ALU.add).then_inc(step, 1)
                else:
                    dve.wait_ge(rstd_ready, b + 1)
                    dve.tensor_scalar(to, rows, mv[:, 0:1], rstd[:, 0:1], ALU.subtract, ALU.mult).then_inc(step, 1)

            def row(b):
                return stream[:, bass.ds(b, 1), :].rearrange("p o d -> p (o d)")

            def ln1(b, part):
                if part == "norm" and not (isinstance(b, int) and b == 0):
                    dve.wait_ge(xnT_done, b)
                ln(ln1_step, 4, 0, b, row(b), stats1, mv1, rstd1_ready, rstd1, xn[:], part)

            def ln2(b, par, part):
                if part == "norm":
                    dve.wait_ge(xn2_stored, b * 16 + 16)
                ln(ln2_step, 5, 1, b, row(b), stats2, mv2, rstd2_ready, rstd2, xn2[:, par, :], part)

            def residual(b):
                dve.wait_ge(wo_done, b + 1)
                dve.wait_ge(bias_added, b + 1)
                dve.tensor_tensor(row(b), p_v[:], row(b), ALU.add).then_inc(ln2_step, 1)
                dve.wait_ge(ln2_step, b * 5 + 1)

            def vlo_make(b, par):
                dve.wait_ge(vhi_ready, b + 1)
                dve.tensor_tensor(vlo[:, par, :, 0:HD], p_v[:].rearrange("p (h d) -> p h d", d=HD),
                                  vhi[:, par, :, 0:HD], ALU.subtract).then_inc(vlo_ready, 1)

            def rotate_cos(b):
                dve.wait_ge(qk_ready, b + 1)
                if not (isinstance(b, int) and b == 0):
                    dve.wait_ge(lo_ready, b)
                c = cos_t[:, bass.ds(b, 1), :].broadcast_to([P, 2 * HEADS, HD])
                dve.tensor_tensor(rot[:].rearrange("p (h d) -> p h d", d=HD), qk[:].rearrange("p (h d) -> p h d", d=HD), c, ALU.mult).then_inc(rot_step, 1)

            def rotate_add(b):
                dve.wait_ge(rot_step, b * 2 + 1)
                dve.wait_ge(swapped, b * 2 + 2)
                dve.tensor_tensor(rot[:], rot[:], swp[:], ALU.add).then_inc(rot_step, 1)

            def parts_double(b):
                dve.wait_ge(lo_ready, b + 1)
                q, k = parts[:, 0:HEADS], parts[:, HEADS:2 * HEADS]
                dve.tensor_copy(q[:, :, 2 * HD:4 * HD], q[:, :, 0:2 * HD]).then_inc(parts_ready, 1)
                dve.tensor_copy(k[:, :, 2 * HD:3 * HD], k[:, :, HD:2 * HD]).then_inc(parts_ready, 1)
                dve.tensor_copy(k[:, :, 3 * HD:4 * HD], k[:, :, 0:HD]).then_inc(parts_ready, 1)

            def kT_copy(b, g):
                dve.wait_ge(st_done, b * 4 + 3 + g)
                for a in range(2):
                    rows = slice(a * STACK, (a + 1) * STACK)
                    dve.tensor_copy(kT[rows, 8 * g:8 * g + 8, a, :], p_st[rows]).then_inc(kT_ready, 1)

            def row_max(b, c):
                dve.wait_ge(scored, b * NCH + c + 1)
                dve.tensor_reduce(rowmax[:, CH * c:CH * c + CH], p_sc[c % 2][:].rearrange("p (h t) -> p h t", t=P),
                                  AX_X, ALU.max).then_inc(max_ready, 1)

            def neg_max(b):
                dve.wait_ge(max_ready, b * NCH + NCH)
                dve.tensor_scalar(negmax[:, 0:HEADS], rowmax[:], -1.0, None, ALU.mult).then_inc(neg_step, 1)
                dve.wait_ge(neg_step, b * 2 + 1)
                dve.scalar_tensor_tensor(negmax[:, HEADS:2 * HEADS], rowmax[:], -1.0, negmax[:, 0:HEADS],
                                         ALU.mult, ALU.subtract).then_inc(neg_step, 1)

            def neg_copy(b):
                dve.wait_ge(negT_done, b + 1)
                dve.tensor_copy(negmaxT[:], p_st[:, 0, :]).then_inc(negT_ready, 1)

            def phi_make(b, c, prev):
                dve.wait_ge(exp_ready, b * NCH + c + 1)
                if prev or c >= RING:
                    dve.wait_ge(pv_done, b * NCH + c + 1 - RING)
                dve.tensor_copy(phi[:, c % RING, :], prob[:, c % RING, :]).then_inc(phi_ready, 1)

            def normalise(b, half, prev):
                dve.wait_ge(pv_done, b * NCH + (half + 1) * (NCH // 2))
                if half:
                    dve.wait_ge(attn_ready, b * 2 + 1)
                elif prev:
                    dve.wait_ge(attnT_done, b)
                dve.reciprocal(recip[:], pv[:, :, HD]).then_inc(recip_ready, 1)
                dve.wait_ge(recip_ready, b * 2 + half + 1)
                to = attn[:].rearrange("p (h d) -> p h d", d=HD)[:, half * HALF:(half + 1) * HALF, :]
                dve.tensor_tensor(to, pv[:, :, 0:HD], recip[:].rearrange("p (h o) -> p h o", o=1).broadcast_to([P, HALF, HD]),
                                  ALU.mult).then_inc(attn_ready, 1)

            dve.wait_ge(x_early, 16)
            ln1(0, "stats")
            ln1(0, "norm")
            dve.wait_ge(tables_ready, 1)
            ln1(1, "stats")
            ln1(1, "norm")
            rotate_cos(0)
            vlo_make(0, 0)
            rotate_add(0)
            parts_double(0)
            dve.wait_ge(x_late, 16)

            def batch(b, par, prev, nxt, nxt2):
                kT_copy(b, 0)
                kT_copy(b, 1)
                for c in range(4):
                    row_max(b, c)
                if nxt:
                    rotate_cos(b + 1)
                if prev:
                    residual(b - 1)
                for c in range(4, NCH):
                    row_max(b, c)
                neg_max(b)
                neg_copy(b)
                if prev:
                    ln2(b - 1, 1 - par, "stats")
                if nxt:
                    vlo_make(b + 1, 1 - par)
                phi_make(b, 0, prev)
                if nxt:
                    rotate_add(b + 1)
                phi_make(b, 1, prev)
                if prev:
                    ln2(b - 1, 1 - par, "norm")
                phi_make(b, 2, prev)
                phi_make(b, 3, prev)
                if nxt2:
                    ln1(b + 2, "stats")
                phi_make(b, 4, prev)
                phi_make(b, 5, prev)
                if nxt2:
                    ln1(b + 2, "norm")
                normalise(b, 0, prev)
                phi_make(b, 6, prev)
                phi_make(b, 7, prev)
                if nxt:
                    parts_double(b + 1)
                normalise(b, 1, prev)
                if not nxt:
                    residual(b)
                    ln2(b, par, "stats")
                    ln2(b, par, "norm")

            batches(batch, dve)

            def hidden_make(n):
                dve.wait_ge(act_ready, n + 1)
                dve.wait_ge(u_done, n + 1)
                if not (isinstance(n, int) and n == 0):
                    dve.wait_ge(hT_done, n)
                dve.tensor_tensor(hidden[:], p_u, act_g[:], ALU.mult).then_inc(hidden_ready, 1)

            def hT_copy(n):
                dve.wait_ge(hT_done, n + 1)
                if not (isinstance(n, int) and n == 0):
                    dve.wait_ge(y_done, n)
                dve.tensor_copy(hiddenT[:, 0:2, :], p_hT[:, 0:2 * P].rearrange("p (c t) -> p c t", t=P)).then_inc(hT_ready, 1)
                k = ICH[2][1]
                dve.tensor_copy(hiddenT[0:k, 2, :], p_hT[0:k, 2 * P:3 * P]).then_inc(hT_ready, 1)

            def y_take(n, m, par, kind):
                dve.wait_ge(y_done, n + 1)
                if kind == "shared":
                    dve.tensor_tensor(row(n), p_y[par][:], row(n), ALU.add).then_inc(y_ready, 1)
                else:
                    dve.wait_ge(y_stored[par], (m - (B // 2 - 1)) * 16)
                    dve.tensor_copy(ye[:, par], p_y[par][:]).then_inc(y_ready, 1)

            hidden_make(0)

            def tile(n, m, par, kind, following, beyond):
                hT_copy(n)
                if following:
                    hidden_make(n + 1)
                y_take(n, m, par, kind)

            steps = [0]

            def then(ins):
                ins.then_inc(route, 1)
                steps[0] += 1
                dve.wait_ge(route, steps[0])

            def each_e(row_of_e, n):
                return row_of_e.rearrange("p (o e) -> p o e", o=1).broadcast_to([P, n, E])

            def scores_and_two_best(batches_of):
                for b in batches_of:
                    then(dve.max(best[:, b, :], routing[:, b, :]))
                    then(dve.max_index(best_at[:, b, :], best[:, b, :], routing[:, b, :]))

            def beside(n):
                if n == 0:
                    dve.wait_ge(gate_exp, 1)
                    then(dve.tensor_scalar(score[:], score[:], 1.0, None, ALU.add))
                    then(dve.reciprocal(score[:], score[:]))
                    then(dve.tensor_tensor(routing[:], score[:], each_e(gbias_sb[:], B), ALU.add))
                    scores_and_two_best(range(0, 2))
                if n == 1:
                    scores_and_two_best(range(2, 9))
                if n == 2:
                    scores_and_two_best(range(9, B))
                    then(dve.tensor_copy(chosen[:], best_at[:, :, 0:TOPK]))
                    chosen_g = chosen[:].rearrange("p b (k o) -> p (b k) o", o=1)
                    then(dve.tensor_tensor(mask[:], each_e(expert_no[:], GROUPS), chosen_g.broadcast_to([P, GROUPS, E]), ALU.is_equal))
                    dve.tensor_copy(mask16[:], mask[:]).then_inc(masks_ready, 1)
                if n == 3:
                    s4 = score[:].rearrange("p b (o e) -> p b o e", o=1).broadcast_to([P, B, TOPK, E])
                    w4 = work[:].rearrange("p (b k) e -> p b k e", k=TOPK)
                    m4 = mask[:].rearrange("p (b k) e -> p b k e", k=TOPK)
                    then(dve.tensor_tensor(w4, m4, s4, ALU.mult))
                    then(dve.tensor_reduce(picked[:], w4, AX_X, ALU.add))
                    then(dve.tensor_reduce(pick_sum[:], picked[:], AX_X, ALU.add))
                    then(dve.reciprocal(pick_sum[:], pick_sum[:]))
                    dve.tensor_tensor(gates[:], picked[:], pick_sum[:].rearrange("p (b o) -> p b o", o=1).broadcast_to([P, B, TOPK]),
                                      ALU.mult).then_inc(gates_known, 1)
                if n == 4:
                    dve.wait_ge(counted, 1)
                    then(dve.tensor_scalar(tiles_of[:], p_total, 1 / P, (P - 1) / P - 0.5 + 0.5 / P, ALU.mult, ALU.add))
                    then(dve.tensor_scalar(tiles_of[:], tiles_of[:], ROUND, -ROUND, ALU.add, ALU.add))
                    then(dve.tensor_tensor_scan(tiles_end[:], one_e[:], tiles_of[:], 0.0, ALU.mult, ALU.add))
                    then(dve.tensor_tensor(first_slot[:], tiles_end[:], tiles_of[:], ALU.subtract))
                    then(dve.tensor_tensor(tile_cmp[:], each_e(tiles_end[:], TILES),
                                           tile_no[:].rearrange("p (t o) -> p t o", o=1).broadcast_to([P, TILES, E]), ALU.is_le))
                    then(dve.tensor_reduce(tile_expert[:], tile_cmp[:], AX_X, ALU.add))
                    then(dve.tensor_scalar(tile_expert[:], tile_expert[:], float(E - 1), None, ALU.min))
                    dve.tensor_copy(tile_expert_i[:], tile_expert[:]).then_inc(experts_known, 1)
                    dve.tensor_tensor(tile_new[:, 2:TILES], tile_expert[:, 2:TILES], tile_expert[:, 0:TILES - 2],
                                      ALU.not_equal).then_inc(experts_known, 1)
                if n == 5:
                    then(dve.scalar_tensor_tensor(work[:], each_e(first_slot[:], GROUPS), float(P), p_rank, ALU.mult, ALU.add))
                    then(dve.tensor_tensor(work[:], work[:], mask[:], ALU.mult))
                    then(dve.tensor_reduce(slot[:], work[:], AX_X, ALU.add))
                    then(dve.tensor_scalar(slot_tile[:], slot[:], 1 / P, -0.5 + 0.5 / P, ALU.mult, ALU.add))
                    then(dve.tensor_scalar(slot_tile[:], slot_tile[:], ROUND, -ROUND, ALU.add, ALU.add))
                    then(dve.tensor_scalar(slot_at[:], slot[:], float(TILES), None, ALU.mult))
                    then(dve.scalar_tensor_tensor(slot_at[:], slot_tile[:], float(1 - P * TILES), slot_at[:], ALU.mult, ALU.add))
                    dve.tensor_copy(slot_u[:], slot[:]).then_inc(slots_known, 1)
                    dve.tensor_copy(slot_at_u[:], slot_at[:]).then_inc(slots_known, 1)

            expert_tiles(tile, dve, beside)

            dve.wait_ge(gates_known, 1)
            dve.nop().then_inc(summed, 4)
            with dve.Fori(0, B // 2) as r:
                for u in range(2):
                    b = r * 2 + u
                    dve.wait_ge(y_gathered[u], r * 32 + 32)
                    for k in range(TOPK):
                        g = gates[:, bass.ds(b, 1), k:k + 1].rearrange("p b k -> p (b k)")
                        dve.scalar_tensor_tensor(row(b), y_got[u][k], g, row(b), ALU.mult, ALU.add).then_inc(summed, 1)
                        dve.wait_ge(summed, b * 2 + (k + 5))

        @block.gpsimd
        def _(pool):
            pool.dma_start(pos_sb[:], pos.rearrange("b p c -> p b c")).then_inc(pos_loaded, 16)
            pool.dma_start(bout_sb[:], bout.partition_broadcast(P)).then_inc(w_bout, 16)
            pool.memset(ident[:], 0.0).then_inc(cleared, 1)
            pool.memset(ident16[:], 0.0).then_inc(cleared, 1)
            pool.memset(before[:], 1.0).then_inc(cleared, 1)
            pool.memset(select[:], 0.0).then_inc(cleared, 1)
            pool.memset(ones16[:], 1.0).then_inc(cleared, 1)
            pool.memset(one_e[:], 1.0).then_inc(cleared, 1)
            pool.memset(minus_half[:], -0.5).then_inc(cleared, 1)
            pool.memset(zero_table[:], 0).then_inc(cleared, 1)
            pool.iota(token_no[:], [[P, B], [0, TOPK]], base=0, channel_multiplier=1).then_inc(cleared, 1)
            pool.iota(expert_no[:], [[1, E]], base=0, channel_multiplier=0, allow_small_or_imprecise_dtypes=True).then_inc(cleared, 1)
            pool.iota(tile_no[:], [[1, TILES]], base=0, channel_multiplier=0, allow_small_or_imprecise_dtypes=True).then_inc(cleared, 1)
            pool.wait_ge(cleared, 11)
            for m in (ident, ident16):
                pool.affine_select(out=m[:], in_=m[:], compare_op=ALU.not_equal, fill=1.0, base=0,
                                   pattern=[[-1, P]], channel_multiplier=1).then_inc(cleared, 1)
            pool.affine_select(out=before[:], in_=before[:], compare_op=ALU.is_gt, fill=0.0, base=0,
                               pattern=[[1, P]], channel_multiplier=-1).then_inc(cleared, 1)
            for a in range(2):
                pool.wait_ge(cleared, 14 + a)
                rows = select[32 * a:32 * a + HEADS]
                pool.affine_select(out=rows, in_=rows, compare_op=ALU.not_equal, fill=1.0, base=0,
                                   pattern=[[-1, HEADS], [0, P]], channel_multiplier=1).then_inc(cleared, 1)
            pool.wait_ge(cleared, 16)
            pool.nop().then_inc(consts, 1)

            def rstd(step, need, to, mv, ready):
                pool.wait_ge(step, need)
                pool.tensor_tensor(to[:], mv[:, 1:2], minus_half[:], ALU.pow).then_inc(ready, 1)

            def rstd1_make(b):
                rstd(ln1_step, b * 4 + 3, rstd1, mv1, rstd1_ready)

            def rstd2_make(b):
                rstd(ln2_step, b * 5 + 4, rstd2, mv2, rstd2_ready)

            def row(b):
                return stream[:, bass.ds(b, 1), :].rearrange("p o d -> p (o d)")

            def bias_add(b):
                pool.wait_ge(ln1_step, b * 4 + 4)
                pool.tensor_tensor(row(b), row(b), bout_sb[:], ALU.add).then_inc(bias_added, 1)

            def rotate_swapped(b):
                pool.wait_ge(qk_ready, b + 1)
                if not (isinstance(b, int) and b == 0):
                    pool.wait_ge(rot_step, b * 2)
                q3 = qk[:].rearrange("p (h r two) -> p h r two", two=2, r=ROT)
                s3 = swp[:].rearrange("p (h r two) -> p h r two", two=2, r=ROT)
                t3 = sin_t[:, bass.ds(b, 1), :].rearrange("p o (r two) -> p o r two", two=2)
                for side in range(2):
                    pool.tensor_tensor(s3[:, :, :, side], q3[:, :, :, 1 - side],
                                       t3[:, :, :, side].broadcast_to([P, 2 * HEADS, ROT]), ALU.mult).then_inc(swapped, 1)

            def lo_make(b):
                pool.wait_ge(hi_ready, b + 1)
                pool.tensor_tensor(parts[:, :, HD:2 * HD], rot[:].rearrange("p (h d) -> p h d", d=HD), parts[:, :, 0:HD],
                                   ALU.subtract).then_inc(lo_ready, 1)

            def plo_make(b, c, prev):
                pool.wait_ge(phi_ready, b * NCH + c + 1)
                if prev or c >= RING:
                    pool.wait_ge(pv_done, b * NCH + c + 1 - RING)
                pool.tensor_tensor(plo[:, c % RING, :], prob[:, c % RING, :], phi[:, c % RING, :], ALU.subtract).then_inc(plo_ready, 1)

            rstd1_make(0)
            pool.wait_ge(tables_ready, 1)
            rstd1_make(1)
            rotate_swapped(0)
            lo_make(0)
            pool.wait_ge(w_bout, 16)

            def batch(b, par, prev, nxt, nxt2):
                bias_add(b)
                if nxt:
                    rotate_swapped(b + 1)
                if prev:
                    rstd2_make(b - 1)
                plo_make(b, 0, prev)
                plo_make(b, 1, prev)
                if nxt:
                    lo_make(b + 1)
                plo_make(b, 2, prev)
                plo_make(b, 3, prev)
                if nxt2:
                    rstd1_make(b + 2)
                for c in range(4, NCH):
                    plo_make(b, c, prev)
                if not nxt:
                    rstd2_make(b)

            batches(batch, pool)

            pool.wait_ge(slots_known, 2)
            pool.wait_ge(xn2_stored, B * 16 + 16)
            with pool.Fori(0, GROUPS // SCATTERS) as r:
                for n in range(SCATTERS):
                    g = r * SCATTERS + n
                    pool.tensor_copy(scat_at[:, n], slot_at_u[:, bass.ds(g, 1)]).then_inc(scat_copied, 1)
                    pool.tensor_copy(scat_id[:, n], token_no[:, bass.ds(g, 1)]).then_inc(scat_copied, 1)
                pool.wait_ge(table_cleared, 16)
                pool.wait_ge(scat_copied, r * (2 * SCATTERS) + 2 * SCATTERS)
                pool.tensor_tensor(carrier_pool[:], minus_half[:], minus_half[:], ALU.mult)
                for n in range(SCATTERS):
                    pool.indirect_dma_start(out=table_dram, out_offset=bass.IndirectOffsetOnAxis(ap=scat_at[:, n], axis=0),
                                            in_=scat_id[:, n], in_offset=None).then_inc(scattered, 16)
                pool.wait_ge(scattered, r * (16 * SCATTERS) + 16 * SCATTERS)
            pool.dma_start(table[:], table_dram.rearrange("(p t) o -> p (t o)", p=P)).then_inc(table_loaded, 16)
            pool.wait_ge(table_loaded, 16)

            def gather_rows(n, m, par):
                pool.wait_ge(xeT_done, n - 1)
                pool.tensor_copy(row_at[:, par], table[:, bass.ds(n - B, 1)]).then_inc(row_copied, 1)
                pool.wait_ge(table_loaded, 16)
                pool.wait_ge(row_copied, n - (B - 1))
                pool.tensor_tensor(carrier_pool[:], minus_half[:], minus_half[:], ALU.mult)
                pool.indirect_dma_start(out=xe[:, par], out_offset=None, in_=xn2_dram,
                                        in_offset=bass.IndirectOffsetOnAxis(ap=row_at[:, par], axis=0)).then_inc(xe_gathered[par], 16)

            with pool.Fori(0, (TILES - 1) // 2) as r:
                for u in range(2):
                    gather_rows(r * 2 + (B + u), None, u)
            gather_rows(B + TILES - 1, None, 0)

            pool.wait_ge(y_stored[0], (TILES + 3) // 2 * 16)
            pool.wait_ge(y_stored[1], (TILES // 2 + 1) * 16)
            with pool.Fori(0, B // 2) as r:
                for u in range(2):
                    b = r * 2 + u
                    pool.wait_ge(summed, b * 2 + 2)
                    pool.tensor_copy(y_at[:, u, :], slot_u[:, bass.ds(b * 2, 2)]).then_inc(y_at_copied, 1)
                    pool.wait_ge(y_at_copied, b + 1)
                    pool.tensor_tensor(carrier_pool[:], minus_half[:], minus_half[:], ALU.mult)
                    for k in range(TOPK):
                        pool.indirect_dma_start(out=y_got[u][k], out_offset=None, in_=y_dram,
                                                in_offset=bass.IndirectOffsetOnAxis(ap=y_at[:, u, k:k + 1], axis=0)).then_inc(y_gathered[u], 16)


def kernel(**inputs):
    import numpy as np
    import concourse.bacc as bacc
    from concourse.bass_utils import run_bass_kernel_spmd

    def turned(a):
        return np.ascontiguousarray(np.swapaxes(np.asarray(a), -1, -2))

    w = {k[len("L0_"):]: np.asarray(v) for k, v in inputs.items() if k.startswith("L0_")}
    arrays = {
        "x": np.ascontiguousarray(inputs["x"]),
        "ctxT": turned(inputs["ctx_1024"]),
        "pos": np.ascontiguousarray(inputs["fside_BxSx2_0"]),
        "wq": w["xattn_Wq"], "wkv": w["xattn_Wkv"], "wo": w["xattn_Wout"], "bout": w["xattn_bout"],
        "gateT": turned(w["ffn_gate_w"]), "gbias": w["ffn_bias"],
        "s13": turned(np.concatenate([w["ffn_shared_w1"], w["ffn_shared_w3"]], axis=0)),
        "s2": turned(w["ffn_shared_w2"]),
        "e13": turned(np.concatenate([w["ffn_w1"], w["ffn_w3"]], axis=1)),
        "e2": turned(w["ffn_w2"]),
    }
    arrays = {k: np.ascontiguousarray(v) for k, v in arrays.items()}
    nc = bacc.Bacc("TRN2", target_bir_lowering=False, num_devices=1)
    args = {k: nc.dram_tensor(k, v.shape, mybir.dt.from_np(v.dtype), kind="ExternalInput").ap() for k, v in arrays.items()}
    out = nc.dram_tensor("out", (B, P, DIM), F32, kind="ExternalOutput").ap()
    build(nc, out=out, **args)
    r = run_bass_kernel_spmd(nc, [arrays], core_ids=[0])
    return r.results[0]["out"]
```

```python
from contextlib import ExitStack
from math import pi

import concourse.bass as bass
from concourse import mybir

F32 = mybir.dt.float32
F16 = mybir.dt.float16
U32 = mybir.dt.uint32
I32 = mybir.dt.int32
ACT = mybir.ActivationFunctionType
ALU = mybir.AluOpType
AX_X = mybir.AxisListType.X

P = 128
B = 16
DIM, CTX_DIM = 512, 256
KC, KCC = DIM // P, CTX_DIM // P
HEADS, HD = 32, 16
PAIRS = HEADS // 2
STACK = 4 * HD
VW = HD + 1
CH = 4
NCH = HEADS // CH
HALF = HEADS // 2
RING = 4
GOT = 4
SCATTERS = 8
PEELED = 8
ROT = HD // 2
E, TOPK = 16, 2
INNER = 352
W13 = 2 * INNER
ICH = [(0, P), (P, P), (2 * P, INNER - 2 * P)]
T = B * P
GROUPS = B * TOPK
TILES = (T * TOPK) // P + E - 1
EPS = 1e-5
SCALE = HD ** -0.5
ROUND = float(3 << 22)


def build(nc, x, ctxT, pos, wq, wkv, wo, bout, gateT, gbias, s13, s2, e13, e2, out):
    with ExitStack() as stack:
        def sb(name, shape, dt=F32):
            return stack.enter_context(nc.sbuf_tensor(name, shape, dt))

        def ps(name, shape, dt=F32):
            return stack.enter_context(nc.psum_tensor(name, shape, dt))

        def sem(name):
            return stack.enter_context(nc.semaphore(name))

        xn2_dram = nc.dram_tensor("xn2_dram", [T, DIM], F32, kind="Internal").ap()
        table_dram = nc.dram_tensor("table_dram", [P * TILES, 1], U32, kind="Internal").ap()
        y_dram = nc.dram_tensor("y_dram", [TILES * P, DIM], F32, kind="Internal").ap()

        stream = sb("stream", [P, B, DIM])
        wq_sb = sb("wq_sb", [P, KC, DIM])
        wkv_sb = sb("wkv_sb", [P, KCC, 2 * DIM])
        wo_sb = sb("wo_sb", [P, KC, DIM])
        bout_sb = sb("bout_sb", [P, DIM])
        gate_sb = sb("gate_sb", [P, KC, E])
        gbias_sb = sb("gbias_sb", [P, E])
        pos_sb = sb("pos_sb", [P, B, 2])
        ident = sb("ident", [P, P])
        ident16 = sb("ident16", [P, P], F16)
        select = sb("select", [P, HEADS, P], F16)
        before = sb("before", [P, P], F16)
        ones16 = sb("ones16", [P, P], F16)
        carrier_dve, carrier_pool = sb("carrier_dve", [P, 1]), sb("carrier_pool", [P, 1])
        minus_half = sb("minus_half", [P, 1])
        angle = sb("angle", [P, B, ROT])
        turns = sb("turns", [P, B, ROT])
        cos_t = sb("cos_t", [P, B, HD])
        sin_t = sb("sin_t", [P, B, HD])
        ctx_sb = sb("ctx_sb", [P, 2, KCC, P])
        stats1, mv1, rstd1 = sb("stats1", [P, 6]), sb("mv1", [P, 2]), sb("rstd1", [P, 1])
        stats2, mv2, rstd2 = sb("stats2", [P, 6]), sb("mv2", [P, 2]), sb("rstd2", [P, 1])
        xn = sb("xn", [P, DIM])
        xnT = sb("xnT", [P, KC, P])
        qk = sb("qk", [P, 2 * DIM])
        rot = sb("rot", [P, 2 * DIM])
        swp = sb("swp", [P, 2 * DIM])
        parts = sb("parts", [P, 2 * HEADS, STACK], F16)
        qT = sb("qT", [P, PAIRS, P], F16)
        kT = sb("kT", [P, PAIRS, 2, P], F16)
        vhi = sb("vhi", [P, 2, HEADS, VW], F16)
        vlo = sb("vlo", [P, 2, HEADS, VW], F16)
        rowmax = sb("rowmax", [P, HEADS])
        negmax = sb("negmax", [P, P], F16)
        negmaxT = sb("negmaxT", [P, P], F16)
        prob = sb("prob", [P, RING, CH * P])
        phi = sb("phi", [P, RING, CH * P], F16)
        plo = sb("plo", [P, RING, CH * P], F16)
        recip = sb("recip", [P, HALF])
        attn = sb("attn", [P, DIM])
        attnT = sb("attnT", [P, KC, P])
        xn2 = sb("xn2", [P, 2, DIM])
        xn2T = sb("xn2T", [P, KC, P])
        logits = sb("logits", [P, B, E])
        score = sb("score", [P, B, E])
        routing = sb("routing", [P, B, E])
        best = sb("best", [P, B, 8])
        best_at = sb("best_at", [P, B, 8], U32)
        chosen = sb("chosen", [P, B, TOPK])
        expert_no = sb("expert_no", [P, E])
        mask = sb("mask", [P, GROUPS, E])
        mask16 = sb("mask16", [P, GROUPS, E], F16)
        work = sb("work", [P, GROUPS, E])
        picked = sb("picked", [P, B, TOPK])
        pick_sum = sb("pick_sum", [P, B])
        gates = sb("gates", [P, B, TOPK])
        tiles_of = sb("tiles_of", [P, E])
        one_e = sb("one_e", [P, E])
        tiles_end = sb("tiles_end", [P, E])
        first_slot = sb("first_slot", [P, E])
        slot = sb("slot", [P, GROUPS])
        slot_tile = sb("slot_tile", [P, GROUPS])
        slot_at = sb("slot_at", [P, GROUPS])
        slot_u = sb("slot_u", [P, GROUPS], U32)
        slot_at_u = sb("slot_at_u", [P, GROUPS], U32)
        token_no = sb("token_no", [P, GROUPS], U32)
        zero_table = sb("zero_table", [P, TILES], U32)
        tile_no = sb("tile_no", [P, TILES])
        tile_cmp = sb("tile_cmp", [P, TILES, E])
        tile_expert = sb("tile_expert", [P, TILES])
        tile_expert_i = sb("tile_expert_i", [P, TILES], I32)
        tile_new = sb("tile_new", [P, TILES], I32)
        tiles_in_use = sb("tiles_in_use", [P, 1], I32)
        table = sb("table", [P, TILES], U32)
        scat_at = sb("scat_at", [P, SCATTERS, 1], U32)
        scat_id = sb("scat_id", [P, SCATTERS, 1], U32)
        w13 = sb("w13", [P, 2, KC, W13])
        w2 = sb("w2", [P, 2, len(ICH), DIM])
        row_at = sb("row_at", [P, 2, 1], U32)
        xe = sb("xe", [P, 2, DIM])
        xeT = sb("xeT", [P, 2, KC, P])
        act_g = sb("act_g", [P, INNER])
        hidden = sb("hidden", [P, INNER])
        hiddenT = sb("hiddenT", [P, len(ICH), P])
        ye = sb("ye", [P, 2, DIM])
        y_at = sb("y_at", [P, GOT, TOPK], U32)
        free = [prob[:, n, :] for n in range(RING)] + [t[:, n * DIM:(n + 1) * DIM] for t in (qk, rot) for n in range(2)]
        y_got = [free[TOPK * n:TOPK * n + TOPK] for n in range(GOT)]

        p_tr = ps("p_tr", [P, KC, P])
        p_qk = ps("p_qk", [P, 2 * DIM])
        p_v = ps("p_v", [P, DIM])
        p_st32 = ps("p_st", [P, 512])
        p_st = p_st32[:].bitcast(F16).rearrange("p (n t) -> p n t", t=P)
        p_sc = [ps(f"p_sc{n}", [P, CH * P]) for n in range(2)]
        p_pv = ps("p_pv", [P, 512])
        pv = p_pv[:, 0:HALF * VW].rearrange("p (h d) -> p h d", d=VW)
        p_xT, p_g, p_u, p_hT = p_tr, p_qk[:, 0:INNER], p_qk[:, DIM:DIM + INNER], p_v
        p_y = p_sc
        p_rank = p_st32[:].rearrange("p (g e) -> p g e", e=E)
        p_total = p_pv[:, 0:E]

        w_q = sem("w_q"); w_kv = sem("w_kv"); w_late = sem("w_late"); w_shared = sem("w_shared")
        x_early = sem("x_early"); x_late = sem("x_late"); pos_loaded = sem("pos_loaded")
        ctx_loaded = sem("ctx_loaded")
        cleared = sem("cleared"); consts = sem("consts"); zeroed = sem("zeroed")
        trig = sem("trig"); sines = sem("sines"); rot_setup = sem("rot_setup"); tables_ready = sem("tables_ready"); w_bout = sem("w_bout"); table_cleared = sem("table_cleared")
        ln1_step = sem("ln1_step"); rstd1_ready = sem("rstd1_ready")
        xnT_done = sem("xnT_done"); xnT_ready = sem("xnT_ready")
        q_done = sem("q_done"); k_done = sem("k_done"); v_done = sem("v_done")
        q_ready = sem("q_ready"); k_ready = sem("k_ready"); vhi_ready = sem("vhi_ready"); vlo_ready = sem("vlo_ready")
        swapped = sem("swapped"); rot_step = sem("rot_step")
        hi_ready = sem("hi_ready"); lo_ready = sem("lo_ready"); parts_ready = sem("parts_ready")
        bias_added = sem("bias_added")
        st_done = sem("st_done"); qT_ready = sem("qT_ready"); kT_ready = [sem(f"kT_ready{g}") for g in range(2)]
        scored = sem("scored"); max_ready = sem("max_ready"); neg_step = sem("neg_step")
        negT_done = sem("negT_done"); negT_ready = sem("negT_ready")
        shifted = sem("shifted"); exp_ready = sem("exp_ready")
        phi_ready = sem("phi_ready"); plo_ready = sem("plo_ready")
        pv_done = sem("pv_done"); recip_ready = sem("recip_ready"); attn_ready = sem("attn_ready")
        attnT_done = sem("attnT_done"); attnT_ready = sem("attnT_ready")
        wo_done = sem("wo_done"); ln2_step = sem("ln2_step"); rstd2_ready = sem("rstd2_ready")
        xn2T_done = sem("xn2T_done"); xn2T_ready = sem("xn2T_ready")
        xn2_stored = sem("xn2_stored"); gate_done = sem("gate_done"); logits_kept = sem("logits_kept")
        gate_exp = sem("gate_exp"); route = sem("route"); masks_ready = sem("masks_ready")
        counted = sem("counted"); experts_known = sem("experts_known"); slots_known = sem("slots_known")
        gates_known = sem("gates_known")
        ids = sem("ids"); scat_copied = sem("scat_copied")
        scattered = sem("scattered")
        table_loaded = sem("table_loaded")
        xe_loaded = [sem(f"xe_loaded{n}") for n in range(2)]
        xe_gathered = [sem(f"xe_gathered{n}") for n in range(2)]
        w13_loaded = [sem(f"w13_loaded{n}") for n in range(2)]
        w2_loaded = [sem(f"w2_loaded{n}") for n in range(2)]
        row_copied = sem("row_copied")
        xeT_done = sem("xeT_done"); xeT_ready = sem("xeT_ready")
        g_done = sem("g_done"); u_done = sem("u_done"); act_ready = sem("act_ready")
        hidden_ready = sem("hidden_ready"); hT_done = sem("hT_done"); hT_ready = sem("hT_ready")
        y_done = sem("y_done"); y_ready = sem("y_ready")
        y_cleared = sem("y_cleared")
        y_stored = [sem(f"y_stored{n}") for n in range(2)]
        y_at_copied = sem("y_at_copied")
        y_gathered = [sem(f"y_gathered{n}") for n in range(GOT)]
        summed = sem("summed")
        out_stored = sem("out_stored")

        x_t = x.rearrange("b p d -> p b d")
        out_t = out.rearrange("b p d -> p b d")

        block = stack.enter_context(nc.Block())

        def later(b, n):
            return not isinstance(b, int) or b >= n

        def pipeline(body, eng, first, last, loop_from, loops):
            def step(b, par):
                def on(d, part, *args):
                    if not isinstance(b, int) or 0 <= b + d < B:
                        part(b + d, (par + d) % 2, *args)
                body(b, on)

            for b in range(first, loop_from):
                step(b, b % 2)
            with eng.Fori(0, loops) as r:
                for u in range(2):
                    step(r * 2 + (loop_from + u), (loop_from + u) % 2)
            for b in range(loop_from + 2 * loops, last + 1):
                step(b, b % 2)

        def tile_count(eng):
            eng.wait_ge(experts_known, 3)
            return eng.value_load(tiles_in_use[0:1, 0:1], min_val=GROUPS, max_val=TILES)

        def if_used(eng, count, j, body, unused):
            with eng.If(count > j):
                body()
            if unused:
                with eng.If(count <= j):
                    unused()

        def expert_tiles(body, eng, beside=lambda n: None, unused=None):
            kinds = ["shared"] * B + ["routed"] * TILES + [None, None]

            def one(n):
                body(n, n // 2, n % 2, *kinds[n:n + 3])

            for n in range(PEELED):
                one(n)
                beside(n)
            with eng.Fori(0, (B - 2 - PEELED) // 2) as r:
                for u in range(2):
                    body(r * 2 + (PEELED + u), r + PEELED // 2, u, *["shared"] * 3)
            one(B - 2)
            one(B - 1)
            with eng.Fori(0, GROUPS // 2) as r:
                for u in range(2):
                    body(r * 2 + (B + u), r + B // 2, u, *["routed"] * 3)
            count = tile_count(eng)
            with eng.Fori(0, (TILES - 3 - GROUPS) // 2) as r:
                for u in range(2):
                    if_used(eng, count, r * 2 + (GROUPS + u), lambda: body(
                        r * 2 + (B + GROUPS + u), r + (B + GROUPS) // 2, u, *["routed"] * 3), unused and (lambda: unused(u, "routed")))
            for n in range(B + TILES - 3, B + TILES):
                if_used(eng, count, n - B, lambda: one(n), unused and (lambda: unused(n % 2, kinds[n + 2])))

        assert B % 2 == 0 and TILES % 2 == 1 and GROUPS % 2 == 0

        @block.sync
        def _(sp):
            sp.nop().then_inc(xn2_stored, 16)
            sp.nop().then_inc(y_stored[0], 16)
            sp.nop().then_inc(y_stored[1], 16)
            sp.dma_start(stream[:, 0:1, :], x_t[:, 0:1, :]).then_inc(x_early, 16)
            sp.dma_start(wkv_sb[:], wkv.rearrange("(c p) n -> p c n", p=P)).then_inc(w_kv, 16)
            sp.dma_start(ctx_sb[:, 0], ctxT[0].rearrange("(c p) t -> p c t", p=P)).then_inc(ctx_loaded, 16)
            sp.dma_start(wq_sb[:], wq.rearrange("(c p) n -> p c n", p=P)).then_inc(w_q, 16)
            sp.wait_ge(ctx_loaded, 16)
            sp.dma_start(ctx_sb[:, 1], ctxT[1].rearrange("(c p) t -> p c t", p=P)).then_inc(ctx_loaded, 16)
            sp.dma_start(stream[:, 1:B, :], x_t[:, 1:B, :]).then_inc(x_late, 16)
            sp.dma_start(wo_sb[:], wo.rearrange("(c p) n -> p c n", p=P)).then_inc(w_late, 16)
            sp.dma_start(gate_sb[:], gateT.rearrange("(c p) n -> p c n", p=P)).then_inc(w_late, 16)
            sp.dma_start(gbias_sb[:], gbias.partition_broadcast(P)).then_inc(w_late, 16)
            sp.dma_start(w13[:, 0], s13.rearrange("(c p) n -> p c n", p=P)).then_inc(w_shared, 16)
            sp.dma_start(w2[:, 0, 0:2, :], s2[0:2 * P].rearrange("(c p) n -> p c n", p=P)).then_inc(w_shared, 16)
            sp.dma_start(w2[0:ICH[2][1], 0, 2, :], s2[2 * P:INNER]).then_inc(w_shared, 16)
            sp.wait_ge(consts, 1)
            sp.dma_start(table_dram.rearrange("(p t) o -> p (t o)", p=P), zero_table[:]).then_inc(table_cleared, 16)

            with sp.Fori(GROUPS, TILES) as j:
                sp.dma_start(y_dram[bass.ds(j * P, P)], ye[:, 0]).then_inc(y_cleared, 16)

            def store_xn2(b, par):
                sp.wait_ge(xn2_stored, b * 16 + 16)
                sp.wait_ge(ln2_step, b * 5 + 5)
                sp.dma_start(xn2_dram[bass.ds(b * P, P)], xn2[:, par, :]).then_inc(xn2_stored, 16)

            def load_ctx(b, half):
                if later(b, 2):
                    sp.wait_ge(k_done, b - 1)
                    sp.wait_ge(v_done, b - 1)
                sp.wait_ge(ctx_loaded, b * 16)
                sp.dma_start(ctx_sb[:, half], ctxT[bass.ds(b, 1)].rearrange("o (c p) t -> p (o c) t", p=P)).then_inc(ctx_loaded, 16)

            def step(b, on):
                on(-1, store_xn2)
                on(3, load_ctx)

            load_ctx(2, 0)
            pipeline(step, sp, 0, B, 2, (B - 5) // 2)

            def load_weights(n, j, buf, kept):
                e = sp.value_load(tile_expert_i[0:1, bass.ds(j, 1)], min_val=0, max_val=E - 1)
                new = {"cond": sp.value_load(tile_new[0:1, bass.ds(j, 1)], min_val=0, max_val=1)} if kept else {}
                if not (isinstance(n, int) and n == B - 2):
                    sp.wait_ge(u_done, n + 1)
                sp.dma_start(w13[:, buf], e13[bass.ds(e, 1)].rearrange("o (c p) n -> p (o c) n", p=P), **new).then_inc(w13_loaded[buf], 16)
                if not (isinstance(n, int) and n == B - 2):
                    sp.wait_ge(y_done, n + 1)
                sp.dma_start(w2[:, buf, 0:2, :], e2[bass.ds(e, 1), 0:2 * P].rearrange("o (c p) n -> p (o c) n", p=P), **new).then_inc(w2_loaded[buf], 16)
                sp.dma_start(w2[0:ICH[2][1], buf, 2, :], e2[bass.ds(e, 1), 2 * P:INNER].rearrange("o p n -> (o p) n"), **new).then_inc(w2_loaded[buf], 16)

            def load_rows(n, par):
                sp.dma_start(xe[:, par], xn2_dram[bass.ds(n * P, P)]).then_inc(xe_loaded[par], 16)

            sp.wait_ge(xn2_stored, B * 16 + 16)
            sp.wait_ge(y_cleared, (TILES - GROUPS) * 16)
            load_rows(0, 0)
            load_rows(1, 1)

            def tile(n, m, par, kind, following, beyond):
                if beyond == "shared":
                    sp.wait_ge(xeT_done, n + 1)
                    load_rows(n + 2, par)
                if beyond == "routed":
                    if kind == "shared":
                        sp.wait_ge(experts_known, 2)
                    load_weights(n, n - (B - 2), 1 - par, kept=kind == "routed")
                if kind == "routed":
                    sp.wait_ge(y_ready, n + 1)
                    sp.dma_start(y_dram[bass.ds((n - B) * P, P)], ye[:, par]).then_inc(y_stored[par], 16)

            def unused(par, beyond):
                sp.nop().then_inc(y_stored[par], 16)
                if beyond:
                    sp.nop().then_inc(w13_loaded[1 - par], 16)
                    sp.nop().then_inc(w2_loaded[1 - par], 32)

            expert_tiles(tile, sp, unused=unused)
            for buf in range(2):
                sp.wait_ge(w13_loaded[buf], (TILES + buf) // 2 * 16)
                sp.wait_ge(w2_loaded[buf], (TILES + buf) // 2 * 32)

            with sp.Fori(0, B) as b:
                sp.wait_ge(summed, b * 2 + (2 * GOT + 2))
                sp.dma_start(out_t[:, bass.ds(b, 1), :], stream[:, bass.ds(b, 1), :]).then_inc(out_stored, 16)
            sp.wait_ge(out_stored, B * 16)

        @block.tensor
        def _(pe):
            def transpose_rows(rows, done):
                for c in range(KC):
                    mm = pe.transpose(p_tr[:, c, :], rows[:, c * P:(c + 1) * P], ident[:])
                mm.then_inc(done, 1)

            def xn_transpose(b, par):
                pe.wait_ge(ln1_step, b * 4 + 4)
                if later(b, 1):
                    pe.wait_ge(xnT_ready, b)
                if later(b, 3):
                    pe.wait_ge(logits_kept, b - 2)
                transpose_rows(xn, xnT_done)

            def project_q(b, par, c):
                if c == 0:
                    pe.wait_ge(xnT_ready, b + 1)
                    if later(b, 1):
                        pe.wait_ge(q_ready, b)
                mm = pe.matmul(p_qk[:, 0:DIM], xnT[:, c, :], wq_sb[:, c, :], start=(c == 0), stop=(c == KC - 1))
                if c == KC - 1:
                    mm.then_inc(q_done, 1)

            def project_k(b, par, c):
                if c == 0:
                    pe.wait_ge(ctx_loaded, b * 16 + 16)
                    if later(b, 1):
                        pe.wait_ge(k_ready, b)
                mm = pe.matmul(p_qk[:, DIM:2 * DIM], ctx_sb[:, par, c, :], wkv_sb[:, c, 0:DIM], start=(c == 0), stop=(c == KCC - 1))
                if c == KCC - 1:
                    mm.then_inc(k_done, 1)

            def project_v(b, par, c):
                if c == 0:
                    pe.wait_ge(ctx_loaded, b * 16 + 16)
                    if later(b, 2):
                        pe.wait_ge(ln2_step, b * 5 - 9)
                    elif later(b, 1):
                        pe.wait_ge(vlo_ready, b)
                mm = pe.matmul(p_v[:], ctx_sb[:, par, c, :], wkv_sb[:, c, DIM:2 * DIM], start=(c == 0), stop=(c == KCC - 1))
                if c == KCC - 1:
                    mm.then_inc(v_done, 1)

            def stack_transpose(b, par, g):
                if g == 0:
                    pe.wait_ge(parts_ready, b * 3 + 3)
                    if later(b, 1):
                        pe.wait_ge(negT_ready, b)
                elif g == 1:
                    pe.wait_ge(qT_ready, b * 2 + 1)
                elif g == 2:
                    pe.wait_ge(kT_ready[0], b * 2 + 2)
                else:
                    pe.wait_ge(qT_ready, b * 2 + 2)
                for n in range(8):
                    h = g % 2 * HEADS + 2 * (8 * (g // 2) + n)
                    mm = pe.transpose(p_st[:, n, :], parts[:, h:h + 2, :].rearrange("p h k -> p (h k)"), ident16[:])
                mm.then_inc(st_done, 1)

            def scores(b, par, c):
                if c == 0:
                    pe.wait_ge(qT_ready, b * 2 + 1)
                    pe.wait_ge(kT_ready[0], b * 2 + 2)
                if c == NCH // 2:
                    pe.wait_ge(qT_ready, b * 2 + 2)
                    pe.wait_ge(kT_ready[1], b * 2 + 2)
                if c >= 2:
                    pe.wait_ge(max_ready, b * NCH + c - 1)
                elif later(b, 1):
                    pe.wait_ge(exp_ready, b * NCH - 1 + c)
                for n in range(2):
                    pair = 2 * c + n
                    mm = pe.matmul(p_sc[c % 2][:, 2 * n * P:(2 * n + 2) * P], qT[:, pair, :],
                                   kT[:, pair].rearrange("p a t -> p (a t)"), start=True, stop=True)
                mm.then_inc(scored, 1)

            def negmax_transpose(b, par):
                pe.wait_ge(neg_step, b * 2 + 2)
                pe.wait_ge(kT_ready[1], b * 2 + 2)
                pe.transpose(p_st[:, 0, :], negmax[:], ident16[:]).then_inc(negT_done, 1)

            def shifted_scores(b, par, c):
                if c == 0:
                    pe.wait_ge(negT_ready, b + 1)
                if c >= 2:
                    pe.wait_ge(exp_ready, b * NCH + c - 1)
                for n in range(CH):
                    h = CH * c + n
                    to = p_sc[c % 2][:, n * P:(n + 1) * P]
                    pe.matmul(to, kT[:, h // 2, h % 2, :], qT[:, h // 2, :], start=True, stop=False)
                    mm = pe.matmul(to, select[:, h, :], negmaxT[:], start=False, stop=True)
                mm.then_inc(shifted, 1)

            def weigh_values(b, par, c):
                if c == 0:
                    pe.wait_ge(vlo_ready, b + 1)
                    if later(b, 1):
                        pe.wait_ge(attn_ready, b * 2)
                if c == NCH // 2:
                    pe.wait_ge(attn_ready, b * 2 + 1)
                pe.wait_ge(plo_ready, b * NCH + c + 1)
                for n in range(CH):
                    h = CH * c + n
                    to = pv[:, h % HALF, :]
                    w_hi, w_lo = (t[:, c % RING, n * P:(n + 1) * P] for t in (phi, plo))
                    pe.matmul(to, w_hi, vhi[:, par, h, :], start=True, stop=False)
                    pe.matmul(to, w_hi, vlo[:, par, h, :], start=False, stop=False)
                    mm = pe.matmul(to, w_lo, vhi[:, par, h, :], start=False, stop=True)
                mm.then_inc(pv_done, 1)

            def attn_transpose(b, par):
                pe.wait_ge(attn_ready, b * 2 + 2)
                last_xn = B if isinstance(b, int) and b + 3 > B else b + 3
                pe.wait_ge(xnT_ready, last_xn)
                if isinstance(b, int) and b + 3 > B:
                    pe.wait_ge(logits_kept, b)
                transpose_rows(attn, attnT_done)

            def project_out(b, par, c):
                if c == 0:
                    pe.wait_ge(attnT_ready, b + 1)
                    last_v = B if isinstance(b, int) and b + 2 > B else b + 2
                    pe.wait_ge(vlo_ready, last_v)
                    if isinstance(b, int) and b + 2 > B:
                        pe.wait_ge(ln2_step, b * 5 - 4)
                mm = pe.matmul(p_v[:], attnT[:, c, :], wo_sb[:, c, :], start=(c == 0), stop=(c == KC - 1))
                if c == KC - 1:
                    mm.then_inc(wo_done, 1)

            def xn2_transpose(b, par):
                pe.wait_ge(ln2_step, b * 5 + 5)
                pe.wait_ge(attnT_ready, b + 1)
                transpose_rows(xn2[:, par], xn2T_done)

            def gate_logits(b, par):
                pe.wait_ge(xn2T_ready, b + 1)
                for c in range(KC):
                    mm = pe.matmul(p_tr[:, 0, 0:E], xn2T[:, c, :], gate_sb[:, c, :], start=(c == 0), stop=(c == KC - 1))
                mm.then_inc(gate_done, 1)

            pe.wait_ge(w_kv, 16)
            pe.wait_ge(w_q, 16)
            pe.wait_ge(consts, 1)
            pe.wait_ge(zeroed, 1)

            def step(b, on):
                if isinstance(b, int) and b == 0:
                    pe.wait_ge(w_late, 3 * 16)
                on(0, scores, 5)
                on(-1, attn_transpose)
                on(2, project_k, 0)
                on(0, scores, 6)
                on(-1, project_out, 0)
                on(0, scores, 7)
                on(-1, project_out, 1)
                on(-1, project_out, 2)
                on(0, negmax_transpose)
                on(-1, project_out, 3)
                on(2, project_k, 1)
                on(0, shifted_scores, 0)
                on(0, shifted_scores, 1)
                on(1, project_v, 0)
                on(0, shifted_scores, 2)
                on(0, shifted_scores, 3)
                on(1, project_v, 1)
                on(0, shifted_scores, 4)
                on(-1, xn2_transpose)
                on(0, shifted_scores, 5)
                on(0, weigh_values, 0)
                on(1, stack_transpose, 0)
                on(0, shifted_scores, 6)
                on(-1, gate_logits)
                on(0, shifted_scores, 7)
                on(0, weigh_values, 1)
                on(2, xn_transpose)
                on(0, weigh_values, 2)
                on(0, weigh_values, 3)
                on(1, stack_transpose, 1)
                on(2, project_q, 0)
                on(2, project_q, 1)
                on(1, stack_transpose, 2)
                on(1, scores, 0)
                on(1, scores, 1)
                on(0, weigh_values, 4)
                on(0, weigh_values, 5)
                on(0, weigh_values, 6)
                on(1, stack_transpose, 3)
                on(1, scores, 2)
                on(1, scores, 3)
                on(0, weigh_values, 7)
                on(2, project_q, 2)
                on(2, project_q, 3)
                on(1, scores, 4)

            pipeline(step, pe, -2, B, 1, (B - 3) // 2)

            def rows_transpose(n, m, par, kind):
                if kind == "shared":
                    pe.wait_ge(xe_loaded[par], m * 16 + 16)
                else:
                    pe.wait_ge(xe_gathered[par], (m - (B // 2 - 1)) * 16)
                for c in range(KC):
                    mm = pe.transpose(p_xT[:, c, :], xe[:, par, c * P:(c + 1) * P], ident[:])
                mm.then_inc(xeT_done, 1)

            def gate_up(n, m, par, kind):
                buf = 0
                pe.wait_ge(xeT_ready, n + 1)
                if kind == "routed":
                    buf = 1 - par
                    pe.wait_ge(w13_loaded[buf], (m - (B // 2 - 1)) * 16)
                for p_out, at, done in ((p_g, 0, g_done), (p_u, INNER, u_done)):
                    for c in range(KC):
                        mm = pe.matmul(p_out, xeT[:, par, c, :], w13[:, buf, c, at:at + INNER], start=(c == 0), stop=(c == KC - 1))
                    mm.then_inc(done, 1)

            def hidden_transpose(n):
                pe.wait_ge(hidden_ready, n + 1)
                for c, (i, k) in enumerate(ICH):
                    mm = pe.transpose(p_hT[0:k, c * P:(c + 1) * P], hidden[:, i:i + k], ident[:])
                mm.then_inc(hT_done, 1)

            def down(n, m, par, kind):
                pe.wait_ge(hT_ready, n * 2 + 2)
                if not (isinstance(n, int) and n < 2):
                    pe.wait_ge(y_ready, n - 1)
                buf = 0 if kind == "shared" else 1 - par
                if kind == "routed":
                    pe.wait_ge(w2_loaded[buf], (m - (B // 2 - 1)) * 32)
                for c, (i, k) in enumerate(ICH):
                    mm = pe.matmul(p_y[par][:], hiddenT[0:k, c, :], w2[0:k, buf, c, :], start=(c == 0), stop=(c == len(ICH) - 1))
                mm.then_inc(y_done, 1)

            def tile(n, m, par, kind, following, beyond):
                if following:
                    rows_transpose(n + 1, m + par, 1 - par, following)
                hidden_transpose(n)
                if following:
                    gate_up(n + 1, m + par, 1 - par, following)
                down(n, m, par, kind)

            def count(n):
                if n != 3:
                    return
                pe.wait_ge(masks_ready, 1)
                pe.matmul(p_st32[:], before[:], mask16[:].rearrange("p g e -> p (g e)"), start=True, stop=False)
                for g in range(GROUPS - 1):
                    rest = GROUPS - 1 - g
                    pe.matmul(p_rank[:, g + 1:GROUPS, :], ones16[:],
                              mask16[:, g:g + 1, :].broadcast_to([P, rest, E]),
                              start=False, stop=(g == GROUPS - 2))
                for g in range(GROUPS):
                    mm = pe.matmul(p_total, ones16[:], mask16[:, g, :], start=(g == 0), stop=(g == GROUPS - 1))
                mm.then_inc(counted, 1)

            pe.wait_ge(w_shared, 3 * 16)
            pe.wait_ge(logits_kept, B)
            pe.wait_ge(q_ready, B)
            pe.wait_ge(k_ready, B)
            rows_transpose(0, 0, 0, "shared")
            gate_up(0, 0, 0, "shared")
            expert_tiles(tile, pe, count)

        @block.scalar
        def _(act):
            act.wait_ge(trig, 4)
            act.activation(sin_t[:].rearrange("p b (r two) -> p b r two", two=2)[:, :, :, 1], angle[:], ACT.Sin).then_inc(sines, 1)
            act.activation(cos_t[:].rearrange("p b (r two) -> p b r two", two=2)[:, :, :, 0], turns[:], ACT.Sin).then_inc(sines, 1)

            def xnT_copy(b, par):
                act.wait_ge(xnT_done, b + 1)
                if later(b, 1):
                    act.wait_ge(q_done, b)
                act.copy(xnT[:], p_tr[:]).then_inc(xnT_ready, 1)

            def q_copy(b, par):
                act.wait_ge(q_done, b + 1)
                if later(b, 1):
                    act.wait_ge(rot_step, b * 2 - 1)
                    act.wait_ge(swapped, b * 2)
                act.copy(qk[:, 0:DIM], p_qk[:, 0:DIM]).then_inc(q_ready, 1)

            def k_copy(b, par):
                act.wait_ge(k_done, b + 1)
                if later(b, 1):
                    act.wait_ge(rot_step, b * 2 - 1)
                    act.wait_ge(swapped, b * 2)
                act.copy(qk[:, DIM:2 * DIM], p_qk[:, DIM:2 * DIM]).then_inc(k_ready, 1)

            def vhi_copy(b, par):
                act.wait_ge(v_done, b + 1)
                if later(b, 2):
                    act.wait_ge(pv_done, b * NCH - NCH)
                act.copy(vhi[:, par, :, 0:HD], p_v[:].rearrange("p (h d) -> p h d", d=HD)).then_inc(vhi_ready, 1)

            def hi_copy(b, par):
                act.wait_ge(rot_step, b * 2 + 2)
                if later(b, 1):
                    act.wait_ge(st_done, b * 4)
                act.copy(parts[:, :, 0:HD], rot[:].rearrange("p (h d) -> p h d", d=HD)).then_inc(hi_ready, 1)

            def qT_copy(b, par, half):
                act.wait_ge(st_done, b * 4 + (2 * half + 1))
                if later(b, 1):
                    act.wait_ge(shifted, b * NCH)
                act.copy(qT[:, 8 * half:8 * half + 8, :], p_st[:]).then_inc(qT_ready, 1)

            def kT_copy(b, par):
                act.wait_ge(st_done, b * 4 + 4)
                for a in range(2):
                    rows = slice(a * STACK, (a + 1) * STACK)
                    act.copy(kT[rows, 8:16, a, :], p_st[rows]).then_inc(kT_ready[1], 1)

            def exp(b, par, c):
                act.wait_ge(shifted, b * NCH + c + 1)
                if later(b, 1) or c >= RING:
                    act.wait_ge(plo_ready, b * NCH + c + 1 - RING)
                act.activation(prob[:, c % RING, :], p_sc[c % 2][:], ACT.Exp, scale=SCALE).then_inc(exp_ready, 1)

            def attnT_copy(b, par):
                act.wait_ge(attnT_done, b + 1)
                act.copy(attnT[:], p_tr[:]).then_inc(attnT_ready, 1)

            def xn2T_copy(b, par):
                act.wait_ge(xn2T_done, b + 1)
                act.copy(xn2T[:], p_tr[:]).then_inc(xn2T_ready, 1)

            def keep_logits(b, par):
                act.wait_ge(gate_done, b + 1)
                act.copy(logits[:, bass.ds(b, 1), :], p_tr[:, 0:1, 0:E]).then_inc(logits_kept, 1)

            act.wait_ge(zeroed, 1)

            def step(b, on):
                on(1, hi_copy)
                on(0, exp, 0)
                on(0, exp, 1)
                on(0, exp, 2)
                on(0, exp, 3)
                on(0, exp, 4)
                on(-1, xn2T_copy)
                on(0, exp, 5)
                on(-1, keep_logits)
                on(1, qT_copy, 0)
                on(2, xnT_copy)
                on(1, vhi_copy)
                on(0, exp, 6)
                on(0, exp, 7)
                on(1, qT_copy, 1)
                on(1, kT_copy)
                on(2, k_copy)
                on(2, q_copy)
                on(0, attnT_copy)

            pipeline(step, act, -2, B, 1, (B - 3) // 2)

            act.wait_ge(logits_kept, B)
            act.activation(score[:], logits[:], ACT.Exp, scale=-1.0).then_inc(gate_exp, 1)

            def xeT_copy(n, par):
                act.wait_ge(xeT_done, n + 1)
                if not (isinstance(n, int) and n < 2):
                    act.wait_ge(u_done, n - 1)
                act.copy(xeT[:, par], p_xT[:]).then_inc(xeT_ready, 1)

            def gate_act(n):
                act.wait_ge(g_done, n + 1)
                if not (isinstance(n, int) and n == 0):
                    act.wait_ge(hidden_ready, n)
                act.activation(act_g[:], p_g, ACT.Silu).then_inc(act_ready, 1)

            xeT_copy(0, 0)
            gate_act(0)

            def tile(n, m, par, kind, following, beyond):
                if following:
                    xeT_copy(n + 1, 1 - par)
                    gate_act(n + 1)

            expert_tiles(tile, act)

        @block.vector
        def _(dve):
            def ln(step, per, at, b, rows, stats, mv, rstd_ready, rstd, to, part):
                base = b * per + at
                if part == "stats":
                    dve.bn_stats(stats[:], rows).then_inc(step, 1)
                    dve.wait_ge(step, base + 1)
                    dve.memset(carrier_dve[:], 0.0)
                    dve.bn_aggr(mv[:], stats[:]).then_inc(step, 1)
                    dve.wait_ge(step, base + 2)
                    dve.tensor_scalar(mv[:, 1:2], mv[:, 1:2], EPS, None, ALU.add).then_inc(step, 1)
                else:
                    dve.wait_ge(rstd_ready, b + 1)
                    dve.tensor_scalar(to, rows, mv[:, 0:1], rstd[:, 0:1], ALU.subtract, ALU.mult).then_inc(step, 1)

            def row(b):
                return stream[:, bass.ds(b, 1), :].rearrange("p o d -> p (o d)")

            def ln1_stats(b, par, ahead=False):
                if not later(b, 1) and not ahead:
                    return
                if later(b, 1):
                    dve.wait_ge(x_late, 16)
                ln(ln1_step, 4, 0, b, row(b), stats1, mv1, rstd1_ready, rstd1, xn[:], "stats")

            def ln1_norm(b, par, ahead=False):
                if not later(b, 1) and not ahead:
                    return
                if later(b, 1):
                    dve.wait_ge(xnT_done, b)
                ln(ln1_step, 4, 0, b, row(b), stats1, mv1, rstd1_ready, rstd1, xn[:], "norm")

            def ln2_stats(b, par):
                dve.wait_ge(ln2_step, b * 5 + 1)
                dve.memset(carrier_dve[:], 0.0)
                ln(ln2_step, 5, 1, b, row(b), stats2, mv2, rstd2_ready, rstd2, xn2[:, par, :], "stats")

            def ln2_norm(b, par):
                if later(b, 1):
                    dve.wait_ge(xn2_stored, b * 16)
                if later(b, 2):
                    dve.wait_ge(xn2T_done, b - 1)
                ln(ln2_step, 5, 1, b, row(b), stats2, mv2, rstd2_ready, rstd2, xn2[:, par, :], "norm")

            def residual(b, par):
                dve.wait_ge(wo_done, b + 1)
                dve.wait_ge(bias_added, b + 1)
                dve.tensor_tensor(row(b), p_v[:], row(b), ALU.add).then_inc(ln2_step, 1)

            def vlo_make(b, par):
                dve.wait_ge(vhi_ready, b + 1)
                dve.tensor_tensor(vlo[:, par, :, 0:HD], p_v[:].rearrange("p (h d) -> p h d", d=HD),
                                  vhi[:, par, :, 0:HD], ALU.subtract).then_inc(vlo_ready, 1)

            def rotate_cos(b, par):
                dve.wait_ge(q_ready, b + 1)
                dve.wait_ge(k_ready, b + 1)
                if later(b, 1):
                    dve.wait_ge(lo_ready, b)
                c = cos_t[:, bass.ds(b, 1), :].broadcast_to([P, 2 * HEADS, HD])
                dve.tensor_tensor(rot[:].rearrange("p (h d) -> p h d", d=HD), qk[:].rearrange("p (h d) -> p h d", d=HD), c, ALU.mult).then_inc(rot_step, 1)

            def rotate_add(b, par):
                dve.wait_ge(rot_step, b * 2 + 1)
                dve.wait_ge(swapped, b * 2 + 2)
                dve.tensor_tensor(rot[:], rot[:], swp[:], ALU.add).then_inc(rot_step, 1)

            def parts_double(b, par):
                dve.wait_ge(lo_ready, b + 1)
                q, k = parts[:, 0:HEADS], parts[:, HEADS:2 * HEADS]
                dve.tensor_copy(q[:, :, 2 * HD:4 * HD], q[:, :, 0:2 * HD]).then_inc(parts_ready, 1)
                dve.tensor_copy(k[:, :, 2 * HD:3 * HD], k[:, :, HD:2 * HD]).then_inc(parts_ready, 1)
                dve.tensor_copy(k[:, :, 3 * HD:4 * HD], k[:, :, 0:HD]).then_inc(parts_ready, 1)

            def kT_copy(b, par):
                dve.wait_ge(st_done, b * 4 + 2)
                for a in range(2):
                    rows = slice(a * STACK, (a + 1) * STACK)
                    dve.tensor_copy(kT[rows, 0:8, a, :], p_st[rows]).then_inc(kT_ready[0], 1)

            def row_max(b, par, c):
                dve.wait_ge(scored, b * NCH + c + 1)
                if c == 0 and later(b, 1):
                    dve.wait_ge(neg_step, b * 2)
                dve.tensor_reduce(rowmax[:, CH * c:CH * c + CH], p_sc[c % 2][:].rearrange("p (h t) -> p h t", t=P),
                                  AX_X, ALU.max).then_inc(max_ready, 1)

            def neg_max(b, par):
                dve.wait_ge(max_ready, b * NCH + NCH)
                if later(b, 1):
                    dve.wait_ge(negT_done, b)
                dve.tensor_scalar(negmax[:, 0:HEADS], rowmax[:], -1.0, None, ALU.mult).then_inc(neg_step, 1)
                dve.wait_ge(neg_step, b * 2 + 1)
                dve.scalar_tensor_tensor(negmax[:, HEADS:2 * HEADS], rowmax[:], -1.0, negmax[:, 0:HEADS],
                                         ALU.mult, ALU.subtract).then_inc(neg_step, 1)

            def neg_copy(b, par):
                dve.wait_ge(negT_done, b + 1)
                if later(b, 1):
                    dve.wait_ge(shifted, b * NCH)
                dve.tensor_copy(negmaxT[:], p_st[:, 0, :]).then_inc(negT_ready, 1)

            def phi_make(b, par, c):
                dve.wait_ge(exp_ready, b * NCH + c + 1)
                if later(b, 1) or c >= RING:
                    dve.wait_ge(pv_done, b * NCH + c + 1 - RING)
                dve.tensor_copy(phi[:, c % RING, :], prob[:, c % RING, :]).then_inc(phi_ready, 1)

            def normalise(b, par, half):
                dve.wait_ge(pv_done, b * NCH + (half + 1) * (NCH // 2))
                if half:
                    dve.wait_ge(attn_ready, b * 2 + 1)
                elif later(b, 1):
                    dve.wait_ge(attnT_done, b)
                dve.reciprocal(recip[:], pv[:, :, HD]).then_inc(recip_ready, 1)
                dve.wait_ge(recip_ready, b * 2 + half + 1)
                to = attn[:].rearrange("p (h d) -> p h d", d=HD)[:, half * HALF:(half + 1) * HALF, :]
                dve.tensor_tensor(to, pv[:, :, 0:HD], recip[:].rearrange("p (h o) -> p h o", o=1).broadcast_to([P, HALF, HD]),
                                  ALU.mult).then_inc(attn_ready, 1)

            dve.wait_ge(x_early, 16)
            ln1_stats(0, 0, ahead=True)
            ln1_norm(0, 0, ahead=True)
            dve.memset(negmax[:].bitcast(F32), 0.0)
            dve.memset(kT[:].bitcast(F32).rearrange("p a b t -> p (a b t)"), 0.0)
            dve.memset(vhi[:], 1.0)
            dve.memset(vlo[:], 0.0).then_inc(zeroed, 1)
            dve.wait_ge(pos_loaded, 16)
            half = ROT // 2
            for p in range(2):
                for i in range(half):
                    last = dve.tensor_scalar(angle[:, :, p * half + i], pos_sb[:, :, p], 10000.0 ** (-i / half), None, ALU.mult)
            last.then_inc(trig, 1)
            dve.wait_ge(trig, 1)
            dve.tensor_scalar(turns[:], angle[:], 1 / (2 * pi), ROUND, ALU.mult, ALU.add).then_inc(trig, 1)
            dve.wait_ge(trig, 2)
            dve.tensor_scalar(turns[:], turns[:], -ROUND, -2 * pi, ALU.add, ALU.mult).then_inc(trig, 1)
            dve.wait_ge(trig, 3)
            dve.tensor_tensor(turns[:], turns[:], angle[:], ALU.add).then_inc(rot_setup, 1)
            dve.wait_ge(rot_setup, 1)
            dve.tensor_scalar(angle[:], turns[:], 3.1415925, -3.1415925, ALU.min, ALU.max).then_inc(rot_setup, 1)
            dve.wait_ge(rot_setup, 2)
            dve.scalar_tensor_tensor(turns[:], angle[:], -1.0, angle[:], ALU.mult, ALU.min).then_inc(rot_setup, 1)
            dve.wait_ge(rot_setup, 3)
            dve.tensor_scalar(turns[:], turns[:], pi / 2, None, ALU.add).then_inc(trig, 1)
            dve.wait_ge(sines, 2)
            cos_p = cos_t[:].rearrange("p b (r two) -> p b r two", two=2)
            sin_p = sin_t[:].rearrange("p b (r two) -> p b r two", two=2)
            dve.tensor_copy(cos_p[:, :, :, 1], cos_p[:, :, :, 0])
            dve.tensor_scalar(sin_p[:, :, :, 0], sin_p[:, :, :, 1], -1.0, None, ALU.mult).then_inc(tables_ready, 1)

            dve.wait_ge(tables_ready, 1)

            def step(b, on):
                on(0, neg_max)
                on(1, rotate_add)
                on(0, neg_copy)
                on(-1, residual)
                on(-1, ln2_stats)
                on(0, phi_make, 0)
                on(2, ln1_norm)
                on(0, phi_make, 1)
                on(-1, ln2_norm)
                on(0, phi_make, 2)
                on(1, parts_double)
                on(0, phi_make, 3)
                on(0, phi_make, 4)
                on(0, phi_make, 5)
                on(3, ln1_stats)
                on(1, kT_copy)
                on(0, phi_make, 6)
                on(0, normalise, 0)
                on(0, phi_make, 7)
                on(1, row_max, 0)
                on(1, row_max, 1)
                on(1, row_max, 2)
                on(1, row_max, 3)
                on(0, normalise, 1)
                on(1, vlo_make)
                on(1, row_max, 4)
                on(1, row_max, 5)
                on(2, rotate_cos)
                on(1, row_max, 6)
                on(1, row_max, 7)

            pipeline(step, dve, -3, B, 3, (B - 6) // 2)

            def hidden_make(n):
                dve.wait_ge(act_ready, n + 1)
                dve.wait_ge(u_done, n + 1)
                if not (isinstance(n, int) and n == 0):
                    dve.wait_ge(hT_done, n)
                dve.tensor_tensor(hidden[:], p_u, act_g[:], ALU.mult).then_inc(hidden_ready, 1)

            def hT_copy(n):
                dve.wait_ge(hT_done, n + 1)
                if not (isinstance(n, int) and n == 0):
                    dve.wait_ge(y_done, n)
                dve.tensor_copy(hiddenT[:, 0:2, :], p_hT[:, 0:2 * P].rearrange("p (c t) -> p c t", t=P)).then_inc(hT_ready, 1)
                k = ICH[2][1]
                dve.tensor_copy(hiddenT[0:k, 2, :], p_hT[0:k, 2 * P:3 * P]).then_inc(hT_ready, 1)

            def y_take(n, m, par, kind):
                dve.wait_ge(y_done, n + 1)
                if kind == "shared":
                    dve.tensor_tensor(row(n), p_y[par][:], row(n), ALU.add).then_inc(y_ready, 1)
                else:
                    dve.wait_ge(y_stored[par], (m - (B // 2 - 1)) * 16)
                    dve.tensor_copy(ye[:, par], p_y[par][:]).then_inc(y_ready, 1)

            hidden_make(0)
            dve.wait_ge(y_cleared, (TILES - GROUPS) * 16)

            def tile(n, m, par, kind, following, beyond):
                hT_copy(n)
                if following:
                    hidden_make(n + 1)
                y_take(n, m, par, kind)

            steps = [0]

            def then(ins):
                ins.then_inc(route, 1)
                steps[0] += 1
                dve.wait_ge(route, steps[0])

            def each_e(row_of_e, n):
                return row_of_e.rearrange("p (o e) -> p o e", o=1).broadcast_to([P, n, E])

            def scores_and_two_best(batches_of):
                for b in batches_of:
                    then(dve.max(best[:, b, :], routing[:, b, :]))
                    then(dve.max_index(best_at[:, b, :], best[:, b, :], routing[:, b, :]))

            def beside(n):
                if n == 0:
                    dve.wait_ge(gate_exp, 1)
                    then(dve.tensor_scalar(score[:], score[:], 1.0, None, ALU.add))
                    then(dve.reciprocal(score[:], score[:]))
                    then(dve.tensor_tensor(routing[:], score[:], each_e(gbias_sb[:], B), ALU.add))
                    scores_and_two_best(range(0, 2))
                if n == 1:
                    scores_and_two_best(range(2, 9))
                if n == 2:
                    scores_and_two_best(range(9, B))
                    then(dve.tensor_copy(chosen[:], best_at[:, :, 0:TOPK]))
                    chosen_g = chosen[:].rearrange("p b (k o) -> p (b k) o", o=1)
                    then(dve.tensor_tensor(mask[:], each_e(expert_no[:], GROUPS), chosen_g.broadcast_to([P, GROUPS, E]), ALU.is_equal))
                    dve.tensor_copy(mask16[:], mask[:]).then_inc(masks_ready, 1)
                if n == 3:
                    s4 = score[:].rearrange("p b (o e) -> p b o e", o=1).broadcast_to([P, B, TOPK, E])
                    w4 = work[:].rearrange("p (b k) e -> p b k e", k=TOPK)
                    m4 = mask[:].rearrange("p (b k) e -> p b k e", k=TOPK)
                    then(dve.tensor_tensor(w4, m4, s4, ALU.mult))
                    then(dve.tensor_reduce(picked[:], w4, AX_X, ALU.add))
                    then(dve.tensor_reduce(pick_sum[:], picked[:], AX_X, ALU.add))
                    then(dve.reciprocal(pick_sum[:], pick_sum[:]))
                    dve.tensor_tensor(gates[:], picked[:], pick_sum[:].rearrange("p (b o) -> p b o", o=1).broadcast_to([P, B, TOPK]),
                                      ALU.mult).then_inc(gates_known, 1)
                if n == 4:
                    dve.wait_ge(counted, 1)
                    then(dve.tensor_scalar(tiles_of[:], p_total, 1 / P, (P - 1) / P - 0.5 + 0.5 / P, ALU.mult, ALU.add))
                    then(dve.tensor_scalar(tiles_of[:], tiles_of[:], ROUND, -ROUND, ALU.add, ALU.add))
                    then(dve.tensor_tensor_scan(tiles_end[:], one_e[:], tiles_of[:], 0.0, ALU.mult, ALU.add))
                    then(dve.tensor_tensor(first_slot[:], tiles_end[:], tiles_of[:], ALU.subtract))
                    then(dve.tensor_tensor(tile_cmp[:], each_e(tiles_end[:], TILES),
                                           tile_no[:].rearrange("p (t o) -> p t o", o=1).broadcast_to([P, TILES, E]), ALU.is_le))
                    then(dve.tensor_reduce(tile_expert[:], tile_cmp[:], AX_X, ALU.add))
                    then(dve.tensor_scalar(tile_expert[:], tile_expert[:], float(E - 1), None, ALU.min))
                    dve.tensor_copy(tile_expert_i[:], tile_expert[:]).then_inc(experts_known, 1)
                    dve.tensor_tensor(tile_new[:, 2:TILES], tile_expert[:, 2:TILES], tile_expert[:, 0:TILES - 2],
                                      ALU.not_equal).then_inc(experts_known, 1)
                    dve.tensor_copy(tiles_in_use[:], tiles_end[:, E - 1:E]).then_inc(experts_known, 1)
                if n == 5:
                    then(dve.scalar_tensor_tensor(work[:], each_e(first_slot[:], GROUPS), float(P), p_rank, ALU.mult, ALU.add))
                    then(dve.tensor_tensor(work[:], work[:], mask[:], ALU.mult))
                    then(dve.tensor_reduce(slot[:], work[:], AX_X, ALU.add))
                    then(dve.tensor_scalar(slot_tile[:], slot[:], 1 / P, -0.5 + 0.5 / P, ALU.mult, ALU.add))
                    then(dve.tensor_scalar(slot_tile[:], slot_tile[:], ROUND, -ROUND, ALU.add, ALU.add))
                    then(dve.tensor_scalar(slot_at[:], slot[:], float(TILES), None, ALU.mult))
                    then(dve.scalar_tensor_tensor(slot_at[:], slot_tile[:], float(1 - P * TILES), slot_at[:], ALU.mult, ALU.add))
                    dve.tensor_copy(slot_u[:], slot[:]).then_inc(slots_known, 1)
                    dve.tensor_copy(slot_at_u[:], slot_at[:]).then_inc(slots_known, 1)

            expert_tiles(tile, dve, beside)

            dve.wait_ge(gates_known, 1)
            dve.nop().then_inc(summed, 2 * GOT)
            with dve.Fori(0, B // GOT) as r:
                for u in range(GOT):
                    b = r * GOT + u
                    dve.wait_ge(y_gathered[u], r * 32 + 32)
                    for k in range(TOPK):
                        g = gates[:, bass.ds(b, 1), k:k + 1].rearrange("p b k -> p (b k)")
                        dve.scalar_tensor_tensor(row(b), y_got[u][k], g, row(b), ALU.mult, ALU.add).then_inc(summed, 1)
                        dve.wait_ge(summed, b * 2 + (2 * GOT + k + 1))

        @block.gpsimd
        def _(pool):
            def rstd(step, need, to, mv, ready):
                pool.wait_ge(step, need)
                pool.tensor_tensor(to[:], mv[:, 1:2], minus_half[:], ALU.pow).then_inc(ready, 1)

            def rstd1_make(b, par, ahead=False):
                if not later(b, 1) and not ahead:
                    return
                rstd(ln1_step, b * 4 + 3, rstd1, mv1, rstd1_ready)

            def rstd2_make(b, par):
                rstd(ln2_step, b * 5 + 4, rstd2, mv2, rstd2_ready)

            pool.dma_start(pos_sb[:], pos.rearrange("b p c -> p b c")).then_inc(pos_loaded, 16)
            pool.dma_start(bout_sb[:], bout.partition_broadcast(P)).then_inc(w_bout, 16)
            pool.memset(minus_half[:], -0.5).then_inc(cleared, 1)
            pool.memset(ident[:], 0.0).then_inc(cleared, 1)
            pool.memset(ident16[:], 0.0).then_inc(cleared, 1)
            pool.memset(before[:], 1.0).then_inc(cleared, 1)
            pool.memset(select[:], 0.0).then_inc(cleared, 1)
            pool.memset(ones16[:], 1.0).then_inc(cleared, 1)
            pool.memset(ye[:, 0], 0.0).then_inc(cleared, 1)
            pool.memset(one_e[:], 1.0).then_inc(cleared, 1)
            pool.memset(zero_table[:], 0).then_inc(cleared, 1)
            pool.iota(token_no[:], [[P, B], [0, TOPK]], base=0, channel_multiplier=1).then_inc(cleared, 1)
            pool.iota(expert_no[:], [[1, E]], base=0, channel_multiplier=0, allow_small_or_imprecise_dtypes=True).then_inc(cleared, 1)
            pool.iota(tile_no[:], [[1, TILES]], base=0, channel_multiplier=0, allow_small_or_imprecise_dtypes=True).then_inc(cleared, 1)
            pool.wait_ge(cleared, 12)
            for m in (ident, ident16):
                pool.affine_select(out=m[:], in_=m[:], compare_op=ALU.not_equal, fill=1.0, base=0,
                                   pattern=[[-1, P]], channel_multiplier=1).then_inc(cleared, 1)
            rstd1_make(0, 0, ahead=True)
            pool.affine_select(out=before[:], in_=before[:], compare_op=ALU.is_gt, fill=0.0, base=0,
                               pattern=[[1, P]], channel_multiplier=-1).then_inc(cleared, 1)
            for a in range(2):
                pool.wait_ge(cleared, 15 + a)
                rows = select[32 * a:32 * a + HEADS]
                pool.affine_select(out=rows, in_=rows, compare_op=ALU.not_equal, fill=1.0, base=0,
                                   pattern=[[-1, HEADS], [0, P]], channel_multiplier=1).then_inc(cleared, 1)
            pool.wait_ge(cleared, 17)
            pool.nop().then_inc(consts, 1)

            def row(b):
                return stream[:, bass.ds(b, 1), :].rearrange("p o d -> p (o d)")

            def bias_add(b, par):
                pool.wait_ge(ln1_step, b * 4 + 4)
                pool.tensor_tensor(row(b), row(b), bout_sb[:], ALU.add).then_inc(bias_added, 1)

            def rotate_swapped(b, par):
                pool.wait_ge(q_ready, b + 1)
                pool.wait_ge(k_ready, b + 1)
                if later(b, 1):
                    pool.wait_ge(rot_step, b * 2)
                q3 = qk[:].rearrange("p (h r two) -> p h r two", two=2, r=ROT)
                s3 = swp[:].rearrange("p (h r two) -> p h r two", two=2, r=ROT)
                t3 = sin_t[:, bass.ds(b, 1), :].rearrange("p o (r two) -> p o r two", two=2)
                for side in range(2):
                    pool.tensor_tensor(s3[:, :, :, side], q3[:, :, :, 1 - side],
                                       t3[:, :, :, side].broadcast_to([P, 2 * HEADS, ROT]), ALU.mult).then_inc(swapped, 1)

            def lo_make(b, par):
                pool.wait_ge(hi_ready, b + 1)
                pool.tensor_tensor(parts[:, :, HD:2 * HD], rot[:].rearrange("p (h d) -> p h d", d=HD), parts[:, :, 0:HD],
                                   ALU.subtract).then_inc(lo_ready, 1)

            def plo_make(b, par, c):
                pool.wait_ge(phi_ready, b * NCH + c + 1)
                if later(b, 1) or c >= RING:
                    pool.wait_ge(pv_done, b * NCH + c + 1 - RING)
                pool.tensor_tensor(plo[:, c % RING, :], prob[:, c % RING, :], phi[:, c % RING, :], ALU.subtract).then_inc(plo_ready, 1)

            pool.wait_ge(tables_ready, 1)
            pool.wait_ge(w_bout, 16)

            def step(b, on):
                on(-1, rstd2_make)
                on(0, plo_make, 0)
                on(0, plo_make, 1)
                on(0, plo_make, 2)
                on(0, plo_make, 3)
                on(0, plo_make, 4)
                on(0, plo_make, 5)
                on(0, plo_make, 6)
                on(0, plo_make, 7)
                on(3, rstd1_make)
                on(2, rotate_swapped)
                on(1, bias_add)
                on(2, lo_make)

            pipeline(step, pool, -3, B, 1, (B - 4) // 2)

            pool.wait_ge(slots_known, 2)
            pool.wait_ge(xn2_stored, B * 16 + 16)
            with pool.Fori(0, GROUPS // SCATTERS) as r:
                for n in range(SCATTERS):
                    g = r * SCATTERS + n
                    pool.tensor_copy(scat_at[:, n], slot_at_u[:, bass.ds(g, 1)]).then_inc(scat_copied, 1)
                    pool.tensor_copy(scat_id[:, n], token_no[:, bass.ds(g, 1)]).then_inc(scat_copied, 1)
                pool.wait_ge(table_cleared, 16)
                pool.wait_ge(scat_copied, r * (2 * SCATTERS) + 2 * SCATTERS)
                pool.tensor_tensor(carrier_pool[:], minus_half[:], minus_half[:], ALU.mult)
                for n in range(SCATTERS):
                    pool.indirect_dma_start(out=table_dram, out_offset=bass.IndirectOffsetOnAxis(ap=scat_at[:, n], axis=0),
                                            in_=scat_id[:, n], in_offset=None).then_inc(scattered, 16)
                pool.wait_ge(scattered, r * (16 * SCATTERS) + 16 * SCATTERS)
            pool.dma_start(table[:], table_dram.rearrange("(p t) o -> p (t o)", p=P)).then_inc(table_loaded, 16)
            pool.wait_ge(table_loaded, 16)

            def gather_rows(n, par):
                pool.wait_ge(xeT_done, n - 1)
                pool.tensor_copy(row_at[:, par], table[:, bass.ds(n - B, 1)]).then_inc(row_copied, 1)
                pool.wait_ge(table_loaded, 16)
                pool.wait_ge(row_copied, n - (B - 1))
                pool.tensor_tensor(carrier_pool[:], minus_half[:], minus_half[:], ALU.mult)
                pool.indirect_dma_start(out=xe[:, par], out_offset=None, in_=xn2_dram,
                                        in_offset=bass.IndirectOffsetOnAxis(ap=row_at[:, par], axis=0)).then_inc(xe_gathered[par], 16)

            with pool.Fori(0, GROUPS // 2) as r:
                for u in range(2):
                    gather_rows(r * 2 + (B + u), u)
            gather_rows(B + GROUPS, 0)
            count = tile_count(pool)
            with pool.Fori(0, (TILES - 1 - GROUPS) // 2) as r:
                for u in range(2):
                    if_used(pool, count, r * 2 + (GROUPS + u), lambda: gather_rows(r * 2 + (B + GROUPS + 1 + u), 1 - u), None)

            pool.wait_ge(y_stored[0], (TILES + 3) // 2 * 16)
            pool.wait_ge(y_stored[1], (TILES // 2 + 1) * 16)
            with pool.Fori(0, B // GOT) as r:
                for u in range(GOT):
                    b = r * GOT + u
                    pool.wait_ge(summed, b * 2 + 2)
                    pool.tensor_copy(y_at[:, u, :], slot_u[:, bass.ds(b * 2, 2)]).then_inc(y_at_copied, 1)
                    pool.wait_ge(y_at_copied, b + 1)
                    pool.tensor_tensor(carrier_pool[:], minus_half[:], minus_half[:], ALU.mult)
                    for k in range(TOPK):
                        pool.indirect_dma_start(out=y_got[u][k], out_offset=None, in_=y_dram,
                                                in_offset=bass.IndirectOffsetOnAxis(ap=y_at[:, u, k:k + 1], axis=0)).then_inc(y_gathered[u], 16)


def kernel(**inputs):
    import numpy as np
    import concourse.bacc as bacc
    from concourse.bass_utils import run_bass_kernel_spmd

    def turned(a):
        return np.ascontiguousarray(np.swapaxes(np.asarray(a), -1, -2))

    w = {k[len("L0_"):]: np.asarray(v) for k, v in inputs.items() if k.startswith("L0_")}
    arrays = {
        "x": np.ascontiguousarray(inputs["x"]),
        "ctxT": turned(inputs["ctx_1024"]),
        "pos": np.ascontiguousarray(inputs["fside_BxSx2_0"]),
        "wq": w["xattn_Wq"], "wkv": w["xattn_Wkv"], "wo": w["xattn_Wout"], "bout": w["xattn_bout"],
        "gateT": turned(w["ffn_gate_w"]), "gbias": w["ffn_bias"],
        "s13": turned(np.concatenate([w["ffn_shared_w1"], w["ffn_shared_w3"]], axis=0)),
        "s2": turned(w["ffn_shared_w2"]),
        "e13": turned(np.concatenate([w["ffn_w1"], w["ffn_w3"]], axis=1)),
        "e2": turned(w["ffn_w2"]),
    }
    arrays = {k: np.ascontiguousarray(v) for k, v in arrays.items()}
    nc = bacc.Bacc("TRN2", target_bir_lowering=False, num_devices=1)
    args = {k: nc.dram_tensor(k, v.shape, mybir.dt.from_np(v.dtype), kind="ExternalInput").ap() for k, v in arrays.items()}
    out = nc.dram_tensor("out", (B, P, DIM), F32, kind="ExternalOutput").ap()
    build(nc, out=out, **args)
    r = run_bass_kernel_spmd(nc, [arrays], core_ids=[0])
    return r.results[0]["out"]
```

```python
from contextlib import ExitStack
from math import pi

import concourse.bass as bass
from concourse import mybir

F32 = mybir.dt.float32
F16 = mybir.dt.float16
U32 = mybir.dt.uint32
I32 = mybir.dt.int32
ACT = mybir.ActivationFunctionType
ALU = mybir.AluOpType
AX_X = mybir.AxisListType.X

P = 128
B = 16
DIM, CTX_DIM = 512, 256
KC, KCC = DIM // P, CTX_DIM // P
HEADS, HD = 32, 16
PAIRS = HEADS // 2
STACK = 4 * HD
VW = HD + 1
CH = 4
NCH = HEADS // CH
HALF = HEADS // 2
RING = 4
GOT = 4
EARLY = 10
PLACED = 8
ROT = HD // 2
E, TOPK = 16, 2
INNER = 352
W13 = 2 * INNER
ICH = [(0, P), (P, P), (2 * P, INNER - 2 * P)]
T = B * P
GROUPS = B * TOPK
TILES = (T * TOPK) // P + E - 1
EPS = 1e-5
SCALE = HD ** -0.5
W_SCALE = 2.0 ** 8
ROUND = float(3 << 22)


class TileSems:

    def __init__(self, sem, stage, first, rows):
        self.first = first
        self.rows = rows
        self.xe_loaded = [sem(f"{stage}_xe_loaded{n}") for n in range(2)]
        self.xeT_done = sem(f"{stage}_xeT_done")
        self.xeT_ready = sem(f"{stage}_xeT_ready")
        self.g_done = sem(f"{stage}_g_done")
        self.u_done = sem(f"{stage}_u_done")
        self.act_ready = sem(f"{stage}_act_ready")
        self.hidden_ready = sem(f"{stage}_hidden_ready")
        self.hT_done = sem(f"{stage}_hT_done")
        self.hT_hi = sem(f"{stage}_hT_hi")
        self.hT_lo = sem(f"{stage}_hT_lo")
        self.y_done = sem(f"{stage}_y_done")
        self.y_ready = sem(f"{stage}_y_ready")


def build(nc, x, ctxT, pos, wq, wkv, wo, bout, gateT, gbias, s13, s2, e13, e2, out):
    with ExitStack() as stack:
        def sb(name, shape, dt=F32):
            return stack.enter_context(nc.sbuf_tensor(name, shape, dt))

        def ps(name, shape, dt=F32):
            return stack.enter_context(nc.psum_tensor(name, shape, dt))

        def sem(name):
            return stack.enter_context(nc.semaphore(name))

        xn2_dram = nc.dram_tensor("xn2_dram", [T, 2 * DIM], F16, kind="Internal").ap()
        y_dram = nc.dram_tensor("y_dram", [TILES * P, DIM], F32, kind="Internal").ap()

        stream = sb("stream", [P, B, DIM])
        used_twice = sb("used_twice", [P, 18 * DIM])
        wq16 = used_twice[:, 0:4 * DIM].bitcast(F16).rearrange("p (a c n) -> p a c n", a=2, c=KC)
        wkv16 = used_twice[:, 4 * DIM:8 * DIM].bitcast(F16).rearrange("p (a c n) -> p a c n", a=2, c=KCC)
        wo16 = used_twice[:, 8 * DIM:12 * DIM].bitcast(F16).rearrange("p (a c n) -> p a c n", a=2, c=KC)
        parts = used_twice[:, 12 * DIM:16 * DIM].bitcast(F16).rearrange("p (h k) -> p h k", k=STACK)
        qk = used_twice[:, 16 * DIM:18 * DIM]
        bout_sb = sb("bout_sb", [P, DIM])
        gate_sb = sb("gate_sb", [P, KC, E])
        gbias_sb = sb("gbias_sb", [P, E])
        pos_sb = sb("pos_sb", [P, B, 2])
        ident = sb("ident", [P, P])
        ident16 = sb("ident16", [P, P], F16)
        before = sb("before", [P, P], F16)
        ones16 = sb("ones16", [P, P], F16)
        carrier_dve, carrier_pool, carrier_act = (sb(f"carrier_{eng}", [P, 1]) for eng in ("dve", "pool", "act"))
        minus_half = sb("minus_half", [P, 1])
        angle = sb("angle", [P, B, ROT])
        turns = sb("turns", [P, B, ROT])
        cos_t = sb("cos_t", [P, B, HD])
        sin_t = sb("sin_t", [P, B, HD])
        ctx_sb = sb("ctx_sb", [P, 2, KCC, P])
        ctx16 = sb("ctx16", [P, 2, 2, KCC, P], F16)
        stats1, mv1, rstd1 = sb("stats1", [P, 6]), sb("mv1", [P, 2]), sb("rstd1", [P, 1])
        stats2, mv2, rstd2 = sb("stats2", [P, 6]), sb("mv2", [P, 2]), sb("rstd2", [P, 1])
        xn = sb("xn", [P, DIM])
        xnT = sb("xnT", [P, 2, KC, P], F16)
        rot = sb("rot", [P, 2 * DIM])
        swp = sb("swp", [P, 2 * DIM])
        used_twice_too = sb("used_twice_too", [P, 10 * DIM])
        select = used_twice_too[:, 0:4 * DIM].bitcast(F16).rearrange("p (h t) -> p h t", t=P)
        kT = used_twice_too[:, 4 * DIM:8 * DIM].bitcast(F16).rearrange("p (m a t) -> p m a t", a=2, t=P)
        qT = used_twice_too[:, 8 * DIM:10 * DIM].bitcast(F16).rearrange("p (m t) -> p m t", t=P)
        vhi = sb("vhi", [P, 2, HEADS, VW], F16)
        vlo = sb("vlo", [P, 2, HEADS, VW], F16)
        rowmax = sb("rowmax", [P, HEADS])
        negmax = sb("negmax", [P, P], F16)
        negmaxT = sb("negmaxT", [P, P], F16)
        prob = sb("prob", [P, RING, CH * P])
        phi = sb("phi", [P, RING, CH * P], F16)
        plo = sb("plo", [P, RING, CH * P], F16)
        recip = sb("recip", [P, HALF])
        attn = sb("attn", [P, DIM])
        attnT = sb("attnT", [P, 2, KC, P], F16)
        xn2 = sb("xn2", [P, 2, DIM])
        xn2T = sb("xn2T", [P, KC, P])
        logits = sb("logits", [P, B, E])
        score = sb("score", [P, B, E])
        routing = sb("routing", [P, B, E])
        best = sb("best", [P, B, 8])
        best_at = sb("best_at", [P, B, 8], U32)
        chosen = sb("chosen", [P, B, TOPK])
        expert_no = sb("expert_no", [P, E])
        mask = sb("mask", [P, GROUPS, E])
        mask16 = sb("mask16", [P, GROUPS, E], F16)
        work = sb("work", [P, GROUPS, E])
        picked = sb("picked", [P, B, TOPK])
        pick_sum = sb("pick_sum", [P, B])
        gates = sb("gates", [P, B, TOPK])
        tiles_of = sb("tiles_of", [P, E])
        one_e = sb("one_e", [P, E])
        tiles_end = sb("tiles_end", [P, E])
        first_slot = sb("first_slot", [P, E])
        slot = sb("slot", [P, GROUPS])
        slot_tile = sb("slot_tile", [P, GROUPS])
        slot_row = sb("slot_row", [P, GROUPS])
        slot_u = sb("slot_u", [P, GROUPS], U32)
        token_no = sb("token_no", [P, GROUPS])
        row_no = sb("row_no", [P, P])
        row_is = prob[:].rearrange("p r n -> p (r n)").bitcast(F16).rearrange("p (g t) -> p g t", t=P)
        number_at = phi[:].rearrange("p r n -> p (r n)")[:, 0:GROUPS * TILES].rearrange("p (g t) -> p g t", t=TILES)
        tile_no = sb("tile_no", [P, TILES])
        tile_cmp = sb("tile_cmp", [P, TILES, E])
        tile_expert = sb("tile_expert", [P, TILES])
        tile_expert_i = sb("tile_expert_i", [P, TILES], I32)
        tile_new = sb("tile_new", [P, TILES], I32)
        tiles_in_use = sb("tiles_in_use", [P, 1], I32)
        table = sb("table", [P, TILES], U32)
        w13 = sb("w13", [P, 2, KC, W13])
        w2 = sb("w2", [P, 2, len(ICH), DIM])
        wq_in = w13[:, 0].rearrange("p c n -> p (c n)")[:, 0:KC * DIM].rearrange("p (c n) -> p c n", c=KC)
        wkv_in = w13[:, 1].rearrange("p c n -> p (c n)")[:, 0:KCC * 2 * DIM].rearrange("p (c n) -> p c n", c=KCC)
        wo_in = w2[:].rearrange("p b c n -> p (b c n)")[:, 0:KC * DIM].rearrange("p (c n) -> p c n", c=KC)
        row_at = sb("row_at", [P, 2, 1], U32)
        W2N = len(ICH) * DIM
        each = 2 * (KC * W13 + W2N) // 2

        def split_in(words):
            at = words.bitcast(F16)
            return (at[:, 0:2 * KC * W13].rearrange("p (a c n) -> p a c n", a=2, c=KC),
                    at[:, 2 * KC * W13:].rearrange("p (a c n) -> p a c n", a=2, c=len(ICH)))

        split = {0: split_in(used_twice[:, 0:each]), 1: split_in(used_twice[:, each:2 * each]),
                 "shared": split_in(used_twice_too[:, 0:each])}
        xe = sb("xe", [P, 2, 2, DIM], F16)
        xeT = sb("xeT", [P, 2, 2, KC, P], F16)
        w_scale = sb("w_scale", [P, 1])
        scaled = swp[:, 0:W13]
        act_g = sb("act_g", [P, INNER])
        hidden = sb("hidden", [P, len(ICH) * P])
        hiddenT = sb("hiddenT", [P, 2, len(ICH), P], F16)
        ye = sb("ye", [P, 2, DIM])
        xn2_parts = ye[:].rearrange("p b d -> p (b d)").bitcast(F16).rearrange("p (b a d) -> p b a d", a=2, d=DIM)
        xe_late = xn2[:].rearrange("p b d -> p (b d)").bitcast(F16).rearrange("p (b a d) -> p b a d", a=2, d=DIM)
        y_at = sb("y_at", [P, GOT, TOPK], U32)
        free = [prob[:, n, :] for n in range(RING)] + [t[:, n * DIM:(n + 1) * DIM] for t in (qk, rot) for n in range(2)]
        y_got = [free[TOPK * n:TOPK * n + TOPK] for n in range(GOT)]

        p_tr = ps("p_tr", [P, KC, P])
        p_qk = ps("p_qk", [P, 2 * DIM])
        p_v = ps("p_v", [P, DIM])
        p_st32 = ps("p_st", [P, 512])
        p_st = p_st32[:].bitcast(F16).rearrange("p (n t) -> p n t", t=P)
        p_sc = [ps(f"p_sc{n}", [P, CH * P]) for n in range(2)]
        p_pv = ps("p_pv", [P, 512])
        pv = p_pv[:, 0:HALF * VW].rearrange("p (h d) -> p h d", d=VW)
        p_xT = p_tr[:].rearrange("p c t -> p (c t)").bitcast(F16).rearrange("p (a c t) -> p a c t", a=2, t=P)
        p_g, p_u, p_hT = p_qk[:, 0:INNER], p_qk[:, DIM:DIM + INNER], p_v[:, 0:len(ICH) * P]
        p_y = p_sc
        p_rank = p_st32[:].rearrange("p (g e) -> p g e", e=E)
        p_total = p_pv[:, 0:E]
        p_table = p_pv[:, 0:TILES]

        w_o = sem("w_o"); w_hi = sem("w_hi"); w_lo = sem("w_lo"); ctx_hi = sem("ctx_hi"); ctx_lo = sem("ctx_lo"); w_q = sem("w_q"); w_kv = sem("w_kv"); w_late = sem("w_late"); w_shared = sem("w_shared")
        x_early = sem("x_early"); x_late = sem("x_late"); pos_loaded = sem("pos_loaded")
        ctx_loaded = sem("ctx_loaded")
        cleared = sem("cleared"); ident_ready = sem("ident_ready"); consts = sem("consts"); zeroed = sem("zeroed")
        trig = sem("trig"); sines = sem("sines"); rot_setup = sem("rot_setup"); tables_ready = sem("tables_ready"); w_bout = sem("w_bout");
        ln1_step = sem("ln1_step"); rstd1_ready = sem("rstd1_ready")
        xnT_done = sem("xnT_done"); xnT_hi = sem("xnT_hi"); xnT_lo = sem("xnT_lo")
        q_done = sem("q_done"); k_done = sem("k_done"); v_done = sem("v_done")
        q_ready = sem("q_ready"); k_ready = sem("k_ready"); vhi_ready = sem("vhi_ready"); vlo_ready = sem("vlo_ready")
        swapped = sem("swapped"); rot_step = sem("rot_step")
        hi_ready = sem("hi_ready"); lo_ready = sem("lo_ready"); parts_ready = sem("parts_ready")
        bias_added = sem("bias_added")
        st_done = sem("st_done"); qT_ready = sem("qT_ready"); kT_ready = [sem(f"kT_ready{g}") for g in range(2)]
        scored = sem("scored"); max_ready = sem("max_ready"); neg_step = sem("neg_step")
        negT_done = sem("negT_done"); negT_ready = sem("negT_ready")
        shifted = sem("shifted"); exp_ready = sem("exp_ready")
        phi_ready = sem("phi_ready"); plo_ready = sem("plo_ready")
        pv_done = sem("pv_done"); recip_ready = sem("recip_ready"); attn_ready = sem("attn_ready")
        attnT_done = sem("attnT_done"); attnT_hi = sem("attnT_hi"); attnT_lo = sem("attnT_lo")
        wo_done = sem("wo_done"); ln2_step = sem("ln2_step"); rstd2_ready = sem("rstd2_ready")
        xn2T_done = sem("xn2T_done"); xn2T_ready = sem("xn2T_ready")
        xn2_hi = sem("xn2_hi"); xn2_lo = sem("xn2_lo")
        xn2_stored = sem("xn2_stored"); gate_done = sem("gate_done"); logits_kept = sem("logits_kept")
        gate_exp = sem("gate_exp"); route = sem("route"); masks_ready = sem("masks_ready")
        counted = sem("counted"); experts_known = sem("experts_known"); slots_known = sem("slots_known")
        gates_known = sem("gates_known")
        placed = sem("placed"); table_made = sem("table_made"); table_ready = sem("table_ready")
        xe_gathered = [sem(f"xe_gathered{n}") for n in range(2)]
        w13_loaded = [sem(f"w13_loaded{n}") for n in range(2)]
        w2_loaded = [sem(f"w2_loaded{n}") for n in range(2)]
        row_copied = sem("row_copied")
        hi13 = sem("hi13"); lo13_dve = sem("lo13_dve"); lo13_pool = sem("lo13_pool")
        hi2 = sem("hi2"); lo2 = sem("lo2"); w13_scaled = sem("w13_scaled")
        early, late = TileSems(sem, "early", 0, xe), TileSems(sem, "late", EARLY, xe_late)
        early_over = sem("early_over")
        y_cleared = sem("y_cleared")
        y_stored = [sem(f"y_stored{n}") for n in range(2)]
        y_at_copied = sem("y_at_copied")
        y_gathered = [sem(f"y_gathered{n}") for n in range(GOT)]
        summed = sem("summed")
        out_stored = sem("out_stored")

        x_t = x.rearrange("b p d -> p b d")
        out_t = out.rearrange("b p d -> p b d")

        block = stack.enter_context(nc.Block())

        def later(b, n):
            return not isinstance(b, int) or b >= n

        def pipeline(body, eng, first, last, loop_from, loops, ahead=()):
            def step(b, par):
                def on(d, part, *args):
                    if isinstance(b, int) and b + d == 0 and part in ahead:
                        return
                    if not isinstance(b, int) or 0 <= b + d < B:
                        part(b + d, (par + d) % 2, *args)
                body(b, on)

            for b in range(first, loop_from):
                step(b, b % 2)
            with eng.Fori(0, loops) as r:
                for u in range(2):
                    step(r * 2 + (loop_from + u), (loop_from + u) % 2)
            for b in range(loop_from + 2 * loops, last + 1):
                step(b, b % 2)

        def tile_count(eng):
            eng.wait_ge(experts_known, 3)
            return eng.value_load(tiles_in_use[0:1, 0:1], min_val=GROUPS, max_val=TILES)

        def expert_tiles(body, eng, beside=lambda n: None, ahead=None, unused=None):
            kinds = ["shared"] * EARLY + ["routed"] * TILES + [None] * 3

            def one(n):
                if ahead:
                    ahead(n, n // 2, n % 2, kinds[n:n + 4])
                body(n, n // 2, n % 2, kinds[n:n + 4])

            def two(r, base, kind):
                for u in range(2):
                    args = r * 2 + (base + u), r + base // 2, u, [kind] * 4
                    if ahead:
                        ahead(*args)
                    body(*args)

            def one_if_used(n, *args):
                if ahead and args[-1][2]:
                    with eng.If(count > n + (1 - EARLY)):
                        ahead(n, *args)
                body(n, *args)

            def some_if_used(tiles_of):
                first, rest = tiles_of[0], tiles_of[1:]
                with eng.If(count > first[0] - EARLY):
                    one_if_used(*first)
                    if rest:
                        some_if_used(rest)
                if unused:
                    with eng.If(count <= first[0] - EARLY):
                        for args in tiles_of:
                            unused(*args[1:])

            for n in range(EARLY):
                one(n)
                beside(n)
            with eng.Fori(0, (GROUPS - 2) // 2) as r:
                two(r, EARLY, "routed")
            count = tile_count(eng)
            with eng.Fori(0, (TILES - 1 - GROUPS) // 2) as r:
                some_if_used([(r * 2 + (EARLY + GROUPS - 2 + u), r + (EARLY + GROUPS - 2) // 2, u, ["routed"] * 4)
                              for u in range(2)])
            some_if_used([(n, n // 2, n % 2, kinds[n:n + 4]) for n in range(EARLY + TILES - 3, EARLY + TILES)])

        def late_tiles(body, ahead=lambda *args: None):
            kinds = ["shared"] * (B - EARLY) + [None] * 3
            for n in range(B - EARLY):
                ahead(n, n // 2, n % 2, kinds[n:n + 4])
                body(n, n // 2, n % 2, kinds[n:n + 4])

        def end_early(eng, last):
            last.then_inc(early_over, 1)
            eng.wait_ge(early_over, 5)

        def split_no(n):
            return n - (EARLY - 2)

        assert B % 2 == 0 and EARLY % 2 == 0 and EARLY >= 6 and B == 3 * (B - EARLY) - 2 and TILES % 2 == 1 and GROUPS % 2 == 0

        @block.sync
        def _(sp):
            sp.nop().then_inc(xn2_stored, 16)
            sp.nop().then_inc(y_stored[0], 16)
            sp.nop().then_inc(y_stored[1], 16)
            sp.dma_start(stream[:, 0:1, :], x_t[:, 0:1, :]).then_inc(x_early, 16)
            sp.dma_start(wkv_in, wkv.rearrange("(c p) n -> p c n", p=P)).then_inc(w_kv, 16)
            sp.dma_start(ctx_sb[:, 0], ctxT[0].rearrange("(c p) t -> p c t", p=P)).then_inc(ctx_loaded, 16)
            sp.dma_start(wq_in, wq.rearrange("(c p) n -> p c n", p=P)).then_inc(w_q, 16)
            sp.wait_ge(ctx_loaded, 16)
            sp.wait_ge(x_early, 16)
            sp.dma_start(ctx_sb[:, 1], ctxT[1].rearrange("(c p) t -> p c t", p=P)).then_inc(ctx_loaded, 16)
            sp.dma_start(stream[:, 1:2, :], x_t[:, 1:2, :]).then_inc(x_early, 16)
            sp.dma_start(wo_in, wo.rearrange("(c p) n -> p c n", p=P)).then_inc(w_o, 16)
            sp.dma_start(stream[:, 2:B, :], x_t[:, 2:B, :]).then_inc(x_late, 16)
            sp.dma_start(gate_sb[:], gateT.rearrange("(c p) n -> p c n", p=P)).then_inc(w_late, 16)
            sp.dma_start(gbias_sb[:], gbias.partition_broadcast(P)).then_inc(w_late, 16)
            sp.wait_ge(consts, 1)

            with sp.Fori(GROUPS, TILES) as j:
                sp.dma_start(y_dram[bass.ds(j * P, P)], ye[:, 0]).then_inc(y_cleared, 16)

            def store_xn2(b, par):
                sp.wait_ge(xn2_lo, b + 1)
                sp.wait_ge(xn2_stored, b * 16 + 16)
                sp.dma_start(xn2_dram[bass.ds(b * P, P)], xn2_parts[:, par].rearrange("p a d -> p (a d)")).then_inc(xn2_stored, 16)

            def load_ctx(b, half):
                if later(b, 2):
                    sp.wait_ge(ctx_lo, b - 1)
                sp.wait_ge(ctx_loaded, b * 16)
                sp.dma_start(ctx_sb[:, half], ctxT[bass.ds(b, 1)].rearrange("o (c p) t -> p (o c) t", p=P)).then_inc(ctx_loaded, 16)

            def step(b, on):
                on(4, load_ctx)
                if isinstance(b, int) and b == B:
                    sp.wait_ge(xn2_stored, 3 * 16)
                    for n in range(2):
                        sp.dma_start(xe[:, n].rearrange("p a d -> p (a d)"), xn2_dram[n * P:(n + 1) * P]).then_inc(early.xe_loaded[n], 16)
                on(-1, store_xn2)

            load_ctx(2, 0)
            load_ctx(3, 1)
            sp.wait_ge(w_lo, KCC + 2 * KC)
            sp.dma_start(w13[:, 0], s13.rearrange("(c p) n -> p c n", p=P)).then_inc(w_shared, 16)
            sp.dma_start(w2[:, 0, 0:2, :], s2[0:2 * P].rearrange("(c p) n -> p c n", p=P)).then_inc(w_shared, 16)
            sp.dma_start(w2[0:ICH[2][1], 0, 2, :], s2[2 * P:INNER]).then_inc(w_shared, 16)
            pipeline(step, sp, 0, B, 2, (B - 6) // 2)
            sp.wait_ge(xn2_stored, B * 16 + 16)

            def tiles(sems):
                def expert_of(j, kept):
                    e = sp.value_load(tile_expert_i[0:1, bass.ds(j, 1)], min_val=0, max_val=E - 1)
                    new = {"cond": sp.value_load(tile_new[0:1, bass.ds(j, 1)], min_val=0, max_val=1)} if kept else {}
                    return e, new

                def load_w13(n, par, kept):
                    e, new = expert_of(n - EARLY, kept)
                    if kept or par == 0:
                        done = split_no(n - 2) if kept else 1
                        sp.wait_ge(lo13_dve, done * (KC - 1))
                        sp.wait_ge(lo13_pool, done)
                    sp.dma_start(w13[:, par], e13[bass.ds(e, 1)].rearrange("o (c p) n -> p (o c) n", p=P), **new).then_inc(w13_loaded[par], 16)

                def load_w2(n, par, kept):
                    e, new = expert_of(n - EARLY, kept)
                    if kept or par == 0:
                        done = split_no(n - 2) if kept else 1
                        sp.wait_ge(lo2, done * len(ICH))
                    sp.dma_start(w2[:, par, 0:2, :], e2[bass.ds(e, 1), 0:2 * P].rearrange("o (c p) n -> p (o c) n", p=P), **new).then_inc(w2_loaded[par], 16)
                    sp.dma_start(w2[0:ICH[2][1], par, 2, :], e2[bass.ds(e, 1), 2 * P:INNER].rearrange("o p n -> (o p) n"), **new).then_inc(w2_loaded[par], 16)

                def load_rows(n, par):
                    if later(n, 2):
                        sp.wait_ge(sems.xeT_done, n - 1)
                    sp.dma_start(sems.rows[:, par].rearrange("p a d -> p (a d)"), xn2_dram[bass.ds((n + sems.first) * P, P)]).then_inc(sems.xe_loaded[par], 16)

                if sems is early:
                    sp.wait_ge(y_cleared, (TILES - GROUPS) * 16)
                    load_rows(2, 0)
                    for n in range(2):
                        sp.dma_start(late.rows[:, n].rearrange("p a d -> p (a d)"), xn2_dram[(EARLY + n) * P:(EARLY + n + 1) * P]).then_inc(late.xe_loaded[n], 16)
                else:
                    load_rows(2, 0)

                def loads(n, m, par, kinds):
                    if kinds[3] == "shared":
                        load_rows(n + 3, 1 - par)
                    if kinds[2:] == ["shared", "routed"]:
                        sp.wait_ge(experts_known, 3)
                    if kinds[3] == "routed":
                        load_w13(n + 3, 1 - par, kept=kinds[1] == "routed")
                    if kinds[2] == "routed":
                        load_w2(n + 2, par, kept=kinds[0] == "routed")

                def tile(n, m, par, kinds):
                    if kinds[0] == "routed":
                        sp.wait_ge(sems.y_ready, n + 1)
                        sp.dma_start(y_dram[bass.ds((n - EARLY) * P, P)], ye[:, par]).then_inc(y_stored[par], 16)

                def unused(m, par, kinds):
                    sp.nop().then_inc(y_stored[par], 16)

                if sems is early:
                    expert_tiles(tile, sp, ahead=loads, unused=unused)
                else:
                    late_tiles(tile, ahead=loads)
            tiles(early)
            end_early(sp, sp.nop())
            tiles(late)

            with sp.Fori(0, B) as b:
                sp.wait_ge(summed, b * 2 + (2 * GOT + 2))
                sp.dma_start(out_t[:, bass.ds(b, 1), :], stream[:, bass.ds(b, 1), :]).then_inc(out_stored, 16)
            sp.wait_ge(out_stored, B * 16)

        @block.tensor
        def _(pe):
            def transpose_rows(rows, done):
                for c in range(KC):
                    mm = pe.transpose(p_tr[:, c, :], rows[:, c * P:(c + 1) * P], ident[:])
                mm.then_inc(done, 1)

            def xn_transpose(b, par):
                pe.wait_ge(ln1_step, b * 4 + 4)
                if later(b, 1):
                    pe.wait_ge(xnT_lo, b)
                if later(b, 3):
                    pe.wait_ge(logits_kept, b - 2)
                transpose_rows(xn, xnT_done)

            PARTS = [(0, 0), (0, 1), (1, 0)]

            def product(to, rows, w, c, last):
                for r_part, w_part in PARTS:
                    mm = pe.matmul(to, rows[:, r_part, c, :], w[:, w_part, c, :],
                                   start=(c == 0 and r_part + w_part == 0), stop=(c == last and r_part == 1))
                return mm

            def project_q(b, par, c):
                if c == 0:
                    pe.wait_ge(xnT_lo, b + 1)
                    if later(b, 1):
                        pe.wait_ge(q_ready, b)
                    else:
                        pe.wait_ge(w_lo, KCC + KC)
                mm = product(p_qk[:, 0:DIM], xnT, wq16, c, KC - 1)
                if c == KC - 1:
                    mm.then_inc(q_done, 1)

            def project_k(b, par, c):
                if c == 0:
                    pe.wait_ge(ctx_lo, b + 1)
                    if later(b, 1):
                        pe.wait_ge(k_ready, b)
                    else:
                        pe.wait_ge(w_lo, KCC)
                mm = product(p_qk[:, DIM:2 * DIM], ctx16[:, par], wkv16[:, :, :, 0:DIM], c, KCC - 1)
                if c == KCC - 1:
                    mm.then_inc(k_done, 1)

            def project_v(b, par, c):
                if c == 0:
                    pe.wait_ge(ctx_lo, b + 1)
                    if later(b, 2):
                        pe.wait_ge(ln2_step, b * 5 - 9)
                    elif later(b, 1):
                        pe.wait_ge(vlo_ready, b)
                mm = product(p_v[:], ctx16[:, par], wkv16[:, :, :, DIM:2 * DIM], c, KCC - 1)
                if c == KCC - 1:
                    mm.then_inc(v_done, 1)

            def stack_transpose(b, par, g):
                if g == 0:
                    pe.wait_ge(parts_ready, b * 3 + 3)
                    if later(b, 1):
                        pe.wait_ge(negT_ready, b)
                elif g == 1:
                    pe.wait_ge(qT_ready, b * 2 + 1)
                elif g == 2:
                    pe.wait_ge(kT_ready[0], b * 2 + 2)
                else:
                    pe.wait_ge(qT_ready, b * 2 + 2)
                for n in range(8):
                    h = g % 2 * HEADS + 2 * (8 * (g // 2) + n)
                    mm = pe.transpose(p_st[:, n, :], parts[:, h:h + 2, :].rearrange("p h k -> p (h k)"), ident16[:])
                mm.then_inc(st_done, 1)

            def scores(b, par, c):
                if c == 0:
                    pe.wait_ge(qT_ready, b * 2 + 1)
                    pe.wait_ge(kT_ready[0], b * 2 + 2)
                if c == NCH // 2:
                    pe.wait_ge(qT_ready, b * 2 + 2)
                    pe.wait_ge(kT_ready[1], b * 2 + 2)
                if c >= 2:
                    pe.wait_ge(max_ready, b * NCH + c - 1)
                elif later(b, 1):
                    pe.wait_ge(exp_ready, b * NCH - 1 + c)
                for n in range(2):
                    pair = 2 * c + n
                    mm = pe.matmul(p_sc[c % 2][:, 2 * n * P:(2 * n + 2) * P], qT[:, pair, :],
                                   kT[:, pair].rearrange("p a t -> p (a t)"), start=True, stop=True)
                mm.then_inc(scored, 1)

            def negmax_transpose(b, par):
                pe.wait_ge(neg_step, b * 2 + 2)
                pe.wait_ge(kT_ready[1], b * 2 + 2)
                pe.transpose(p_st[:, 0, :], negmax[:], ident16[:]).then_inc(negT_done, 1)

            def shifted_scores(b, par, c):
                if c == 0:
                    pe.wait_ge(negT_ready, b + 1)
                if c >= 2:
                    pe.wait_ge(exp_ready, b * NCH + c - 1)
                for n in range(CH):
                    h = CH * c + n
                    to = p_sc[c % 2][:, n * P:(n + 1) * P]
                    pe.matmul(to, kT[:, h // 2, h % 2, :], qT[:, h // 2, :], start=True, stop=False)
                    mm = pe.matmul(to, select[:, h, :], negmaxT[:], start=False, stop=True)
                mm.then_inc(shifted, 1)

            def weigh_values(b, par, c):
                if c == 0:
                    pe.wait_ge(vlo_ready, b + 1)
                    if later(b, 1):
                        pe.wait_ge(attn_ready, b * 2)
                if c == NCH // 2:
                    pe.wait_ge(attn_ready, b * 2 + 1)
                pe.wait_ge(plo_ready, b * NCH + c + 1)
                for n in range(CH):
                    h = CH * c + n
                    to = pv[:, h % HALF, :]
                    w_hi, w_lo = (t[:, c % RING, n * P:(n + 1) * P] for t in (phi, plo))
                    pe.matmul(to, w_hi, vhi[:, par, h, :], start=True, stop=False)
                    pe.matmul(to, w_hi, vlo[:, par, h, :], start=False, stop=False)
                    mm = pe.matmul(to, w_lo, vhi[:, par, h, :], start=False, stop=True)
                mm.then_inc(pv_done, 1)

            def attn_transpose(b, par):
                pe.wait_ge(attn_ready, b * 2 + 2)
                last_xn = B if isinstance(b, int) and b + 3 > B else b + 3
                pe.wait_ge(xnT_lo, last_xn)
                if isinstance(b, int) and b + 3 > B:
                    pe.wait_ge(logits_kept, b)
                transpose_rows(attn, attnT_done)

            def project_out(b, par, c):
                if c == 0:
                    pe.wait_ge(attnT_lo, b + 1)
                    if not later(b, 1):
                        pe.wait_ge(w_lo, KCC + 2 * KC)
                    last_v = B if isinstance(b, int) and b + 2 > B else b + 2
                    pe.wait_ge(vlo_ready, last_v)
                    if isinstance(b, int) and b + 2 > B:
                        pe.wait_ge(ln2_step, b * 5 - 4)
                mm = product(p_v[:], attnT, wo16, c, KC - 1)
                if c == KC - 1:
                    mm.then_inc(wo_done, 1)

            def xn2_transpose(b, par):
                pe.wait_ge(ln2_step, b * 5 + 5)
                pe.wait_ge(attnT_lo, b + 1)
                transpose_rows(xn2[:, par], xn2T_done)

            def gate_logits(b, par):
                pe.wait_ge(xn2T_ready, b + 1)
                for c in range(KC):
                    mm = pe.matmul(p_tr[:, 0, 0:E], xn2T[:, c, :], gate_sb[:, c, :], start=(c == 0), stop=(c == KC - 1))
                mm.then_inc(gate_done, 1)

            pe.wait_ge(ident_ready, 1)
            xn_transpose(0, 0)

            def step(b, on):
                if isinstance(b, int) and b == 0:
                    pe.wait_ge(w_late, 2 * 16)
                    pe.wait_ge(consts, 1)
                on(-1, attn_transpose)
                on(2, project_k, 0)
                on(0, negmax_transpose)
                on(2, project_k, 1)
                on(0, shifted_scores, 0)
                on(0, shifted_scores, 1)
                on(-1, project_out, 0)
                on(0, shifted_scores, 2)
                on(-1, project_out, 1)
                on(-1, project_out, 2)
                on(-1, project_out, 3)
                on(0, weigh_values, 0)
                on(0, shifted_scores, 3)
                on(0, weigh_values, 1)
                on(0, shifted_scores, 4)
                on(0, shifted_scores, 5)
                on(1, project_v, 0)
                on(0, shifted_scores, 6)
                on(0, shifted_scores, 7)
                on(1, stack_transpose, 0)
                on(0, weigh_values, 2)
                on(1, project_v, 1)
                on(-1, xn2_transpose)
                on(1, stack_transpose, 1)
                on(0, weigh_values, 3)
                on(-1, gate_logits)
                on(2, xn_transpose)
                on(1, stack_transpose, 2)
                on(1, scores, 0)
                on(1, scores, 1)
                on(0, weigh_values, 4)
                on(0, weigh_values, 5)
                on(0, weigh_values, 6)
                on(1, stack_transpose, 3)
                on(0, weigh_values, 7)
                on(1, scores, 2)
                on(2, project_q, 0)
                on(1, scores, 3)
                on(2, project_q, 1)
                on(1, scores, 4)
                on(2, project_q, 2)
                on(1, scores, 5)
                on(1, scores, 6)
                on(2, project_q, 3)
                on(1, scores, 7)

            pipeline(step, pe, -2, B, 2, (B - 4) // 2, ahead=[xn_transpose])

            def tiles(sems):
                def rows_transpose(n, m, par, kind):
                    if kind == "shared":
                        pe.wait_ge(sems.xe_loaded[par], m * 16 + 16)
                    else:
                        pe.wait_ge(xe_gathered[par], (m - (EARLY // 2 - 1)) * 16)
                    for a in range(2):
                        for c in range(KC):
                            mm = pe.transpose(p_xT[:, a, c, :], sems.rows[:, par, a, c * P:(c + 1) * P], ident16[:])
                    mm.then_inc(sems.xeT_done, 1)

                def gate_up(n, m, par, kind):
                    pe.wait_ge(sems.xeT_ready, n + 1)
                    if kind == "routed":
                        pe.wait_ge(lo13_dve, split_no(n) * (KC - 1))
                        pe.wait_ge(lo13_pool, split_no(n))
                    w = split["shared" if kind == "shared" else par][0]
                    for p_out, at, done in ((p_g, 0, sems.g_done), (p_u, INNER, sems.u_done)):
                        for c in range(KC):
                            for x_part, w_part in PARTS:
                                mm = pe.matmul(p_out, xeT[:, par, x_part, c, :], w[:, w_part, c, at:at + INNER],
                                               start=(c == 0 and x_part + w_part == 0), stop=(c == KC - 1 and x_part == 1))
                        mm.then_inc(done, 1)

                def hidden_transpose(n):
                    pe.wait_ge(sems.hidden_ready, n + 1)
                    for c in range(len(ICH)):
                        mm = pe.transpose(p_hT[:, c * P:(c + 1) * P], hidden[:, c * P:(c + 1) * P], ident[:])
                    mm.then_inc(sems.hT_done, 1)

                def down(n, m, par, kind):
                    pe.wait_ge(sems.hT_hi, n + 1)
                    pe.wait_ge(sems.hT_lo, n + 1)
                    if later(n, 2):
                        pe.wait_ge(sems.y_ready, n - 1)
                    if kind == "routed":
                        pe.wait_ge(lo2, split_no(n) * len(ICH))
                    w = split["shared" if kind == "shared" else par][1]
                    for c, (i, k) in enumerate(ICH):
                        for h_part, w_part in PARTS:
                            mm = pe.matmul(p_y[par][:], hiddenT[0:k, h_part, c, :], w[0:k, w_part, c, :],
                                           start=(c == 0 and h_part + w_part == 0), stop=(c == len(ICH) - 1 and h_part == 1))
                    mm.then_inc(sems.y_done, 1)

                def tile(n, m, par, kinds):
                    hidden_transpose(n)
                    if kinds[1]:
                        gate_up(n + 1, m + par, 1 - par, kinds[1])
                    if kinds[2]:
                        rows_transpose(n + 2, m + 1, par, kinds[2])
                    down(n, m, par, kinds[0])

                def count():
                    pe.wait_ge(masks_ready, 1)
                    pe.matmul(p_st32[:], before[:], mask16[:].rearrange("p g e -> p (g e)"), start=True, stop=False)
                    for g in range(GROUPS - 1):
                        rest = GROUPS - 1 - g
                        pe.matmul(p_rank[:, g + 1:GROUPS, :], ones16[:],
                                  mask16[:, g:g + 1, :].broadcast_to([P, rest, E]),
                                  start=False, stop=(g == GROUPS - 2))
                    for g in range(GROUPS):
                        mm = pe.matmul(p_total, ones16[:], mask16[:, g, :], start=(g == 0), stop=(g == GROUPS - 1))
                    mm.then_inc(counted, 1)

                def place():
                    pe.wait_ge(placed, GROUPS // PLACED + 1)
                    for g in range(GROUPS):
                        mm = pe.matmul(p_table, row_is[:, g, :], number_at[:, g, :], start=(g == 0), stop=(g == GROUPS - 1))
                    mm.then_inc(table_made, 1)

                def beside(n):
                    if n == 2:
                        count()
                    if n == 5:
                        place()

                pe.wait_ge(logits_kept, B)
                pe.wait_ge(q_ready, B)
                pe.wait_ge(k_ready, B)
                rows_transpose(0, 0, 0, "shared")
                pe.wait_ge(sems.xeT_ready, 1)
                rows_transpose(1, 0, 1, "shared")
                pe.wait_ge(lo13_dve, KC - 1)
                pe.wait_ge(lo13_pool, 1)
                pe.wait_ge(lo2, len(ICH))
                gate_up(0, 0, 0, "shared")
                if sems is early:
                    expert_tiles(tile, pe, beside)
                else:
                    late_tiles(tile)
            tiles(early)
            end_early(pe, pe.matmul(p_pv[:, 0:E], ident16[:], ones16[:, 0:E], start=True, stop=True))
            tiles(late)

        @block.scalar
        def _(act):
            def xnT_copy(b, par):
                act.wait_ge(xnT_done, b + 1)
                if later(b, 1):
                    act.wait_ge(q_done, b)
                act.copy(xnT[:, 0], p_tr[:]).then_inc(xnT_hi, 1)

            def q_copy(b, par):
                act.wait_ge(q_done, b + 1)
                if later(b, 1):
                    act.wait_ge(rot_step, b * 2 - 1)
                    act.wait_ge(swapped, b * 2)
                act.activation(qk[:, 0:DIM], p_qk[:, 0:DIM], ACT.Copy, scale=1 / W_SCALE).then_inc(q_ready, 1)

            def k_copy(b, par):
                act.wait_ge(k_done, b + 1)
                if later(b, 1):
                    act.wait_ge(rot_step, b * 2 - 1)
                    act.wait_ge(swapped, b * 2)
                act.activation(qk[:, DIM:2 * DIM], p_qk[:, DIM:2 * DIM], ACT.Copy, scale=1 / W_SCALE).then_inc(k_ready, 1)

            def vhi_copy(b, par):
                act.wait_ge(v_done, b + 1)
                if later(b, 2):
                    act.wait_ge(pv_done, b * NCH - NCH)
                act.activation(vhi[:, par, :, 0:HD], p_v[:].rearrange("p (h d) -> p h d", d=HD), ACT.Copy, scale=1 / W_SCALE).then_inc(vhi_ready, 1)

            def hi_copy(b, par):
                act.wait_ge(rot_step, b * 2 + 2)
                if later(b, 1):
                    act.wait_ge(st_done, b * 4)
                act.copy(parts[:, :, 0:HD], rot[:].rearrange("p (h d) -> p h d", d=HD)).then_inc(hi_ready, 1)

            def qT_copy(b, par, half):
                act.wait_ge(st_done, b * 4 + (2 * half + 1))
                if later(b, 1):
                    act.wait_ge(shifted, b * NCH)
                act.copy(qT[:, 8 * half:8 * half + 8, :], p_st[:]).then_inc(qT_ready, 1)

            def kT_copy(b, par):
                act.wait_ge(st_done, b * 4 + 4)
                for a in range(2):
                    rows = slice(a * STACK, (a + 1) * STACK)
                    act.copy(kT[rows, 8:16, a, :], p_st[rows]).then_inc(kT_ready[1], 1)

            def exp(b, par, c):
                act.wait_ge(shifted, b * NCH + c + 1)
                if later(b, 1) or c >= RING:
                    act.wait_ge(plo_ready, b * NCH + c + 1 - RING)
                act.activation(prob[:, c % RING, :], p_sc[c % 2][:], ACT.Exp, scale=SCALE).then_inc(exp_ready, 1)

            def attnT_copy(b, par):
                act.wait_ge(attnT_done, b + 1)
                if later(b, 1):
                    act.wait_ge(wo_done, b)
                act.copy(attnT[:, 0], p_tr[:]).then_inc(attnT_hi, 1)

            def xn2T_copy(b, par):
                act.wait_ge(xn2T_done, b + 1)
                act.copy(xn2T[:], p_tr[:]).then_inc(xn2T_ready, 1)

            def xn2_high(b, par):
                act.wait_ge(ln2_step, b * 5 + 5)
                if later(b, 1):
                    act.wait_ge(xn2_stored, b * 16)
                else:
                    act.wait_ge(y_cleared, (TILES - GROUPS) * 16)
                act.copy(xn2_parts[:, par, 0], xn2[:, par]).then_inc(xn2_hi, 1)

            def ctx_high(b, par):
                act.wait_ge(ctx_loaded, b * 16 + 16)
                if later(b, 2):
                    act.wait_ge(k_done, b - 1)
                    act.wait_ge(v_done, b - 1)
                act.copy(ctx16[:, par, 0], ctx_sb[:, par]).then_inc(ctx_hi, 1)

            def weights_high(to, rows, chunks, loaded):
                act.wait_ge(loaded, 16)
                for c in range(chunks):
                    act.activation(to[:, 0, c], rows[:, c], ACT.Copy, scale=W_SCALE).then_inc(w_hi, 1)

            def split_shared():
                act.wait_ge(w_shared, 3 * 16)
                act.wait_ge(shifted, B * NCH)
                for c in (0, 2, 1, 3):
                    act.activation(split["shared"][0][:, 0, c], w13[:, 0, c], ACT.Copy, scale=W_SCALE).then_inc(hi13, 1)
                for c, (i, k) in enumerate(ICH):
                    act.activation(split["shared"][1][0:k, 0, c], w2[0:k, 0, c], ACT.Copy, scale=W_SCALE).then_inc(hi2, 1)

            def keep_logits(b, par):
                act.wait_ge(gate_done, b + 1)
                act.copy(logits[:, bass.ds(b, 1), :], p_tr[:, 0:1, 0:E]).then_inc(logits_kept, 1)

            weights_high(wkv16, wkv_in, KCC, w_kv)
            ctx_high(0, 0)
            xnT_copy(0, 0)
            weights_high(wq16, wq_in, KC, w_q)
            act.wait_ge(trig, 4)
            act.activation(sin_t[:].rearrange("p b (r two) -> p b r two", two=2)[:, :, :, 1], angle[:], ACT.Sin).then_inc(sines, 1)
            act.activation(cos_t[:].rearrange("p b (r two) -> p b r two", two=2)[:, :, :, 0], turns[:], ACT.Sin).then_inc(sines, 1)
            act.wait_ge(zeroed, 1)

            def step(b, on):
                on(0, exp, 1)
                on(0, exp, 2)
                on(1, hi_copy)
                on(0, exp, 3)
                on(0, exp, 4)
                on(0, exp, 5)
                on(0, exp, 6)
                on(1, qT_copy, 0)
                on(-1, xn2_high)
                on(-1, xn2T_copy)
                on(0, exp, 7)
                on(-1, keep_logits)
                on(1, vhi_copy)
                on(2, xnT_copy)
                on(1, qT_copy, 1)
                on(3, ctx_high)
                on(2, k_copy)
                on(1, kT_copy)
                on(2, q_copy)
                on(0, attnT_copy)
                on(1, exp, 0)
                if isinstance(b, int) and b == B - 1:
                    split_shared()
                if isinstance(b, int) and b == -2:
                    weights_high(wo16, wo_in, KC, w_o)

            pipeline(step, act, -3, B, 2, (B - 5) // 2, ahead=[ctx_high, xnT_copy])

            act.wait_ge(logits_kept, B)
            act.activation(score[:], logits[:], ACT.Exp, scale=-1.0).then_inc(gate_exp, 1)

            def tiles(sems):
                def xeT_copy(n, par):
                    act.wait_ge(sems.xeT_done, n + 1)
                    if later(n, 2):
                        act.wait_ge(sems.u_done, n - 1)
                    act.copy(xeT[:, par], p_xT).then_inc(sems.xeT_ready, 1)

                def gate_act(n):
                    act.wait_ge(sems.g_done, n + 1)
                    if later(n, 1):
                        act.wait_ge(sems.hidden_ready, n)
                    act.activation(act_g[:], p_g, ACT.Silu, scale=1 / W_SCALE).then_inc(sems.act_ready, 1)

                def hT_high(n):
                    act.wait_ge(sems.hT_done, n + 1)
                    if later(n, 1):
                        act.wait_ge(sems.y_done, n)
                    act.copy(hiddenT[:, 0], p_hT.rearrange("p (c t) -> p c t", t=P)).then_inc(sems.hT_hi, 1)

                def w13_high(n, m, par, c):
                    act.wait_ge(w13_loaded[par], (m - (EARLY // 2 - 1)) * 16)
                    act.wait_ge(sems.u_done, n - 1)
                    act.activation(split[par][0][:, 0, c], w13[:, par, c], ACT.Copy, scale=W_SCALE).then_inc(hi13, 1)

                def w2_high(to, par, c):
                    k = ICH[c][1]
                    act.activation(to[1][0:k, 0, c], w2[0:k, par, c], ACT.Copy, scale=W_SCALE).then_inc(hi2, 1)

                xeT_copy(0, 0)
                xeT_copy(1, 1)
                gate_act(0)

                def tile(n, m, par, kinds):
                    hT_high(n)
                    if kinds[2] == "routed":
                        for c in (0, 2):
                            w13_high(n + 2, m + 1, par, c)
                    if kinds[1]:
                        gate_act(n + 1)
                    if kinds[2] == "routed":
                        for c in (1, 3):
                            w13_high(n + 2, m + 1, par, c)
                    if kinds[2]:
                        xeT_copy(n + 2, par)
                    if kinds[1] == "routed":
                        act.wait_ge(w2_loaded[1 - par], (m + par - (EARLY // 2 - 1)) * 32)
                        if later(n, 1):
                            act.wait_ge(sems.y_done, n)
                        for c in range(len(ICH)):
                            w2_high(split[1 - par], 1 - par, c)

                if sems is early:
                    expert_tiles(tile, act)
                else:
                    late_tiles(tile)
            tiles(early)
            end_early(act, act.copy(carrier_act[:], minus_half[:]))
            tiles(late)

        @block.vector
        def _(dve):
            def ln(step, per, at, b, rows, stats, mv, rstd_ready, rstd, to, part):
                base = b * per + at
                if part == "stats":
                    dve.bn_stats(stats[:], rows).then_inc(step, 1)
                    dve.wait_ge(step, base + 1)
                    dve.memset(carrier_dve[:], 0.0)
                    dve.bn_aggr(mv[:], stats[:]).then_inc(step, 1)
                    dve.wait_ge(step, base + 2)
                    dve.tensor_scalar(mv[:, 1:2], mv[:, 1:2], EPS, None, ALU.add).then_inc(step, 1)
                else:
                    dve.wait_ge(rstd_ready, b + 1)
                    dve.tensor_scalar(to, rows, mv[:, 0:1], rstd[:, 0:1], ALU.subtract, ALU.mult).then_inc(step, 1)

            def row(b):
                return stream[:, bass.ds(b, 1), :].rearrange("p o d -> p (o d)")

            def ln1_stats(b, par):
                if not later(b, 2):
                    dve.wait_ge(x_early, b * 16 + 16)
                else:
                    dve.wait_ge(x_late, 16)
                ln(ln1_step, 4, 0, b, row(b), stats1, mv1, rstd1_ready, rstd1, xn[:], "stats")

            def ln1_norm(b, par):
                if later(b, 1):
                    dve.wait_ge(xnT_done, b)
                ln(ln1_step, 4, 0, b, row(b), stats1, mv1, rstd1_ready, rstd1, xn[:], "norm")

            def ln2_stats(b, par):
                dve.wait_ge(ln2_step, b * 5 + 1)
                dve.memset(carrier_dve[:], 0.0)
                ln(ln2_step, 5, 1, b, row(b), stats2, mv2, rstd2_ready, rstd2, xn2[:, par, :], "stats")

            def ln2_norm(b, par):
                if later(b, 2):
                    dve.wait_ge(xn2_lo, b - 1)
                    dve.wait_ge(xn2T_done, b - 1)
                ln(ln2_step, 5, 1, b, row(b), stats2, mv2, rstd2_ready, rstd2, xn2[:, par, :], "norm")

            def xnT_low(b, par):
                dve.wait_ge(xnT_hi, b + 1)
                dve.tensor_tensor(xnT[:, 1], p_tr[:], xnT[:, 0], ALU.subtract).then_inc(xnT_lo, 1)

            def attnT_low(b, par):
                dve.wait_ge(attnT_hi, b + 1)
                dve.tensor_tensor(attnT[:, 1], p_tr[:], attnT[:, 0], ALU.subtract).then_inc(attnT_lo, 1)

            def weights_low(to, rows, chunks, before_them):
                for c in range(chunks):
                    dve.wait_ge(w_hi, before_them + c + 1)
                    dve.scalar_tensor_tensor(to[:, 1, c], rows[:, c], W_SCALE, to[:, 0, c], ALU.mult, ALU.subtract).then_inc(w_lo, 1)

            def residual(b, par):
                dve.wait_ge(wo_done, b + 1)
                dve.wait_ge(bias_added, b + 1)
                dve.scalar_tensor_tensor(row(b), p_v[:], 1 / W_SCALE, row(b), ALU.mult, ALU.add).then_inc(ln2_step, 1)

            def vlo_make(b, par):
                dve.wait_ge(vhi_ready, b + 1)
                dve.scalar_tensor_tensor(vlo[:, par, :, 0:HD], p_v[:].rearrange("p (h d) -> p h d", d=HD), 1 / W_SCALE,
                                         vhi[:, par, :, 0:HD], ALU.mult, ALU.subtract).then_inc(vlo_ready, 1)

            def rotate_cos(b, par):
                dve.wait_ge(q_ready, b + 1)
                dve.wait_ge(k_ready, b + 1)
                if later(b, 1):
                    dve.wait_ge(lo_ready, b)
                c = cos_t[:, bass.ds(b, 1), :].broadcast_to([P, 2 * HEADS, HD])
                dve.tensor_tensor(rot[:].rearrange("p (h d) -> p h d", d=HD), qk[:].rearrange("p (h d) -> p h d", d=HD), c, ALU.mult).then_inc(rot_step, 1)

            def rotate_add(b, par):
                dve.wait_ge(rot_step, b * 2 + 1)
                dve.wait_ge(swapped, b * 2 + 2)
                dve.tensor_tensor(rot[:], rot[:], swp[:], ALU.add).then_inc(rot_step, 1)

            def parts_double(b, par):
                dve.wait_ge(lo_ready, b + 1)
                q, k = parts[:, 0:HEADS], parts[:, HEADS:2 * HEADS]
                dve.tensor_copy(q[:, :, 2 * HD:4 * HD], q[:, :, 0:2 * HD]).then_inc(parts_ready, 1)
                dve.tensor_copy(k[:, :, 2 * HD:3 * HD], k[:, :, HD:2 * HD]).then_inc(parts_ready, 1)
                dve.tensor_copy(k[:, :, 3 * HD:4 * HD], k[:, :, 0:HD]).then_inc(parts_ready, 1)

            def kT_copy(b, par):
                dve.wait_ge(st_done, b * 4 + 2)
                for a in range(2):
                    rows = slice(a * STACK, (a + 1) * STACK)
                    dve.tensor_copy(kT[rows, 0:8, a, :], p_st[rows]).then_inc(kT_ready[0], 1)

            def row_max(b, par, c):
                dve.wait_ge(scored, b * NCH + c + 1)
                if c == 0 and later(b, 1):
                    dve.wait_ge(neg_step, b * 2)
                dve.tensor_reduce(rowmax[:, CH * c:CH * c + CH], p_sc[c % 2][:].rearrange("p (h t) -> p h t", t=P),
                                  AX_X, ALU.max).then_inc(max_ready, 1)

            def neg_max(b, par):
                dve.wait_ge(max_ready, b * NCH + NCH)
                if later(b, 1):
                    dve.wait_ge(negT_done, b)
                dve.tensor_scalar(negmax[:, 0:HEADS], rowmax[:], -1.0, None, ALU.mult).then_inc(neg_step, 1)
                dve.wait_ge(neg_step, b * 2 + 1)
                dve.scalar_tensor_tensor(negmax[:, HEADS:2 * HEADS], rowmax[:], -1.0, negmax[:, 0:HEADS],
                                         ALU.mult, ALU.subtract).then_inc(neg_step, 1)

            def neg_copy(b, par):
                dve.wait_ge(negT_done, b + 1)
                if later(b, 1):
                    dve.wait_ge(shifted, b * NCH)
                dve.tensor_copy(negmaxT[:], p_st[:, 0, :]).then_inc(negT_ready, 1)

            def phi_make(b, par, c):
                dve.wait_ge(exp_ready, b * NCH + c + 1)
                if later(b, 1) or c >= RING:
                    dve.wait_ge(pv_done, b * NCH + c + 1 - RING)
                dve.tensor_copy(phi[:, c % RING, :], prob[:, c % RING, :]).then_inc(phi_ready, 1)

            def normalise(b, par, half):
                dve.wait_ge(pv_done, b * NCH + (half + 1) * (NCH // 2))
                if half:
                    dve.wait_ge(attn_ready, b * 2 + 1)
                elif later(b, 1):
                    dve.wait_ge(attnT_done, b)
                dve.reciprocal(recip[:], pv[:, :, HD]).then_inc(recip_ready, 1)
                dve.wait_ge(recip_ready, b * 2 + half + 1)
                to = attn[:].rearrange("p (h d) -> p h d", d=HD)[:, half * HALF:(half + 1) * HALF, :]
                dve.tensor_tensor(to, pv[:, :, 0:HD], recip[:].rearrange("p (h o) -> p h o", o=1).broadcast_to([P, HALF, HD]),
                                  ALU.mult).then_inc(attn_ready, 1)

            def w2_low(to, par, c):
                k = ICH[c][1]
                dve.scalar_tensor_tensor(to[1][0:k, 1, c], w2[0:k, par, c], W_SCALE, to[1][0:k, 0, c],
                                         ALU.mult, ALU.subtract).then_inc(lo2, 1)

            def w13_low(to, par, c):
                dve.scalar_tensor_tensor(to[0][:, 1, c], w13[:, par, c], W_SCALE, to[0][:, 0, c],
                                         ALU.mult, ALU.subtract).then_inc(lo13_dve, 1)

            def split_shared():
                dve.wait_ge(w_shared, 3 * 16)
                for c, at in ((2, 2), (1, 3), (3, 4)):
                    dve.wait_ge(hi13, at)
                    w13_low(split["shared"], 0, c)
                for c in range(len(ICH)):
                    dve.wait_ge(hi2, c + 1)
                    w2_low(split["shared"], 0, c)

            dve.wait_ge(x_early, 16)
            ln1_stats(0, 0)
            ln1_norm(0, 0)
            weights_low(wkv16, wkv_in, KCC, 0)
            xnT_low(0, 0)
            weights_low(wq16, wq_in, KC, KCC)
            dve.memset(negmax[:].bitcast(F32), 0.0)
            dve.memset(hidden[:], 0.0)
            dve.memset(used_twice_too[:, 4 * DIM:8 * DIM], 0.0)
            dve.memset(vhi[:], 1.0)
            dve.memset(vlo[:], 0.0).then_inc(zeroed, 1)
            dve.wait_ge(pos_loaded, 16)
            half = ROT // 2
            for p in range(2):
                for i in range(half):
                    last = dve.tensor_scalar(angle[:, :, p * half + i], pos_sb[:, :, p], 10000.0 ** (-i / half), None, ALU.mult)
            last.then_inc(trig, 1)
            dve.wait_ge(trig, 1)
            dve.tensor_scalar(turns[:], angle[:], 1 / (2 * pi), ROUND, ALU.mult, ALU.add).then_inc(trig, 1)
            dve.wait_ge(trig, 2)
            dve.tensor_scalar(turns[:], turns[:], -ROUND, -2 * pi, ALU.add, ALU.mult).then_inc(trig, 1)
            dve.wait_ge(trig, 3)
            dve.tensor_tensor(turns[:], turns[:], angle[:], ALU.add).then_inc(rot_setup, 1)
            dve.wait_ge(rot_setup, 1)
            dve.tensor_scalar(angle[:], turns[:], 3.1415925, -3.1415925, ALU.min, ALU.max).then_inc(rot_setup, 1)
            dve.wait_ge(rot_setup, 2)
            dve.scalar_tensor_tensor(turns[:], angle[:], -1.0, angle[:], ALU.mult, ALU.min).then_inc(rot_setup, 1)
            dve.wait_ge(rot_setup, 3)
            dve.tensor_scalar(turns[:], turns[:], pi / 2, None, ALU.add).then_inc(trig, 1)
            dve.wait_ge(sines, 2)
            cos_p = cos_t[:].rearrange("p b (r two) -> p b r two", two=2)
            sin_p = sin_t[:].rearrange("p b (r two) -> p b r two", two=2)
            dve.tensor_copy(cos_p[:, :, :, 1], cos_p[:, :, :, 0])
            dve.tensor_scalar(sin_p[:, :, :, 0], sin_p[:, :, :, 1], -1.0, None, ALU.mult).then_inc(tables_ready, 1)

            dve.wait_ge(tables_ready, 1)

            def step(b, on):
                on(0, kT_copy)
                on(-1, normalise, 0)
                on(-1, phi_make, 7)
                on(0, vlo_make)
                on(0, row_max, 0)
                on(1, xnT_low)
                on(0, row_max, 1)
                on(0, row_max, 2)
                on(-1, normalise, 1)
                on(0, row_max, 3)
                on(0, row_max, 4)
                on(0, row_max, 5)
                on(0, row_max, 6)
                on(0, row_max, 7)
                on(0, neg_max)
                on(0, neg_copy)
                on(-1, attnT_low)
                if isinstance(b, int) and b == B - 0:
                    split_shared()
                on(1, rotate_cos)
                on(0, phi_make, 0)
                on(1, rotate_add)
                on(0, phi_make, 1)
                on(0, phi_make, 2)
                on(2, ln1_norm)
                on(-1, residual)
                on(3, ln1_stats)
                on(-1, ln2_stats)
                on(1, parts_double)
                on(0, phi_make, 3)
                on(0, phi_make, 4)
                on(-1, ln2_norm)
                on(0, phi_make, 5)
                on(0, phi_make, 6)
                if isinstance(b, int) and b == -2:
                    weights_low(wo16, wo_in, KC, KCC + KC)

            pipeline(step, dve, -3, B, 3, (B - 6) // 2, ahead=[ln1_stats, ln1_norm, xnT_low])

            def combine(b):
                dve.wait_ge(y_gathered[b % GOT], b // GOT * 32 + 32)
                if b >= EARLY:
                    dve.wait_ge(late.y_ready, b - EARLY + 1)
                for k in range(TOPK):
                    g = gates[:, b:b + 1, k:k + 1].rearrange("p b k -> p (b k)")
                    dve.scalar_tensor_tensor(row(b), y_got[b % GOT][k], g, row(b), ALU.mult, ALU.add).then_inc(summed, 1)
                    dve.wait_ge(summed, b * 2 + (2 * GOT + k + 1))

            def combine_some(n, part):
                b = 3 * n + part - 2
                if b >= 0:
                    combine(b)

            def tiles(sems):
                def hidden_make(n):
                    dve.wait_ge(sems.act_ready, n + 1)
                    dve.wait_ge(sems.u_done, n + 1)
                    if later(n, 1):
                        dve.wait_ge(sems.hT_done, n)
                    dve.tensor_tensor(hidden[:, 0:INNER], p_u, act_g[:], ALU.mult).then_inc(sems.hidden_ready, 1)

                def hT_low(n):
                    dve.wait_ge(sems.hT_hi, n + 1)
                    dve.tensor_tensor(hiddenT[:, 1], p_hT.rearrange("p (c t) -> p c t", t=P), hiddenT[:, 0], ALU.subtract).then_inc(sems.hT_lo, 1)

                def y_take(n, m, par, kind):
                    dve.wait_ge(sems.y_done, n + 1)
                    if kind == "shared":
                        b = n + sems.first
                        dve.scalar_tensor_tensor(row(b), p_y[par][:], W_SCALE ** -2, row(b), ALU.mult, ALU.add).then_inc(sems.y_ready, 1)
                    else:
                        dve.wait_ge(y_stored[par], (m - (EARLY // 2 - 1)) * 16)
                        dve.tensor_scalar(ye[:, par], p_y[par][:], W_SCALE ** -2, None, ALU.mult).then_inc(sems.y_ready, 1)

                hidden_make(0)
                dve.wait_ge(y_cleared, (TILES - GROUPS) * 16)

                def tile(n, m, par, kinds):
                    hT_low(n)
                    if kinds[0] == "routed":
                        for c in range(len(ICH)):
                            dve.wait_ge(hi2, split_no(n) * 3 - 2 + c)
                            w2_low(split[par], par, c)
                    if kinds[2] == "routed":
                        dve.wait_ge(hi13, split_no(n + 2) * KC - 2)
                        w13_low(split[par], par, 2)
                    if sems is late:
                        combine_some(n, 0)
                    if kinds[1]:
                        hidden_make(n + 1)
                    if sems is late:
                        combine_some(n, 1)
                    if kinds[2] == "routed":
                        for c in (1, 3):
                            dve.wait_ge(hi13, split_no(n + 2) * KC - (3 - c) // 2)
                            w13_low(split[par], par, c)
                    y_take(n, m, par, kinds[0])
                    if sems is late:
                        combine_some(n, 2)

                steps = [0]

                def then(ins):
                    ins.then_inc(route, 1)
                    steps[0] += 1
                    dve.wait_ge(route, steps[0])

                def each_e(row_of_e, n):
                    return row_of_e.rearrange("p (o e) -> p o e", o=1).broadcast_to([P, n, E])

                def scores_and_two_best(batches_of):
                    for b in batches_of:
                        then(dve.max(best[:, b, :], routing[:, b, :]))
                        then(dve.max_index(best_at[:, b, :], best[:, b, :], routing[:, b, :]))

                def beside(n):
                    if n == 0:
                        dve.wait_ge(gate_exp, 1)
                        then(dve.tensor_scalar(score[:], score[:], 1.0, None, ALU.add))
                        then(dve.reciprocal(score[:], score[:]))
                        then(dve.tensor_tensor(routing[:], score[:], each_e(gbias_sb[:], B), ALU.add))
                        scores_and_two_best(range(0, B // 2))
                    if n == 1:
                        scores_and_two_best(range(B // 2, B))
                        then(dve.tensor_copy(chosen[:], best_at[:, :, 0:TOPK]))
                        chosen_g = chosen[:].rearrange("p b (k o) -> p (b k) o", o=1)
                        then(dve.tensor_tensor(mask[:], each_e(expert_no[:], GROUPS), chosen_g.broadcast_to([P, GROUPS, E]), ALU.is_equal))
                        dve.tensor_copy(mask16[:], mask[:]).then_inc(masks_ready, 1)
                    if n == 2:
                        s4 = score[:].rearrange("p b (o e) -> p b o e", o=1).broadcast_to([P, B, TOPK, E])
                        w4 = work[:].rearrange("p (b k) e -> p b k e", k=TOPK)
                        m4 = mask[:].rearrange("p (b k) e -> p b k e", k=TOPK)
                        then(dve.tensor_tensor(w4, m4, s4, ALU.mult))
                        then(dve.tensor_reduce(picked[:], w4, AX_X, ALU.add))
                        then(dve.tensor_reduce(pick_sum[:], picked[:], AX_X, ALU.add))
                        then(dve.reciprocal(pick_sum[:], pick_sum[:]))
                        dve.tensor_tensor(gates[:], picked[:], pick_sum[:].rearrange("p (b o) -> p b o", o=1).broadcast_to([P, B, TOPK]),
                                          ALU.mult).then_inc(gates_known, 1)
                    if n == 3:
                        dve.wait_ge(counted, 1)
                        then(dve.tensor_scalar(tiles_of[:], p_total, 1 / P, (P - 1) / P - 0.5 + 0.5 / P, ALU.mult, ALU.add))
                        then(dve.tensor_scalar(tiles_of[:], tiles_of[:], ROUND, -ROUND, ALU.add, ALU.add))
                        then(dve.tensor_tensor_scan(tiles_end[:], one_e[:], tiles_of[:], 0.0, ALU.mult, ALU.add))
                        then(dve.tensor_tensor(first_slot[:], tiles_end[:], tiles_of[:], ALU.subtract))
                        then(dve.tensor_tensor(tile_cmp[:], each_e(tiles_end[:], TILES),
                                               tile_no[:].rearrange("p (t o) -> p t o", o=1).broadcast_to([P, TILES, E]), ALU.is_le))
                        then(dve.tensor_reduce(tile_expert[:], tile_cmp[:], AX_X, ALU.add))
                        then(dve.tensor_scalar(tile_expert[:], tile_expert[:], float(E - 1), None, ALU.min))
                        dve.tensor_copy(tile_expert_i[:], tile_expert[:]).then_inc(experts_known, 1)
                        dve.tensor_tensor(tile_new[:, 2:TILES], tile_expert[:, 2:TILES], tile_expert[:, 0:TILES - 2],
                                          ALU.not_equal).then_inc(experts_known, 1)
                        dve.tensor_copy(tiles_in_use[:], tiles_end[:, E - 1:E]).then_inc(experts_known, 1)
                    if n == 3:
                        then(dve.scalar_tensor_tensor(work[:], each_e(first_slot[:], GROUPS), float(P), p_rank, ALU.mult, ALU.add))
                        then(dve.tensor_tensor(work[:], work[:], mask[:], ALU.mult))
                        then(dve.tensor_reduce(slot[:], work[:], AX_X, ALU.add))
                        then(dve.tensor_scalar(slot_tile[:], slot[:], 1 / P, -0.5 + 0.5 / P, ALU.mult, ALU.add))
                        then(dve.tensor_scalar(slot_tile[:], slot_tile[:], ROUND, -ROUND, ALU.add, ALU.add))
                        then(dve.scalar_tensor_tensor(slot_row[:], slot_tile[:], float(-P), slot[:], ALU.mult, ALU.add))
                        dve.tensor_copy(slot_u[:], slot[:]).then_inc(slots_known, 1)
                    if n == 4:
                        for g in range(0, GROUPS, PLACED):
                            dve.tensor_tensor(row_is[:, g:g + PLACED], slot_row[:, g:g + PLACED].rearrange("p (g o) -> p g o", o=1).broadcast_to([P, PLACED, P]),
                                              row_no[:].rearrange("p (o t) -> p o t", o=1).broadcast_to([P, PLACED, P]), ALU.is_equal).then_inc(placed, 1)
                        each_tile = lambda t: t[:].rearrange("p (g o) -> p g o", o=1).broadcast_to([P, GROUPS, TILES])
                        then(dve.tensor_tensor(number_at[:], each_tile(slot_tile), tile_no[:].rearrange("p (o t) -> p o t", o=1).broadcast_to([P, GROUPS, TILES]),
                                               ALU.is_equal))
                        dve.tensor_tensor(number_at[:], number_at[:], each_tile(token_no), ALU.mult).then_inc(placed, 1)
                    if n == 5:
                        dve.wait_ge(table_made, 1)
                        dve.tensor_copy(table[:], p_table).then_inc(table_ready, 1)

                if sems is early:
                    expert_tiles(tile, dve, beside)
                else:
                    late_tiles(tile)
            dve.nop().then_inc(summed, 2 * GOT)
            tiles(early)
            end_early(dve, dve.memset(carrier_dve[:], 0.0))
            tiles(late)

        @block.gpsimd
        def _(pool):
            def rstd(step, need, to, mv, ready):
                pool.wait_ge(step, need)
                pool.tensor_tensor(to[:], mv[:, 1:2], minus_half[:], ALU.pow).then_inc(ready, 1)

            def rstd1_make(b, par):
                rstd(ln1_step, b * 4 + 3, rstd1, mv1, rstd1_ready)

            def rstd2_make(b, par):
                rstd(ln2_step, b * 5 + 4, rstd2, mv2, rstd2_ready)

            def ctx_low(b, par):
                pool.wait_ge(ctx_hi, b + 1)
                pool.tensor_tensor(ctx16[:, par, 1], ctx_sb[:, par], ctx16[:, par, 0], ALU.subtract).then_inc(ctx_lo, 1)

            pool.dma_start(pos_sb[:], pos.rearrange("b p c -> p b c")).then_inc(pos_loaded, 16)
            pool.memset(minus_half[:], -0.5).then_inc(cleared, 1)
            pool.memset(ident[:], 0.0).then_inc(cleared, 1)
            pool.memset(ident16[:], 0.0).then_inc(cleared, 1)
            pool.wait_ge(cleared, 3)
            for m in (ident, ident16):
                pool.affine_select(out=m[:], in_=m[:], compare_op=ALU.not_equal, fill=1.0, base=0,
                                   pattern=[[-1, P]], channel_multiplier=1).then_inc(cleared, 1)
            pool.wait_ge(cleared, 5)
            pool.nop().then_inc(ident_ready, 1)
            rstd1_make(0, 0)
            ctx_low(0, 0)
            pool.dma_start(bout_sb[:], bout.partition_broadcast(P)).then_inc(w_bout, 16)
            pool.memset(w_scale[:], W_SCALE).then_inc(cleared, 1)
            pool.memset(before[:], 1.0).then_inc(cleared, 1)
            pool.memset(select, 0.0).then_inc(cleared, 1)
            pool.memset(ones16[:], 1.0).then_inc(cleared, 1)
            pool.memset(ye[:, 0], 0.0).then_inc(cleared, 1)
            pool.memset(one_e[:], 1.0).then_inc(cleared, 1)
            pool.iota(row_no[:], [[1, P]], base=0, channel_multiplier=0, allow_small_or_imprecise_dtypes=True).then_inc(cleared, 1)
            pool.iota(token_no[:], [[P, B], [0, TOPK]], base=0, channel_multiplier=1, allow_small_or_imprecise_dtypes=True).then_inc(cleared, 1)
            pool.iota(expert_no[:], [[1, E]], base=0, channel_multiplier=0, allow_small_or_imprecise_dtypes=True).then_inc(cleared, 1)
            pool.iota(tile_no[:], [[1, TILES]], base=0, channel_multiplier=0, allow_small_or_imprecise_dtypes=True).then_inc(cleared, 1)
            pool.wait_ge(cleared, 15)
            pool.affine_select(out=before[:], in_=before[:], compare_op=ALU.is_gt, fill=0.0, base=0,
                               pattern=[[1, P]], channel_multiplier=-1).then_inc(cleared, 1)
            for a in range(2):
                pool.wait_ge(cleared, 16 + a)
                rows = select[32 * a:32 * a + HEADS]
                pool.affine_select(out=rows, in_=rows, compare_op=ALU.not_equal, fill=1.0, base=0,
                                   pattern=[[-1, HEADS], [0, P]], channel_multiplier=1).then_inc(cleared, 1)
            pool.wait_ge(cleared, 18)
            pool.nop().then_inc(consts, 1)

            def row(b):
                return stream[:, bass.ds(b, 1), :].rearrange("p o d -> p (o d)")

            def bias_add(b, par):
                pool.wait_ge(ln1_step, b * 4 + 4)
                pool.tensor_tensor(row(b), row(b), bout_sb[:], ALU.add).then_inc(bias_added, 1)

            def rotate_swapped(b, par):
                pool.wait_ge(q_ready, b + 1)
                pool.wait_ge(k_ready, b + 1)
                if later(b, 1):
                    pool.wait_ge(rot_step, b * 2)
                q3 = qk[:].rearrange("p (h r two) -> p h r two", two=2, r=ROT)
                s3 = swp[:].rearrange("p (h r two) -> p h r two", two=2, r=ROT)
                t3 = sin_t[:, bass.ds(b, 1), :].rearrange("p o (r two) -> p o r two", two=2)
                for side in range(2):
                    pool.tensor_tensor(s3[:, :, :, side], q3[:, :, :, 1 - side],
                                       t3[:, :, :, side].broadcast_to([P, 2 * HEADS, ROT]), ALU.mult).then_inc(swapped, 1)

            def lo_make(b, par):
                pool.wait_ge(hi_ready, b + 1)
                pool.tensor_tensor(parts[:, :, HD:2 * HD], rot[:].rearrange("p (h d) -> p h d", d=HD), parts[:, :, 0:HD],
                                   ALU.subtract).then_inc(lo_ready, 1)

            def plo_make(b, par, c):
                pool.wait_ge(phi_ready, b * NCH + c + 1)
                if later(b, 1) or c >= RING:
                    pool.wait_ge(pv_done, b * NCH + c + 1 - RING)
                pool.tensor_tensor(plo[:, c % RING, :], prob[:, c % RING, :], phi[:, c % RING, :], ALU.subtract).then_inc(plo_ready, 1)

            pool.wait_ge(tables_ready, 1)
            def w13_low(to, par, number):
                pool.wait_ge(hi13, number * KC - (KC - 1))
                if later(number, 2):
                    pool.wait_ge(lo13_pool, number - 1)
                pool.tensor_tensor(scaled, w13[:, par, 0], w_scale[:].broadcast_to([P, W13]), ALU.mult).then_inc(w13_scaled, 1)
                pool.wait_ge(w13_scaled, number)
                pool.tensor_tensor(to[0][:, 1, 0], scaled, to[0][:, 0, 0], ALU.subtract).then_inc(lo13_pool, 1)

            def split_shared():
                pool.wait_ge(rot_step, 2 * B)
                w13_low(split["shared"], 0, 1)

            def xn2_low(b, par):
                pool.wait_ge(xn2_hi, b + 1)
                pool.tensor_tensor(xn2_parts[:, par, 1], xn2[:, par], xn2_parts[:, par, 0], ALU.subtract).then_inc(xn2_lo, 1)

            pool.wait_ge(w_bout, 16)

            def step(b, on):
                on(2, lo_make)
                on(1, plo_make, 2)
                on(0, rstd2_make)
                on(1, plo_make, 3)
                on(1, plo_make, 4)
                on(1, plo_make, 5)
                on(1, plo_make, 6)
                on(1, plo_make, 7)
                on(1, bias_add)
                on(-1, xn2_low)
                on(4, ctx_low)
                on(3, rotate_swapped)
                on(4, rstd1_make)
                on(2, plo_make, 0)
                on(2, plo_make, 1)
                if isinstance(b, int) and b == B - 1:
                    split_shared()

            pipeline(step, pool, -4, B, 1, (B - 5) // 2, ahead=[rstd1_make, ctx_low])

            pool.wait_ge(table_ready, 1)
            pool.wait_ge(xn2_stored, B * 16 + 16)

            def gather_rows(n, par):
                pool.wait_ge(early.xeT_done, n - 1)
                pool.tensor_copy(row_at[:, par], table[:, bass.ds(n - EARLY, 1)]).then_inc(row_copied, 1)
                pool.wait_ge(row_copied, n - (EARLY - 1))
                pool.tensor_tensor(carrier_pool[:], minus_half[:], minus_half[:], ALU.mult)
                pool.indirect_dma_start(out=xe[:, par].rearrange("p a d -> p (a d)"), out_offset=None, in_=xn2_dram,
                                        in_offset=bass.IndirectOffsetOnAxis(ap=row_at[:, par], axis=0)).then_inc(xe_gathered[par], 16)

            def gather(n, m, par, kinds):
                if kinds[3] == "routed":
                    gather_rows(n + 3, 1 - par)

            def tile(n, m, par, kinds):
                if kinds[2] == "routed":
                    w13_low(split[par], par, split_no(n + 2))

            expert_tiles(tile, pool, ahead=gather)
            end_early(pool, pool.tensor_tensor(carrier_pool[:], minus_half[:], minus_half[:], ALU.mult))

            pool.wait_ge(y_stored[0], (TILES + 3) // 2 * 16)
            pool.wait_ge(y_stored[1], (TILES // 2 + 1) * 16)
            with pool.Fori(0, B // GOT) as r:
                for u in range(GOT):
                    b = r * GOT + u
                    pool.wait_ge(summed, b * 2 + 2)
                    pool.tensor_copy(y_at[:, u, :], slot_u[:, bass.ds(b * 2, 2)]).then_inc(y_at_copied, 1)
                    pool.wait_ge(y_at_copied, b + 1)
                    pool.tensor_tensor(carrier_pool[:], minus_half[:], minus_half[:], ALU.mult)
                    for k in range(TOPK):
                        pool.indirect_dma_start(out=y_got[u][k], out_offset=None, in_=y_dram,
                                                in_offset=bass.IndirectOffsetOnAxis(ap=y_at[:, u, k:k + 1], axis=0)).then_inc(y_gathered[u], 16)


def kernel(**inputs):
    import numpy as np
    import concourse.bacc as bacc
    from concourse.bass_utils import run_bass_kernel_spmd

    def turned(a):
        return np.ascontiguousarray(np.swapaxes(np.asarray(a), -1, -2))

    w = {k[len("L0_"):]: np.asarray(v) for k, v in inputs.items() if k.startswith("L0_")}
    arrays = {
        "x": np.ascontiguousarray(inputs["x"]),
        "ctxT": turned(inputs["ctx_1024"]),
        "pos": np.ascontiguousarray(inputs["fside_BxSx2_0"]),
        "wq": w["xattn_Wq"], "wkv": w["xattn_Wkv"], "wo": w["xattn_Wout"], "bout": w["xattn_bout"],
        "gateT": turned(w["ffn_gate_w"]), "gbias": w["ffn_bias"],
        "s13": turned(np.concatenate([w["ffn_shared_w1"], w["ffn_shared_w3"]], axis=0)),
        "s2": turned(w["ffn_shared_w2"]),
        "e13": turned(np.concatenate([w["ffn_w1"], w["ffn_w3"]], axis=1)),
        "e2": turned(w["ffn_w2"]),
    }
    arrays = {k: np.ascontiguousarray(v) for k, v in arrays.items()}
    nc = bacc.Bacc("TRN2", target_bir_lowering=False, num_devices=1)
    args = {k: nc.dram_tensor(k, v.shape, mybir.dt.from_np(v.dtype), kind="ExternalInput").ap() for k, v in arrays.items()}
    out = nc.dram_tensor("out", (B, P, DIM), F32, kind="ExternalOutput").ap()
    build(nc, out=out, **args)
    r = run_bass_kernel_spmd(nc, [arrays], core_ids=[0])
    return r.results[0]["out"]
```
